# Optimizing a Trainium2 kernel written in Bass

```python
import numpy as np
import jax
import jax.numpy as jnp

def _softmax(x, axis=-1):
    return jax.nn.softmax(x, axis=axis)

def _gelu(x):
    return jax.nn.gelu(x, approximate=True)

def _silu(x):
    return jax.nn.silu(x)

def _sigmoid(x):
    return jax.nn.sigmoid(x)

def _layernorm(x, axis=-1, eps=1e-05):
    m = jnp.mean(x, axis=axis, keepdims=True)
    v = jnp.var(x, axis=axis, keepdims=True)
    return (x - m) / jnp.sqrt(v + eps)

def _scatter_add(tgt, idx, src, axis=0):
    return tgt.at[idx].add(src)

def _segment_sum(src, seg, n):
    return jax.ops.segment_sum(src, seg, n)
kernel_name = 'mk_xattn_ffn_d1_seqx_r4_401216'

def setup_inputs(seed: int=0):
    np.random.seed(seed)
    _w = jnp.asarray

    def _rec_inputs():
        import jax
        import jax.numpy as jnp
        _rk = jax.random.key(seed)
        x = 7.22e-05 + 1 * jax.random.normal(jax.random.fold_in(_rk, 1), (4, 1024, 256), jnp.float32)
        _lenS = 1024 - jax.random.randint(jax.random.fold_in(_rk, 7), (4,), 0, max(1, 1024 // 4) + 1, jnp.int32)
        _lenS2 = 154 - jax.random.randint(jax.random.fold_in(_rk, 8), (4,), 0, max(1, 154 // 4) + 1, jnp.int32)
        _ctx_1024P = jax.random.normal(jax.random.fold_in(_rk, 11), (4, 16, 256), jnp.float32)
        _ctx_1024c = jax.random.dirichlet(jax.random.fold_in(_rk, 511), 0.3 * jnp.ones((16,), jnp.float32), (4, 154))
        _ctx_1024t = jnp.einsum('bsk,bkd->bsd', _ctx_1024c, _ctx_1024P)
        _ctx_1024t = _ctx_1024t * jax.lax.rsqrt(jnp.mean(jnp.square(_ctx_1024t)) + 1e-12) * 0.953939
        ctx_1024 = 4.13588e-05 + 0.999923 * (_ctx_1024t + 0.3 * jax.random.normal(jax.random.fold_in(_rk, 611), (4, 154, 256), jnp.float32))
        return (x, ctx_1024)
    x, ctx_1024 = _rec_inputs()

    def _L0_xattn_setup():
        import jax, jax.numpy as jnp
        import numpy as np
        EMBED = 256
        HEADS = 16
        HEAD_DIM = EMBED // HEADS

        def _split_heads(x):
            B, S, _ = x.shape
            return x.reshape(B, S, HEADS, HEAD_DIM).transpose(0, 2, 1, 3)
        key = jax.random.key(seed)
        ks = jax.random.split(key, 11)
        B, S = (4, 512)
        scale = 1.0 / np.sqrt(EMBED)
        inp = {'query': jax.random.normal(ks[0], (B, S, EMBED), dtype=jnp.float32), 'key': jax.random.normal(ks[1], (B, S, EMBED), dtype=jnp.float32), 'value': jax.random.normal(ks[2], (B, S, EMBED), dtype=jnp.float32), 'Wq': jax.random.normal(ks[3], (EMBED, EMBED), dtype=jnp.float32) * scale, 'bq': jnp.zeros((EMBED,), dtype=jnp.float32), 'Wk': jax.random.normal(ks[4], (EMBED, EMBED), dtype=jnp.float32) * scale, 'bk': jnp.zeros((EMBED,), dtype=jnp.float32), 'Wv': jax.random.normal(ks[5], (EMBED, EMBED), dtype=jnp.float32) * scale, 'bv': jnp.zeros((EMBED,), dtype=jnp.float32), 'Wo': jax.random.normal(ks[6], (EMBED, EMBED), dtype=jnp.float32) * scale, 'bo': jnp.zeros((EMBED,), dtype=jnp.float32)}
        return inp
    _L0_xattn_all = _L0_xattn_setup()
    _L0_xattn_in = {k: v for k, v in _L0_xattn_all.items() if k in ('Wq', 'bq', 'Wk', 'bk', 'Wv', 'bv', 'Wo', 'bo')}
    del _L0_xattn_all

    def _L0_ffn_setup():
        import jax, jax.numpy as jnp
        import numpy as np
        DIM = 256
        NQ = 16
        NKV = 4
        HD = DIM // NQ
        HID = 512
        E = 8
        B, S = (1, 256)
        EPS = 1e-06

        def rmsnorm(x, w):
            ms = jnp.mean(x * x, axis=-1, keepdims=True)
            return w * (x * jax.lax.rsqrt(ms + EPS))

        def rope_tables(seq_len, head_dim):
            inv_freq = 1.0 / 10000.0 ** (jnp.arange(0, head_dim, 2, dtype=jnp.float32) / head_dim)
            t = jnp.arange(seq_len, dtype=jnp.float32)
            freqs = jnp.einsum('i,j->ij', t, inv_freq)
            return (jnp.cos(freqs), jnp.sin(freqs))

        def apply_rope(x, cos, sin):
            c = cos[None, :, None, :]
            s = sin[None, :, None, :]
            half = x.shape[-1] // 2
            x1, x2 = (x[..., :half], x[..., half:])
            return jnp.concatenate([x1 * c - x2 * s, x1 * s + x2 * c], axis=-1)

        def _forward(x, ln1_w, ln2_w, Wq, bq, Wk, bk, Wv, bv, qn_w, kn_w, Wg, bg, Wo, bo, Wr, br, W1, b1, W2, b2):
            batch, seq, _ = x.shape
            cos, sin = rope_tables(seq, HD)
            h = rmsnorm(x, ln1_w)
            q = (h @ Wq + bq).reshape(batch, seq, NQ, HD)
            k = (h @ Wk + bk).reshape(batch, seq, NKV, HD)
            v = (h @ Wv + bv).reshape(batch, seq, NKV, HD)
            q = rmsnorm(apply_rope(q, cos, sin), qn_w)
            k = rmsnorm(apply_rope(k, cos, sin), kn_w)
            rep = NQ // NKV
            k = jnp.repeat(k, rep, axis=2)
            v = jnp.repeat(v, rep, axis=2)
            scores = jnp.einsum('bthd,bshd->bhts', q, k) / np.sqrt(HD)
            causal = jnp.tril(jnp.ones((seq, seq), dtype=bool))
            scores = jnp.where(causal[None, None], scores, -jnp.inf)
            attn = jax.nn.softmax(scores, axis=-1)
            out = jnp.einsum('bhts,bshd->bthd', attn, v)
            gate = jax.nn.sigmoid(out @ Wg + bg)
            out = (out * gate).reshape(batch, seq, DIM)
            x = x + out @ Wo + bo
            h2 = rmsnorm(x, ln2_w)
            logits = h2 @ Wr + br
            top1 = jnp.argmax(logits, axis=-1).reshape(-1)
            xt = h2.reshape(-1, DIM)
            u = jnp.einsum('td,edf->tef', xt, W1) + b1
            u1, u2 = (u[..., :HID], u[..., HID:])
            act = u1 * jax.nn.sigmoid(u2)
            y_all = jnp.einsum('teh,ehd->ted', act, W2) + b2
            y = jnp.take_along_axis(y_all, top1[:, None, None], axis=1)[:, 0, :]
            return x + y.reshape(batch, seq, DIM)
        key = jax.random.key(seed)
        ks = jax.random.split(key, 20)
        sc = lambda fan_in: 1.0 / np.sqrt(fan_in)
        d = {}
        d['x'] = jax.random.normal(ks[0], (B, S, DIM), dtype=jnp.float32)
        d['ln1_w'] = jnp.ones((DIM,), jnp.float32)
        d['ln2_w'] = jnp.ones((DIM,), jnp.float32)
        d['Wq'] = jax.random.normal(ks[1], (DIM, DIM), jnp.float32) * sc(DIM)
        d['bq'] = jnp.zeros((DIM,), jnp.float32)
        d['Wk'] = jax.random.normal(ks[2], (DIM, HD * NKV), jnp.float32) * sc(DIM)
        d['bk'] = jnp.zeros((HD * NKV,), jnp.float32)
        d['Wv'] = jax.random.normal(ks[3], (DIM, HD * NKV), jnp.float32) * sc(DIM)
        d['bv'] = jnp.zeros((HD * NKV,), jnp.float32)
        d['qn_w'] = jnp.ones((HD,), jnp.float32)
        d['kn_w'] = jnp.ones((HD,), jnp.float32)
        d['Wg'] = jax.random.normal(ks[4], (HD, HD), jnp.float32) * sc(HD)
        d['bg'] = jnp.zeros((HD,), jnp.float32)
        d['Wo'] = jax.random.normal(ks[5], (DIM, DIM), jnp.float32) * sc(DIM)
        d['bo'] = jnp.zeros((DIM,), jnp.float32)
        d['Wr'] = jax.random.normal(ks[6], (DIM, E), jnp.float32) * sc(DIM)
        d['br'] = jnp.zeros((E,), jnp.float32)
        d['W1'] = jax.random.normal(ks[7], (E, DIM, 2 * HID), jnp.float32) * sc(DIM)
        d['b1'] = jnp.zeros((E, 2 * HID), jnp.float32)
        d['W2'] = jax.random.normal(ks[8], (E, HID, DIM), jnp.float32) * sc(HID)
        d['b2'] = jnp.zeros((E, DIM), jnp.float32)
        return d
    _L0_ffn_all = _L0_ffn_setup()
    _L0_ffn_in = {k: v for k, v in _L0_ffn_all.items() if k in ('ln1_w', 'ln2_w', 'Wq', 'bq', 'Wk', 'bk', 'Wv', 'bv', 'qn_w', 'kn_w', 'Wg', 'bg', 'Wo', 'bo', 'Wr', 'br', 'W1', 'b1', 'W2', 'b2')}
    del _L0_ffn_all
    return {'x': x, 'ctx_1024': ctx_1024, 'L0_xattn_Wq': _L0_xattn_in['Wq'], 'L0_xattn_bq': _L0_xattn_in['bq'], 'L0_xattn_Wk': _L0_xattn_in['Wk'], 'L0_xattn_bk': _L0_xattn_in['bk'], 'L0_xattn_Wv': _L0_xattn_in['Wv'], 'L0_xattn_bv': _L0_xattn_in['bv'], 'L0_xattn_Wo': _L0_xattn_in['Wo'], 'L0_xattn_bo': _L0_xattn_in['bo'], 'L0_ffn_ln1_w': _L0_ffn_in['ln1_w'], 'L0_ffn_ln2_w': _L0_ffn_in['ln2_w'], 'L0_ffn_Wq': _L0_ffn_in['Wq'], 'L0_ffn_bq': _L0_ffn_in['bq'], 'L0_ffn_Wk': _L0_ffn_in['Wk'], 'L0_ffn_bk': _L0_ffn_in['bk'], 'L0_ffn_Wv': _L0_ffn_in['Wv'], 'L0_ffn_bv': _L0_ffn_in['bv'], 'L0_ffn_qn_w': _L0_ffn_in['qn_w'], 'L0_ffn_kn_w': _L0_ffn_in['kn_w'], 'L0_ffn_Wg': _L0_ffn_in['Wg'], 'L0_ffn_bg': _L0_ffn_in['bg'], 'L0_ffn_Wo': _L0_ffn_in['Wo'], 'L0_ffn_bo': _L0_ffn_in['bo'], 'L0_ffn_Wr': _L0_ffn_in['Wr'], 'L0_ffn_br': _L0_ffn_in['br'], 'L0_ffn_W1': _L0_ffn_in['W1'], 'L0_ffn_b1': _L0_ffn_in['b1'], 'L0_ffn_W2': _L0_ffn_in['W2'], 'L0_ffn_b2': _L0_ffn_in['b2']}

def reference(x, ctx_1024, L0_xattn_Wq, L0_xattn_bq, L0_xattn_Wk, L0_xattn_bk, L0_xattn_Wv, L0_xattn_bv, L0_xattn_Wo, L0_xattn_bo, L0_ffn_ln1_w, L0_ffn_ln2_w, L0_ffn_Wq, L0_ffn_bq, L0_ffn_Wk, L0_ffn_bk, L0_ffn_Wv, L0_ffn_bv, L0_ffn_qn_w, L0_ffn_kn_w, L0_ffn_Wg, L0_ffn_bg, L0_ffn_Wo, L0_ffn_bo, L0_ffn_Wr, L0_ffn_br, L0_ffn_W1, L0_ffn_b1, L0_ffn_W2, L0_ffn_b2):
    import jax
    import jax.numpy as jnp

    def _L0_xattn_ref(query, key, value, Wq, bq, Wk, bk, Wv, bv, Wo, bo):
        import jax, jax.numpy as jnp
        import numpy as np
        EMBED = 256
        HEADS = 16
        HEAD_DIM = EMBED // HEADS

        def _split_heads(x):
            B, S, _ = x.shape
            return x.reshape(B, S, HEADS, HEAD_DIM).transpose(0, 2, 1, 3)
        B, S, _ = query.shape
        q = _split_heads(query @ Wq.T + bq)
        k = _split_heads(key @ Wk.T + bk)
        v = _split_heads(value @ Wv.T + bv)
        scores = jnp.einsum('bhqd,bhkd->bhqk', q, k) / jnp.sqrt(jnp.float32(HEAD_DIM))
        attn = jax.nn.softmax(scores, axis=-1)
        out = jnp.einsum('bhqk,bhkd->bhqd', attn, v)
        out = out.transpose(0, 2, 1, 3).reshape(B, S, EMBED)
        return out @ Wo.T + bo

    def _L0_ffn_ref(x, ln1_w, ln2_w, Wq, bq, Wk, bk, Wv, bv, qn_w, kn_w, Wg, bg, Wo, bo, Wr, br, W1, b1, W2, b2):
        import jax, jax.numpy as jnp
        import numpy as np
        DIM = 256
        NQ = 16
        NKV = 4
        HD = DIM // NQ
        HID = 512
        E = 8
        B, S = (1, 256)
        EPS = 1e-06

        def rmsnorm(x, w):
            ms = jnp.mean(x * x, axis=-1, keepdims=True)
            return w * (x * jax.lax.rsqrt(ms + EPS))

        def rope_tables(seq_len, head_dim):
            inv_freq = 1.0 / 10000.0 ** (jnp.arange(0, head_dim, 2, dtype=jnp.float32) / head_dim)
            t = jnp.arange(seq_len, dtype=jnp.float32)
            freqs = jnp.einsum('i,j->ij', t, inv_freq)
            return (jnp.cos(freqs), jnp.sin(freqs))

        def apply_rope(x, cos, sin):
            c = cos[None, :, None, :]
            s = sin[None, :, None, :]
            half = x.shape[-1] // 2
            x1, x2 = (x[..., :half], x[..., half:])
            return jnp.concatenate([x1 * c - x2 * s, x1 * s + x2 * c], axis=-1)

        def _forward(x, ln1_w, ln2_w, Wq, bq, Wk, bk, Wv, bv, qn_w, kn_w, Wg, bg, Wo, bo, Wr, br, W1, b1, W2, b2):
            batch, seq, _ = x.shape
            cos, sin = rope_tables(seq, HD)
            h = rmsnorm(x, ln1_w)
            q = (h @ Wq + bq).reshape(batch, seq, NQ, HD)
            k = (h @ Wk + bk).reshape(batch, seq, NKV, HD)
            v = (h @ Wv + bv).reshape(batch, seq, NKV, HD)
            q = rmsnorm(apply_rope(q, cos, sin), qn_w)
            k = rmsnorm(apply_rope(k, cos, sin), kn_w)
            rep = NQ // NKV
            k = jnp.repeat(k, rep, axis=2)
            v = jnp.repeat(v, rep, axis=2)
            scores = jnp.einsum('bthd,bshd->bhts', q, k) / np.sqrt(HD)
            causal = jnp.tril(jnp.ones((seq, seq), dtype=bool))
            scores = jnp.where(causal[None, None], scores, -jnp.inf)
            attn = jax.nn.softmax(scores, axis=-1)
            out = jnp.einsum('bhts,bshd->bthd', attn, v)
            gate = jax.nn.sigmoid(out @ Wg + bg)
            out = (out * gate).reshape(batch, seq, DIM)
            x = x + out @ Wo + bo
            h2 = rmsnorm(x, ln2_w)
            logits = h2 @ Wr + br
            top1 = jnp.argmax(logits, axis=-1).reshape(-1)
            xt = h2.reshape(-1, DIM)
            u = jnp.einsum('td,edf->tef', xt, W1) + b1
            u1, u2 = (u[..., :HID], u[..., HID:])
            act = u1 * jax.nn.sigmoid(u2)
            y_all = jnp.einsum('teh,ehd->ted', act, W2) + b2
            y = jnp.take_along_axis(y_all, top1[:, None, None], axis=1)[:, 0, :]
            return x + y.reshape(batch, seq, DIM)
        return _forward(x, ln1_w, ln2_w, Wq, bq, Wk, bk, Wv, bv, qn_w, kn_w, Wg, bg, Wo, bo, Wr, br, W1, b1, W2, b2)
    x = x + _L0_xattn_ref(_layernorm(x, axis=-1), ctx_1024, ctx_1024, L0_xattn_Wq, L0_xattn_bq, L0_xattn_Wk, L0_xattn_bk, L0_xattn_Wv, L0_xattn_bv, L0_xattn_Wo, L0_xattn_bo)
    x = x + _L0_ffn_ref(_layernorm(x, axis=-1), L0_ffn_ln1_w, L0_ffn_ln2_w, L0_ffn_Wq, L0_ffn_bq, L0_ffn_Wk, L0_ffn_bk, L0_ffn_Wv, L0_ffn_bv, L0_ffn_qn_w, L0_ffn_kn_w, L0_ffn_Wg, L0_ffn_bg, L0_ffn_Wo, L0_ffn_bo, L0_ffn_Wr, L0_ffn_br, L0_ffn_W1, L0_ffn_b1, L0_ffn_W2, L0_ffn_b2)
    return x

_drawn_inputs = setup_inputs


def setup_inputs(seed=0):
    import zlib

    import numpy as np

    out = dict(_drawn_inputs(seed))
    spreads = {'L0_xattn_bq': (0.0, 0.1),
     'L0_xattn_bk': (0.0, 0.8),
     'L0_xattn_bv': (0.0, 0.1),
     'L0_xattn_bo': (0.0, 0.1),
     'L0_ffn_ln1_w': (1.0, 0.2),
     'L0_ffn_ln2_w': (1.0, 0.2),
     'L0_ffn_bq': (0.0, 0.298),
     'L0_ffn_bk': (0.0, 0.325),
     'L0_ffn_bv': (0.0, 0.1),
     'L0_ffn_qn_w': (1.0, 0.2),
     'L0_ffn_kn_w': (1.0, 0.2),
     'L0_ffn_bg': (0.0, 0.1),
     'L0_ffn_bo': (0.0, 0.1),
     'L0_ffn_br': (0.0, 0.1),
     'L0_ffn_b1': (0.0, 0.303),
     'L0_ffn_b2': (0.0, 0.1)}
    factors = {}
    for name, (base, spread) in spreads.items():
        noise = np.random.default_rng([zlib.crc32(name.encode()), seed]).standard_normal(out[name].shape)
        drawn = base * np.exp(spread * noise) if base else spread * noise
        out[name] = jnp.asarray(drawn.astype(out[name].dtype))
    for name, factor in factors.items():
        out[name] = (out[name] * factor).astype(out[name].dtype)
    return out
```

```python
import numpy as np
import concourse.bass as bass
from concourse import mybir
from contextlib import ExitStack

fp32 = mybir.dt.float32
bf16 = mybir.dt.bfloat16
i32 = mybir.dt.int32
u32 = mybir.dt.uint32
ALU = mybir.AluOpType
ACT = mybir.ActivationFunctionType
AX = mybir.AxisListType

P = 128
B, S, D = 4, 1024, 256
C = 154
CR = C - P
KR = 32
H, HD = 16, 16
KV = 4
HQ = H // KV
ST = S // P
T = B * ST
NE, HID = 8, 512
MT = T + NE - 1
PARTS = 6
RS = PARTS * HD
QKV = D + 2 * KV * HD
NH2 = H + KV
EPS_LN, EPS_RMS = 1e-5, 1e-6
SCALE = HD ** -0.5
Q_SLOTS = ((0, 3), (3, 5), (5, 6))
K_SLOTS = ((0, 3, 5), (1, 4), (2,))


def build(nc, a, out):
    ctx = ExitStack()
    with ctx:
        def sb(name, shape, dt=fp32):
            return ctx.enter_context(nc.sbuf_tensor(name, shape, dt))

        def ps(name, shape, dt=fp32):
            return ctx.enter_context(nc.psum_tensor(name, shape, dt))

        def sem(name):
            return ctx.enter_context(nc.semaphore(name))

        h2_dram = nc.dram_tensor("h2_rows", (T, P, D), fp32, kind="Internal").ap()
        base_dram = nc.dram_tensor("base_rows", (T, P, D), fp32, kind="Internal").ap()
        xs_dram = nc.dram_tensor("sorted_rows", (MT * P, D), fp32, kind="Internal").ap()
        ys_dram = nc.dram_tensor("sorted_results", (MT * P, D), fp32, kind="Internal").ap()

        identf = sb("identf", [P, P])
        identb = sb("identb", [P, P], bf16)
        xw = sb("xw", [P, 4, 2, D])
        xbias = sb("xbias", [P, 4, D])
        w_qkv = sb("w_qkv", [P, 2, QKV])
        b_qkv = sb("b_qkv", [P, QKV])
        w_o = sb("w_o", [P, 2, D])
        b_o = sb("b_o", [P, D])
        w_gate = sb("w_gate", [P, P])
        b_gate = sb("b_gate", [P, 1])
        w_r = sb("w_r", [P, 2, NE])
        b_r = sb("b_r", [P, NE])
        ln1 = sb("ln1", [P, D])
        ln2 = sb("ln2", [P, D])
        qk_w = sb("qk_w", [P, NH2, HD])
        rope_c = sb("rope_c", [P, ST, HD])
        rope_s = sb("rope_s", [P, ST, HD])
        W1 = sb("W1", [P, NE, 2, 2 * HID])
        W2 = sb("W2", [P, NE, HID // P, D])
        b1_parts = sb("b1_parts", [P, 2 * HID], bf16)
        b2_parts = sb("b2_parts", [P, D], bf16)
        pick = sb("pick", [P, NE, P], bf16)
        bshift = sb("bshift", [P, 1])
        upper = sb("upper", [P, P])
        ones = sb("ones", [P, P])
        count_e = sb("count_e", [P, NE])
        tile_row = sb("tile_row", [P, MT])
        zero_rows = sb("zero_rows", [P, D])

        ctxT = sb("ctxT", [P, 2, C])
        Kx = sb("Kx", [P, H, P + KR], bf16)
        Vx = sb("Vx", [P, H, 32])
        Vr = sb("Vr", [P, H // 4, P])
        xb = sb("xb", [P, ST, D])
        stats = sb("stats", [P, 6])
        mv = sb("mv", [P, 2])
        rstd = sb("rstd", [P, 1])
        xn = sb("xn", [P, D])
        xnT = sb("xnT", [P, 2, P])
        qf = sb("qf", [P, D])
        rest = sb("rest", [P, D])
        q_tok = sb("q_tok", [P, H, RS], bf16)
        Qst = sb("Qst", [P, H, P], bf16)
        mx = sb("mx", [P, H])
        nmx = sb("nmx", [P, 2, H], bf16)
        E = [sb(f"E{i}", [P, 1024]) for i in range(3)]
        oT = sb("oT", [P, 512])
        rsum = sb("rsum", [P, H])
        on = sb("on", [P, D])
        onT = sb("onT", [P, 2, P])

        y0_q = W1[:, NE - 2:].rearrange("p e k n -> p (e k n)")
        y0 = W1[:, NE - 1].rearrange("p k (j n) -> p (k j) n", n=D)
        hh = sb("hh", [P, D])
        sq = sb("sq", [P, NH2 * HD])
        ss = sb("ss", [P, 1])
        qkv = sb("qkv", [P, QKV])
        hs = sb("hs", [P, NH2])
        h_rs = sb("h_rs", [P, NH2])
        safe = sb("safe", [P, NH2])
        minus_half = sb("minus_half", [P, NH2])
        rs_row = sb("rs_row", [P, 1])
        nmT = sb("nmT", [P, 1, P], bf16)
        nb_gate = sb("nb_gate", [P, 1])
        ra = sb("ra", [P, NH2 * HD])
        rb = sb("rb", [P, NH2 * HD])
        q_hat = W1[:, NE - 2].rearrange("p k (j n) -> p (k j) n", n=D)
        ks_tok = sb("ks_tok", [P, KV, RS + 1], bf16)
        qs_tok = sb("qs_tok", [P, H, RS + 1], bf16)
        Kst = sb("Kst", [P, KV, S], bf16)
        Va = sb("Va", [P, ST, KV, 32])
        gt = sb("gt", [P, 2 * P])
        x2 = sb("x2", [P, D])
        base = sb("base", [P, D])
        h2 = sb("h2", [P, D])
        logits = sb("logits", [P, T, NE])

        ps_u = [ps(f"ps_u{i}", [P, 1024]) for i in range(3)]
        ps_o = ps("ps_o", [P, 512])
        ps_z = ps("ps_z", [P, 512])

        onehot = sb("onehot", [P, T, NE])
        ev_ = sb("ev_", [P, T, NE])
        best = sb("best", [P, T])
        total = sb("total", [P, NE, T])
        cum = sb("cum", [P, NE, T])
        padded = sb("padded", [P, NE])
        whole = sb("whole", [P, NE], i32)
        offset = sb("offset", [P, NE])
        placef = sb("placef", [P, T])
        place = sb("place", [P, T], u32)
        owns = sb("owns", [P, MT, NE])
        expertf = sb("expertf", [P, MT])
        expert = sb("expert", [P, MT], i32)
        rows, got, fin = ([xb[:, n + i] for i in range(2)] for n in (0, 2, 4))
        xr, yr = xb[:, 6], xb[:, 7]

        names = {}

        def ev(name):
            if name not in names:
                names[name] = sem(name)
            return names[name]

        s_w = sem("s_w")
        s_big = sem("s_big")
        s_ctx = sem("s_ctx")
        s_x = sem("s_x")
        s_st = sem("s_st")
        s_zero = sem("s_zero")
        s_ld = [sem(f"s_ld{i}") for i in range(2)]
        s_sc = [sem(f"s_sc{i}") for i in range(2)]
        s_xr = sem("s_xr")
        s_yr = sem("s_yr")
        s_bl = [sem(f"s_bl{i}") for i in range(2)]
        s_gt = [sem(f"s_gt{i}") for i in range(2)]
        s_out = [sem(f"s_out{i}") for i in range(2)]
        STAGE = 1 if "dbg_h2" in a else 9

        which_f = y0_q[RS:P, 0:H * (P + KR)]
        pick_f = y0_q[:, 3072:3072 + NE * P]
        small = [
            (identf[:], a["identf"]),
            (upper[:], a["upper"]), (ones[:], a["ones"]),
            (count_e[:], a["count_e"].to_broadcast([P, NE])),
            (tile_row[:], a["tile_row"].to_broadcast([P, MT])),
            (w_qkv[:], a["w_qkv"].rearrange("(k p) n -> p k n", p=P)),
            (w_o[:], a["L0_ffn_Wo"].rearrange("(k p) n -> p k n", p=P)),
            (w_gate[:], a["w_gate"]), (b_gate[:], a["b_gate"]),
            (w_r[:], a["L0_ffn_Wr"].rearrange("(k p) n -> p k n", p=P)),
            (b_qkv[:], a["b_qkv"].to_broadcast([P, QKV])),
            (b_o[:], a["bo"].to_broadcast([P, D])),
            (b_r[:], a["br"].to_broadcast([P, NE])),
            (ln1[:], a["ln1"].to_broadcast([P, D])),
            (ln2[:], a["ln2"].to_broadcast([P, D])),
            (qk_w[:].rearrange("p h d -> p (h d)"), a["qk_w"].to_broadcast([P, NH2 * HD])),
            (rope_c[:], a["rope_c"].rearrange("(j p) d -> p j d", p=P)),
            (rope_s[:], a["rope_s"].rearrange("(j p) d -> p j d", p=P)),
            (which_f, a["which_head"]),
            (pick_f, a["pick"]),
            (E[0][:], a["b1_rows"]),
            (E[1][:, 0:D], a["b2_rows"]),
        ]
        for n in range(4):
            small.append((xw[:, n], a["xw"][n].rearrange("(k p) n -> p k n", p=P)))
            small.append((xbias[:, n, :], a["xb"][n:n + 1, :].to_broadcast([P, D])))
        NW = len(small)

        N_CLEARED = 14
        N_CTX, N_X, N_SELF = 12, 22, ST * 7

        class Own:

            def __init__(self, eng, sem_, base):
                self.eng, self.sem, self.n, self.base = eng, sem_, 0, base

            def link(self, ins):
                ins.then_inc(self.sem, 1)
                self.n += 1
                self.eng.wait_ge(self.sem, self.base + self.n)

        s_alone = sem("s_alone")

        def alone(eng):
            eng.sem_inc(s_alone, 1)

        block = ctx.enter_context(nc.Block())

        @block.sync
        def _(sp):
            for dst, src in small:
                sp.dma_start(dst, src).then_inc(s_w, 16)
            sp.dma_start(ctxT[:], a["ctxT"][0].rearrange("(k p) n -> p k n", p=P)).then_inc(s_ctx, 16)
            sp.dma_start(xb[:], a["x"][0:P * ST].rearrange("(j p) n -> p j n", p=P)).then_inc(s_x, 16)
            for e in range(NE - 2):
                sp.dma_start(W1[:, e], a["L0_ffn_W1"][e].rearrange("(k p) n -> p k n", p=P)).then_inc(s_big, 16)
            for e in range(NE):
                sp.dma_start(W2[:, e], a["L0_ffn_W2"][e].rearrange("(k p) n -> p k n", p=P)).then_inc(s_big, 16)
            sp.wait_ge(ev("zeros"), 1)
            sp.sem_inc(s_st, 32)
            sp.sem_inc(s_yr, 16)
            for m in range(MT):
                sp.dma_start(xs_dram[m * P:(m + 1) * P], zero_rows[:]).then_inc(s_zero, 16)
            for b in range(B):
                if b > 0:
                    sp.wait_ge(ev("ctx_proj"), b)
                    sp.dma_start(ctxT[:], a["ctxT"][b].rearrange("(k p) n -> p k n", p=P)).then_inc(s_ctx, 16)
                    sp.wait_ge(ev("base"), b * ST)
                    sp.dma_start(xb[:], a["x"][b * S:(b + 1) * S].rearrange("(j p) n -> p j n", p=P)).then_inc(s_x, 16)
                with sp.Fori(b * ST, (b + 1) * ST) as t:
                    sp.wait_ge(ev("base"), t + 1)
                    sp.dma_start(base_dram[bass.ds(t, 1)].rearrange("a p n -> p (a n)"), base[:]).then_inc(s_st, 16)
                    sp.wait_ge(ev("h2"), t + 1)
                    sp.dma_start(h2_dram[bass.ds(t, 1)].rearrange("a p n -> p (a n)"), h2[:]).then_inc(s_st, 16)
            if STAGE == 1:
                sp.wait_ge(s_st, 32 * (T + 1))
                sp.wait_ge(ev("logits"), T)
                sp.dma_start(a["dbg_h2"], h2_dram).then_inc(s_out[0], 16)
                sp.dma_start(a["dbg_base"], base_dram).then_inc(s_out[0], 16)
                sp.dma_start(a["dbg_log"], logits[:]).then_inc(s_out[0], 16)
                sp.wait_ge(s_out[0], 48)
                return

            sp.wait_ge(ev("x2"), T)
            for e in range(NE - 2, NE):
                sp.dma_start(W1[:, e], a["L0_ffn_W1"][e].rearrange("(k p) n -> p k n", p=P)).then_inc(s_big, 16)
            for t in range(T):
                if t >= 2:
                    sp.wait_ge(s_sc[t % 2], 16 * (t // 2))
                if t == 0:
                    sp.wait_ge(s_st, 32 * (T + 1))
                sp.dma_start(rows[t % 2], h2_dram[t]).then_inc(s_ld[t % 2], 16)
            for i in range(2):
                sp.wait_ge(s_sc[i], 16 * (T // 2))
            with sp.Fori(0, MT) as m:
                sp.wait_ge(ev("rowsT_ps"), m + 1)
                sp.dma_start(xr, xs_dram[bass.ds(m * P, P)]).then_inc(s_xr, 16)
                sp.wait_ge(ev("y_rows"), m + 1)
                sp.dma_start(ys_dram[bass.ds(m * P, P)], yr).then_inc(s_yr, 16)
            for t in range(T):
                if t >= 2:
                    sp.wait_ge(ev("summed"), t - 1)
                sp.dma_start(rows[t % 2], base_dram[t]).then_inc(s_bl[t % 2], 16)
                if t >= 1:
                    sp.wait_ge(ev("summed"), t)
                    sp.dma_start(out[(t - 1) * P:t * P], fin[(t - 1) % 2]).then_inc(s_out[(t - 1) % 2], 16)
            sp.wait_ge(ev("summed"), T)
            sp.dma_start(out[(T - 1) * P:T * P], fin[(T - 1) % 2]).then_inc(s_out[(T - 1) % 2], 16)
            for i in range(2):
                sp.wait_ge(s_out[i], 16 * (T // 2))

        @block.gpsimd
        def _(pool):
            pool.memset(zero_rows[:], 0.0).then_inc(ev("zeros"), 1)
            n = 0
            for dst in (Vx[:], Vr[:], Va[:], Kx[0:RS, :, P:P + KR], b1_parts[:], b2_parts[:]):
                pool.memset(dst, 0.0).then_inc(ev("cleared"), 1)
                n += 1
                pool.wait_ge(ev("cleared"), n)
            pool.memset(minus_half[:], -0.5).then_inc(ev("cleared"), 1)
            n += 1
            for dst in (Vx[:, :, HD:HD + 1], Va[:, :, :, HD:HD + 1], ks_tok[:, :, RS:RS + 1],
                        *(Vr[32 * q:32 * q + CR, :, 32 * q + HD:32 * q + HD + 1] for q in range(4))):
                pool.memset(dst, 1.0).then_inc(ev("cleared"), 1)
                n += 1
                pool.wait_ge(ev("cleared"), n)
            assert n == N_CLEARED
            def root(ready, n, k, dst, src, eps, done):
                w = dst.shape[1]
                pool.wait_ge(ev(ready), n)
                alone(pool)
                pool.tensor_scalar(safe[:, 0:w], src, eps, None, ALU.add).then_inc(ev("safe"), 1)
                pool.wait_ge(ev("safe"), k + 1)
                pool.tensor_tensor(dst, safe[:, 0:w], minus_half[:, 0:w], ALU.pow).then_inc(ev(done), 1)

            with pool.Fori(0, B) as b:
                with pool.Fori(0, ST) as j:
                    t = b * ST + j
                    root("mv", 2 * t + 1, 5 * b * ST + 4 * j, rstd[:], mv[:, 1:2], EPS_LN, "rstd")
                    root("mv", 2 * t + 2, 5 * b * ST + 4 * j + 1, rstd[:], mv[:, 1:2], EPS_LN, "rstd")
                    root("y0_ss", t + 1, 5 * b * ST + 4 * j + 2, rs_row[:], ss[:], EPS_RMS, "y0_rs")
                    root("h_ms", t + 1, 5 * b * ST + 4 * j + 3, h_rs[:], hs[:], EPS_RMS, "h_rs")
                for j in range(ST):
                    for half in range(2):
                        u = j * (j + 1) + 2 * j + half
                        pool.wait_ge(ev("u_probs"), b * (ST * (ST + 1)) + u + 1)
                        alone(pool)
                        e3 = E[u % 3][:].rearrange("p (h n) -> p h n", n=P)
                        pool.affine_select(out=e3, in_=e3, compare_op=ALU.is_ge, fill=0.0, base=0,
                                           pattern=[[0, 1024 // P], [1, P]], channel_multiplier=-1).then_inc(ev("u_masked"), 1)
                    root("x2_ss", b * ST + j + 1, 5 * b * ST + 4 * ST + j, rs_row[:], ss[:], EPS_RMS, "x2_rs")
            if STAGE == 1:
                return
            pool.wait_ge(ev("places"), 1)
            pool.wait_ge(s_zero, 16 * MT)
            for t in range(T):
                pool.wait_ge(s_ld[t % 2], 16 * (t // 2 + 1))
                pool.indirect_dma_start(out=xs_dram, out_offset=bass.IndirectOffsetOnAxis(ap=place[:, t:t + 1], axis=0),
                                        in_=rows[t % 2], in_offset=None).then_inc(s_sc[t % 2], 16)
            pool.wait_ge(s_yr, 16 * (MT + 1))
            for t in range(T):
                if t >= 2:
                    pool.wait_ge(ev("summed"), t - 1)
                pool.indirect_dma_start(out=got[t % 2], out_offset=None, in_=ys_dram,
                                        in_offset=bass.IndirectOffsetOnAxis(ap=place[:, t:t + 1], axis=0)).then_inc(s_gt[t % 2], 16)

        @block.tensor
        def _(pe):
            pe.sem_inc(ev("rowsT_ps"), 1)

            def ctx_tiles(b):
                pe.wait_ge(s_ctx, b * 16 + 16)
                for w, o in ((1, 0), (2, 256)):
                    for k in range(2):
                        mm = pe.matmul(ps_u[0][:, o:o + D], ctxT[:, k, 0:P], xw[:, w, k], start=(k == 0), stop=(k == 1), skip_group_check=True)
                for k in range(2):
                    pe.matmul(ps_u[0][0:CR, 512:512 + D], ctxT[:, k, P:C], xw[:, 1, k], start=(k == 0), stop=(k == 1))
                for q in range(4):
                    for k in range(2):
                        mm = pe.matmul(ps_u[1][32 * q:32 * q + CR, 0:D], ctxT[:, k, P:C], xw[:, 2, k],
                                       start=(k == 0), stop=(k == 1))
                mm.then_inc(ev("ctx_proj"), 1)
                for n, rows in ((0, P), (1, CR)):
                    pe.wait_ge(ev("k_split"), b * 2 + n + 1)
                    alone(pe)
                    ub = ps_u[2][:].bitcast(bf16)
                    for h in range(H):
                        mm = pe.transpose(ub[0:RS, h * P:h * P + rows], q_tok[0:rows, h, :], identb[0:rows, 0:rows])
                    mm.then_inc(ev("k_turned"), 1)

            def cross_tile(t):
                pe.wait_ge(ev("xn"), t + 1)
                for k in range(2):
                    mm = pe.transpose(ps_z[:, k * P:(k + 1) * P], xn[:, k * P:(k + 1) * P], identf[:])
                mm.then_inc(ev("xnT_ps"), 1)
                pe.wait_ge(ev("xnT"), t + 1)
                for k in range(2):
                    mm = pe.matmul(ps_z[:, 256:512], xnT[:, k], xw[:, 0, k], start=(k == 0), stop=(k == 1))
                mm.then_inc(ev("q_ps"), 1)
                pe.wait_ge(ev("q_split"), t + 1)
                ub = ps_u[0][:].bitcast(bf16)
                for h in range(H):
                    mm = pe.transpose(ub[0:RS, h * P:(h + 1) * P], q_tok[:, h, :], identb[:])
                mm.then_inc(ev("q_turned"), 1)
                pe.wait_ge(ev("q_stack"), t + 1)
                for h in range(H):
                    c, r = h // 3, h % 3
                    dst = ps_u[(c // 2 + 1) % 3][:, (c % 2) * 512 + r * C:(c % 2) * 512 + r * C + C]
                    mm = pe.matmul(dst, Qst[0:RS, h], Kx[0:RS, h, 0:C], start=True, stop=True, skip_group_check=True)
                    if r == 2 or h == H - 1:
                        mm.then_inc(ev("s_rows"), 1)
                pe.wait_ge(ev("shift"), t + 1)
                pe.transpose(ps_z[:].bitcast(bf16)[RS:P, 0:P], nmx[:].rearrange("p a h -> p (a h)"), identb[:], tile_position=(0, RS)).then_inc(ev("shiftT_ps"), 1)
                pe.wait_ge(ev("shiftT"), t + 1)
                for h in range(H):
                    mm = pe.matmul(ps_u[h // 8][:, (h % 8) * P:(h % 8 + 1) * P], Kx[:, h, 0:P], Qst[:, h], start=True, stop=True, skip_group_check=True)
                    if h % 8 == 7:
                        mm.then_inc(ev("s_keys"), 1)
                for h in range(H):
                    q, g = h % 4, h // 4
                    mm = pe.matmul(ps_u[2][32 * q:32 * q + 32, g * P:(g + 1) * P], Kx[:, h, P:P + KR], Qst[:, h],
                                   start=True, stop=True, skip_group_check=True)
                mm.then_inc(ev("s_keys"), 1)
                for h in range(H):
                    q, g = h % 4, h // 4
                    if h % 8 == 0:
                        pe.wait_ge(ev("probs"), t * 3 + h // 8 + 1)
                    pe.matmul(ps_o[32 * q:32 * q + 32, g * P:(g + 1) * P], Vx[:, h], E[h // 8][:, (h % 8) * P:(h % 8 + 1) * P],
                              start=(g == 0), stop=False, skip_group_check=True)
                pe.wait_ge(ev("probs"), t * 3 + 3)
                for g in range(4):
                    mm = pe.matmul(ps_o[:, g * P:(g + 1) * P], Vr[:, g], E[2][:, g * P:(g + 1) * P], start=False, stop=True, skip_group_check=True)
                mm.then_inc(ev("oT_ps"), 1)
                pe.wait_ge(ev("oT"), t + 1)
                for g in range(4):
                    mm = pe.transpose(ps_o[:, g * P:(g + 1) * P], oT[:, g * P:(g + 1) * P], identf[:])
                mm.then_inc(ev("o_ps"), 1)
                pe.wait_ge(ev("on"), t + 1)
                for k in range(2):
                    mm = pe.transpose(ps_z[:, k * P:(k + 1) * P], on[:, k * P:(k + 1) * P], identf[:])
                mm.then_inc(ev("onT_ps"), 1)
                pe.wait_ge(ev("onT"), t + 1)
                for k in range(2):
                    mm = pe.matmul(ps_z[:, 256:512], onT[:, k], xw[:, 3, k], start=(k == 0), stop=(k == 1))
                mm.then_inc(ev("xo_ps"), 1)

            def qkv_tile(t, j):
                pe.wait_ge(ev("hh"), t + 1)
                for k in range(2):
                    mm = pe.transpose(ps_z[:, k * P:(k + 1) * P], hh[:, k * P:(k + 1) * P], identf[:])
                mm.then_inc(ev("hT_ps"), 1)
                pe.wait_ge(ev("hT"), t + 1)
                for k in range(2):
                    mm = pe.matmul(ps_o[:, 0:QKV], xnT[:, k], w_qkv[:, k], start=(k == 0), stop=(k == 1))
                mm.then_inc(ev("qkv_ps"), 1)
                pe.wait_ge(ev("ks_split"), t + 1)
                zb = ps_z[:].bitcast(bf16)
                for g in range(KV):
                    mm = pe.transpose(zb[0:RS + 1, g * P:(g + 1) * P], ks_tok[:, g, :], identb[:])
                mm.then_inc(ev("ks_turned"), 1)

            def prep_self(b, j):
                pe.wait_ge(ev("qs_split"), b * ST + j + 1)
                ub = ps_u[0][:].bitcast(bf16)
                for h in range(H):
                    mm = pe.transpose(ub[0:RS + 1, h * P:(h + 1) * P], qs_tok[:, h, :], identb[:])
                mm.then_inc(ev("qs_turned"), 1)
                pe.wait_ge(ev("qs_stack"), b * ST + j + 1)

            def units(b, j):
                base = 2 * (j * (j + 1) // 2)
                per = ST * (ST + 1)
                n = 2 * (j + 1)

                def scores(u):
                    i, half = u // 2, u % 2
                    if base + u >= 3:
                        pe.wait_ge(ev("u_probs"), b * per + base + u - 2)
                    for g in (2 * half, 2 * half + 1):
                        mm = pe.matmul(ps_u[(base + u) % 3][:, (g % 2) * 512:(g % 2) * 512 + 512],
                                       Kst[0:RS + 1, g, i * P:(i + 1) * P], Qst[0:RS + 1, HQ * g:HQ * g + HQ].rearrange("p h n -> p (h n)"),
                                       start=True, stop=True)
                    mm.then_inc(ev("u_scores"), 1)

                def values(u):
                    i, half = u // 2, u % 2
                    if i == j:
                        pe.wait_ge(ev("u_masked"), (b * ST + j) * 2 + half + 1)
                    else:
                        pe.wait_ge(ev("u_probs"), b * per + base + u + 1)
                    for g in (2 * half, 2 * half + 1):
                        mm = pe.matmul(ps_o[32 * g:32 * g + 32, :], Va[:, i, g], E[(base + u) % 3][:, (g % 2) * 512:(g % 2) * 512 + 512],
                                       start=(i == 0), stop=(i == j), skip_group_check=True)
                    mm.then_inc(ev("u_values"), 1)

                for u in range(n):
                    scores(u)
                    if u >= 2:
                        values(u - 2)
                for u in range(n - 2, n):
                    values(u)

            def tail_self(t):
                pe.wait_ge(ev("so_T"), t + 1)
                for g in range(4):
                    mm = pe.transpose(ps_o[:, g * P:(g + 1) * P], oT[:, g * P:(g + 1) * P], identf[:])
                mm.then_inc(ev("so_ps"), 1)
                pe.wait_ge(ev("so_n"), t + 1)
                for k in range(2):
                    mm = pe.transpose(ps_z[:, k * P:(k + 1) * P], on[:, k * P:(k + 1) * P], identf[:])
                mm.then_inc(ev("soT_ps"), 1)
                pe.wait_ge(ev("soT"), t + 1)
                pe.matmul(ps_z[:, 256:512], w_gate[:], onT[:].rearrange("p k n -> p (k n)"), start=True, stop=True).then_inc(ev("gate_ps"), 1)
                pe.wait_ge(ev("gated"), t + 1)
                for k in range(2):
                    mm = pe.matmul(ps_z[:, 0:256], gt[:, k * P:(k + 1) * P], w_o[:, k], start=(k == 0), stop=(k == 1))
                mm.then_inc(ev("wo_ps"), 1)
                pe.wait_ge(ev("h2"), t + 1)
                for k in range(2):
                    mm = pe.transpose(ps_z[:, 256 + k * P:256 + (k + 1) * P], h2[:, k * P:(k + 1) * P], identf[:])
                mm.then_inc(ev("h2T_ps"), 1)
                pe.wait_ge(ev("h2T"), t + 1)
                for k in range(2):
                    mm = pe.matmul(ps_z[:, 0:NE], xnT[:, k], w_r[:, k], start=(k == 0), stop=(k == 1))
                mm.then_inc(ev("logit_ps"), 1)

            pe.wait_ge(s_w, NW * 16)
            with pe.Fori(0, B) as b:
                ctx_tiles(b)
                pe.wait_ge(ev("k_ready"), b * 2 + 2)
                alone(pe)
                with pe.Fori(0, ST) as j:
                    cross_tile(b * ST + j)
                    qkv_tile(b * ST + j, j)
                pe.wait_ge(ev("ks_stack"), b * ST + ST)
                for j in range(ST):
                    prep_self(b, j)
                    units(b, j)
                    tail_self(b * ST + j)

            if STAGE == 1:
                return
            pe.wait_ge(ev("onehot"), 1)
            oh = onehot[:].rearrange("p t e -> p (t e)")
            pe.matmul(ps_u[0][:, 0:T * NE], upper[:], oh, start=True, stop=True)
            pe.matmul(ps_u[0][:, 512:512 + T * NE], ones[:], oh, start=True, stop=True).then_inc(ev("ranks"), 1)
            pe.wait_ge(ev("places"), 1)
            pe.wait_ge(s_big, 2 * NE * 16)
            with pe.Fori(0, MT) as m:
                alone(pe)
                e = pe.value_load(expert[0:1, bass.ds(m, 1)], min_val=0, max_val=NE - 1)
                pe.wait_ge(s_xr, 16 * m + 16)
                for k in range(2):
                    mm = pe.transpose(ps_z[:, k * P:(k + 1) * P], xr[:, k * P:(k + 1) * P], identf[:])
                mm.then_inc(ev("rowsT_ps"), 1)
                pe.wait_ge(ev("rowsT"), m + 1)
                for half in (1, 0):
                    dst = ps_u[0][:, half * HID:(half + 1) * HID]
                    for k in range(2):
                        w = W1[:, bass.ds(e, 1), k, half * HID:(half + 1) * HID].rearrange("p a n -> p (a n)")
                        pe.matmul(dst, xnT[:, k], w, start=(k == 0), stop=False)
                    mm = pe.matmul(dst, pick[:, bass.ds(e, 1), :].rearrange("p a n -> p (a n)"), b1_parts[:, half * HID:(half + 1) * HID], start=False, stop=True)
                    mm.then_inc(ev("u_ps"), 1)
                pe.wait_ge(ev("act"), m + 1)
                for k in range(4):
                    mm = pe.transpose(ps_o[:, k * P:(k + 1) * P], E[2][:, k * P:(k + 1) * P], identf[:])
                mm.then_inc(ev("actT_ps"), 1)
                pe.wait_ge(ev("actT"), m + 1)
                for k in range(4):
                    w = W2[:, bass.ds(e, 1), k].rearrange("p a n -> p (a n)")
                    pe.matmul(ps_u[1][:, 0:D], E[1][:, k * P:(k + 1) * P], w, start=(k == 0), stop=False)
                pe.matmul(ps_u[1][:, 0:D], pick[:, bass.ds(e, 1), :].rearrange("p a n -> p (a n)"), b2_parts[:], start=False, stop=True).then_inc(ev("y_ps"), 1)

        @block.scalar
        def _(act):
            def copy(dst, src, name):
                act.activation(dst, src, ACT.Copy).then_inc(ev(name), 1)

            def cross_tile(t):
                act.wait_ge(ev("xnT_ps"), t + 1)
                copy(xnT[:].rearrange("p k n -> p (k n)"), ps_z[:, 0:256], "xnT")
                for u in range(3):
                    act.wait_ge(ev("s_keys"), t * 3 + u + 1)
                    n = 1024 if u < 2 else 512
                    act.activation(E[u][:, 0:n], ps_u[u][:, 0:n], ACT.Exp).then_inc(ev("probs"), 1)
                act.wait_ge(ev("oT_ps"), t + 1)
                copy(oT[:], ps_o[:], "oT")
                act.wait_ge(ev("onT_ps"), t + 1)
                copy(onT[:].rearrange("p k n -> p (k n)"), ps_z[:, 0:256], "onT")

            def qkv_tile(t, y):
                act.wait_ge(ev("y0"), t + 1)
                act.activation(sq[:, 0:D], y, ACT.Square, scale=D ** -0.5, accum_out=ss[:]).then_inc(ev("y0_ss"), 1)
                act.wait_ge(ev("hT_ps"), t + 1)
                copy(xnT[:].rearrange("p k n -> p (k n)"), ps_z[:, 0:256], "hT")

            def units(b, j):
                base = 2 * (j * (j + 1) // 2)
                per = ST * (ST + 1)
                for u in range(2 * (j + 1)):
                    act.wait_ge(ev("u_scores"), b * per + base + u + 1)
                    if base + u >= 3:
                        act.wait_ge(ev("u_values"), b * per + base + u - 2)
                    act.activation(E[(base + u) % 3][:], ps_u[(base + u) % 3][:], ACT.Exp).then_inc(ev("u_probs"), 1)
                act.wait_ge(ev("u_values"), b * per + base + 2 * (j + 1))
                copy(oT[:], ps_o[:], "so_T")

            def tail_self(t):
                act.wait_ge(ev("soT_ps"), t + 1)
                copy(onT[:].rearrange("p k n -> p (k n)"), ps_z[:, 0:256], "soT")
                act.wait_ge(ev("gate_ps"), t + 1)
                act.activation(gt[:], ps_z[:, 256:512], ACT.Exp, bias=nb_gate[:], scale=-1.0).then_inc(ev("gate_exp"), 1)
                act.wait_ge(ev("x2"), t + 1)
                act.activation(sq[:, 0:D], x2[:], ACT.Square, scale=D ** -0.5, accum_out=ss[:]).then_inc(ev("x2_ss"), 1)
                act.wait_ge(ev("h2T_ps"), t + 1)
                copy(xnT[:].rearrange("p k n -> p (k n)"), ps_z[:, 256:512], "h2T")

            with act.Fori(0, B) as b:
                with act.Fori(0, ST) as j:
                    cross_tile(b * ST + j)
                    qkv_tile(b * ST + j, y0[:, bass.ds(j, 1), :].rearrange("p a n -> p (a n)"))
                for j in range(ST):
                    units(b, j)
                    tail_self(b * ST + j)
            if STAGE == 1:
                return
            with act.Fori(0, MT) as m:
                act.wait_ge(ev("rowsT_ps"), m + 2)
                copy(xnT[:].rearrange("p k n -> p (k n)"), ps_z[:, 0:256], "rowsT")
                act.wait_ge(ev("u_ps"), 2 * m + 1)
                act.activation(E[0][:, 0:HID], ps_u[0][:, HID:2 * HID], ACT.Sigmoid).then_inc(ev("sig"), 1)
                act.wait_ge(ev("actT_ps"), m + 1)
                copy(E[1][:, 0:HID], ps_o[:], "actT")

        @block.vector
        def _(dve):
            tt, ts, stt = dve.tensor_tensor, dve.tensor_scalar, dve.scalar_tensor_tensor

            def parts(own, tok, rows, heads, src, scale, hi, mid, lo, done):
                v = tok[0:rows, :, 0:RS].rearrange("p h (s d) -> p h s d", d=HD)
                s4 = src.rearrange("p (h s d) -> p h s d", s=1, d=HD)
                for sl in hi:
                    n = len(range(*sl.indices(PARTS)))
                    own.link(ts(v[:, :, sl], s4.to_broadcast([rows, heads, n, HD]), scale, None, ALU.mult))
                r4 = rest[0:rows, 0:heads * HD].rearrange("p (h s d) -> p h s d", s=1, d=HD)
                r3 = rest[0:rows, 0:heads * HD].rearrange("p (h d) -> p h d", d=HD)
                s3 = src.rearrange("p (h d) -> p h d", d=HD)
                at = lambda sl: v[:, :, range(*sl.indices(PARTS))[0]]
                own.link(stt(r3, s3, scale, at(hi[0]), ALU.mult, ALU.subtract))
                for sl in mid:
                    n = len(range(*sl.indices(PARTS)))
                    own.link(dve.tensor_copy(v[:, :, sl], r4.to_broadcast([rows, heads, n, HD])))
                tt(at(lo[0]), r3, at(mid[0]), ALU.subtract).then_inc(ev(done), 1)

            Q = dict(hi=(slice(0, 3),), mid=(slice(3, 5),), lo=(slice(5, 6),))
            K = dict(hi=(slice(0, 4, 3), slice(5, 6)), mid=(slice(1, 5, 3),), lo=(slice(2, 3),))

            def ctx_tiles(b):
                own = Own(dve, ev("d_ctx"), b * N_CTX)
                dve.wait_ge(ev("ctx_proj"), b + 1)
                v3 = lambda ap: ap.rearrange("p (h d) -> p h d", d=HD)
                own.link(tt(Vx[:, :, 0:HD], v3(ps_u[0][:, 256:512]), v3(xbias[:, 2]), ALU.add))
                for q in range(4):
                    r = slice(32 * q, 32 * q + CR)
                    vr = Vr[r, :, 32 * q:32 * q + HD]
                    own.link(tt(vr, v3(ps_u[1][r, 0:D])[:, q:H:4], v3(xbias[r, 2])[:, q:H:4], ALU.add)) if q == 3 else \
                        tt(vr, v3(ps_u[1][r, 0:D])[:, q:H:4], v3(xbias[r, 2])[:, q:H:4], ALU.add)
                for n, (rows, col, at) in enumerate(((P, 0, 0), (CR, 512, P))):
                    own.link(tt(qf[0:rows], ps_u[0][0:rows, col:col + D], xbias[0:rows, 1], ALU.add))
                    parts(own, q_tok, rows, H, qf[0:rows], 1.0, done="k_split", **K)
                    dve.wait_ge(ev("k_turned"), b * 2 + n + 1)
                    ub = ps_u[2][:].bitcast(bf16).rearrange("p (h n) -> p h n", n=P)
                    i = dve.tensor_copy(Kx[0:RS, :, at:at + rows], ub[0:RS, :, 0:rows])
                    i.then_inc(ev("k_ready"), 1)
                assert own.n == N_CTX, own.n

            def norm(own, src, dst, n):
                alone(dve)
                own.link(dve.bn_stats(stats[:], src))
                alone(dve)
                dve.bn_aggr(mv[:], stats[:]).then_inc(ev("mv"), 1)
                dve.wait_ge(ev("rstd"), n)
                return ts(dst, src, mv[:, 0:1], rstd[:], ALU.subtract, ALU.mult)

            def cross_tile(own, t, j):
                row = lambda buf: buf[:, bass.ds(j, 1), :].rearrange("p a n -> p (a n)")
                norm(own, row(xb), xn[:], 2 * t + 1).then_inc(ev("xn"), 1)
                dve.wait_ge(ev("q_ps"), t + 1)
                own.link(tt(qf[:], ps_z[:, 256:512], xbias[:, 0], ALU.add))
                parts(own, q_tok, P, H, qf[:], SCALE, done="q_split", **Q)
                dve.wait_ge(ev("q_turned"), t + 1)
                ub = ps_u[0][:].bitcast(bf16)
                dve.tensor_copy(Qst[0:RS].rearrange("p h n -> p (h n)"), ub[0:RS, :]).then_inc(ev("q_stack"), 1)
                for c in range(6):
                    n = 3 if c < 5 else 1
                    dve.wait_ge(ev("s_rows"), t * 6 + c + 1)
                    src = ps_u[(c // 2 + 1) % 3][:, (c % 2) * 512:(c % 2) * 512 + n * C].rearrange("p (h n) -> p h n", n=C)
                    i = dve.tensor_reduce(out=mx[:, 3 * c:3 * c + n], in_=src, axis=AX.X, op=ALU.max)
                own.link(i)
                own.link(ts(nmx[:, 0], mx[:], -1.0, None, ALU.mult))
                stt(nmx[:, 1], mx[:], -1.0, nmx[:, 0], ALU.mult, ALU.subtract).then_inc(ev("shift"), 1)
                dve.wait_ge(ev("shiftT_ps"), t + 1)
                own.link(dve.tensor_copy(nmT[RS:P, 0, :], ps_z[:].bitcast(bf16)[RS:P, 0:P]))
                dve.tensor_copy(Qst[RS:P], nmT[RS:P].to_broadcast([P - RS, H, P])).then_inc(ev("shiftT"), 1)
                normalise(own, "o_ps", "on", t)
                dve.wait_ge(ev("xo_ps"), t + 1)
                own.link(tt(row(xb), row(xb), ps_z[:, 256:512], ALU.add))
                own.link(tt(row(xb), row(xb), xbias[:, 3], ALU.add))
                norm(own, row(xb), row(y0), 2 * t + 2).then_inc(ev("y0"), 1)

            def normalise(own, ready, done, t):
                dve.wait_ge(ev(ready), t + 1)
                o4 = ps_o[:].rearrange("p (h n) -> p h n", n=32)
                own.link(dve.reciprocal(rsum[:], o4[:, :, HD]))
                if done == "on":
                    src, dst, r = o4[:, :, 0:HD], on[:].rearrange("p (h d) -> p h d", d=HD), rsum[:]
                    tt(dst, src, r.rearrange("p (h d) -> p h d", d=1).to_broadcast([P, H, HD]), ALU.mult).then_inc(ev(done), 1)
                else:
                    dst4 = on[:].rearrange("p (g q d) -> p g q d", g=KV, d=HD)
                    for q in range(HQ):
                        r = rsum[:, KV * q:KV * q + KV].rearrange("p (g d) -> p g d", d=1).to_broadcast([P, KV, HD])
                        i = tt(dst4[:, :, q], o4[:, KV * q:KV * q + KV, 0:HD], r, ALU.mult)
                    i.then_inc(ev(done), 1)

            def qkv_tile(own, t, j):
                row = lambda buf: buf[:, bass.ds(j, 1), :].rearrange("p a n -> p (a n)")
                dve.wait_ge(ev("y0_rs"), t + 1)
                stt(hh[:], row(y0), rs_row[:], ln1[:], ALU.mult, ALU.mult).then_inc(ev("hh"), 1)
                dve.wait_ge(ev("qkv_ps"), t + 1)
                own.link(tt(qkv[:], ps_o[:, 0:QKV], b_qkv[:], ALU.add))
                dve.tensor_copy(Va[:, bass.ds(j, 1), :, 0:HD].rearrange("p a g d -> p (a g) d"), qkv[:, NH2 * HD:].rearrange("p (g d) -> p g d", d=HD))
                n = NH2 * HD
                own.link(stt(sq[:, 0:n], qkv[:, 0:n], 1.0 / HD, qkv[:, 0:n], ALU.mult, ALU.mult))
                dve.tensor_reduce(out=hs[:], in_=sq[:, 0:n].rearrange("p (h d) -> p h d", d=HD), axis=AX.X, op=ALU.add).then_inc(ev("h_ms"), 1)
                h3 = lambda buf: buf[:, 0:n].rearrange("p (h d) -> p h d", d=HD)
                cb = rope_c[:, bass.ds(j, 1), :].to_broadcast([P, NH2, HD])
                tt(h3(ra), h3(qkv), cb, ALU.mult)
                for half in range(2):
                    o, f = half * (HD // 2), (1 - half) * (HD // 2)
                    sn = rope_s[:, bass.ds(j, 1), o:o + HD // 2].to_broadcast([P, NH2, HD // 2])
                    i = tt(h3(rb)[:, :, o:o + HD // 2], h3(qkv)[:, :, f:f + HD // 2], sn, ALU.mult)
                own.link(i)
                own.link(tt(ra[:], ra[:], rb[:], ALU.add))
                dve.wait_ge(ev("h_rs"), t + 1)
                own.link(tt(h3(ra), h3(ra), h_rs[:].rearrange("p (h d) -> p h d", d=1).to_broadcast([P, NH2, HD]), ALU.mult))
                own.link(tt(ra[:, D:n], ra[:, D:n], qk_w[:].rearrange("p h d -> p (h d)")[:, D:n], ALU.mult))
                tt(row(q_hat), ra[:, 0:D], qk_w[:].rearrange("p h d -> p (h d)")[:, 0:D], ALU.mult)
                parts(own, ks_tok, P, KV, ra[:, D:n], 1.0, done="ks_split", **K)
                dve.wait_ge(ev("ks_turned"), t + 1)
                dve.tensor_copy(Kst[0:RS + 1, :, bass.ds(j * P, P)],
                                ps_z[:].bitcast(bf16)[0:RS + 1, 0:KV * P].rearrange("p (g n) -> p g n", n=P)).then_inc(ev("ks_stack"), 1)

            def prep_self(own, b, j):
                parts(own, qs_tok, P, H, q_hat[:, j], SCALE, done="qs_split", **Q)
                dve.wait_ge(ev("qs_turned"), b * ST + j + 1)
                dve.tensor_copy(Qst[0:RS + 1].rearrange("p h n -> p (h n)"), ps_u[0][:].bitcast(bf16)[0:RS + 1, :]).then_inc(ev("qs_stack"), 1)

            def tail_self(own, b, j):
                t = b * ST + j
                normalise(own, "so_ps", "so_n", t)
                dve.wait_ge(ev("gate_exp"), t + 1)
                own.link(ts(gt[:], gt[:], 1.0, None, ALU.add))
                own.link(dve.reciprocal(gt[:], gt[:]))
                tt(gt[:], gt[:], onT[:].rearrange("p k n -> p (k n)"), ALU.mult).then_inc(ev("gated"), 1)
                dve.wait_ge(ev("wo_ps"), t + 1)
                own.link(tt(x2[:], y0[:, j], ps_z[:, 0:256], ALU.add))
                tt(x2[:], x2[:], b_o[:], ALU.add).then_inc(ev("x2"), 1)
                dve.wait_ge(ev("x2"), t + 1)
                dve.wait_ge(s_st, 32 * t + 32)
                tt(base[:], x2[:], xb[:, j], ALU.add).then_inc(ev("base"), 1)
                dve.wait_ge(ev("x2_rs"), t + 1)
                stt(h2[:], x2[:], rs_row[:], ln2[:], ALU.mult, ALU.mult).then_inc(ev("h2"), 1)
                dve.wait_ge(ev("logit_ps"), t + 1)
                tt(logits[:, bass.ds(t, 1), :].rearrange("p a e -> p (a e)"), ps_z[:, 0:NE], b_r[:], ALU.add).then_inc(ev("logits"), 1)

            dve.wait_ge(s_w, NW * 16)
            dve.wait_ge(ev("cleared"), N_CLEARED)
            own = Own(dve, ev("d_first"), 0)
            dve.tensor_copy(identb[:], identf[:])
            dve.tensor_copy(pick[:].rearrange("p e n -> p (e n)"), pick_f)
            own.link(dve.tensor_copy(Kx[RS:P].rearrange("p h n -> p (h n)"), which_f))
            own.link(ts(nb_gate[:], b_gate[:], -1.0, None, ALU.mult))
            own.link(tt(ra[:, 0:HD], qk_w[:, 0], qk_w[:, H], ALU.mult))
            own.link(dve.tensor_reduce(out=bshift[:], in_=ra[:, 0:HD], axis=AX.X, op=ALU.max, apply_absolute_value=True))
            own.link(ts(bshift[:], bshift[:], -SCALE * HD, None, ALU.mult))
            own.link(dve.tensor_copy(qs_tok[:, :, RS:RS + 1], bshift[:].rearrange("p (a b) -> p a b", a=1).to_broadcast([P, H, 1])))
            for src, dst, n in ((E[0], b1_parts, 2 * HID), (E[1], b2_parts, D)):
                tb = E[2][:].bitcast(bf16)
                for r in (0, 32, 64):
                    g = slice(r, r + NE)
                    for left_over in range(r // 32):
                        own.link(dve.tensor_copy(tb[g, 0:n], src[g, 0:n]))
                        own.link(tt(src[g, 0:n], src[g, 0:n], tb[g, 0:n], ALU.subtract))
                    own.link(dve.tensor_copy(dst[g, 0:n], src[g, 0:n]))
            with dve.Fori(0, B) as b:
                dve.wait_ge(s_x, b * 16 + 16)
                ctx_tiles(b)
                with dve.Fori(0, ST) as j:
                    own = Own(dve, ev("d_x"), (b * ST + j) * N_X)
                    cross_tile(own, b * ST + j, j)
                    qkv_tile(own, b * ST + j, j)
                    assert own.n == N_X, own.n
                own = Own(dve, ev("d_self"), b * N_SELF)
                for j in range(ST):
                    prep_self(own, b, j)
                    tail_self(own, b, j)
                assert own.n == N_SELF, own.n
            if STAGE == 1:
                return

            own = Own(dve, ev("d_route"), 0)
            te = lambda ap: ap.rearrange("p (t e) -> p t e", e=1).to_broadcast([P, T, NE])
            dve.wait_ge(ev("logits"), T)
            own.link(dve.tensor_reduce(out=best[:], in_=logits[:], axis=AX.X, op=ALU.max))
            own.link(tt(ev_[:], logits[:], te(best[:]), ALU.is_ge))
            own.link(tt(ev_[:], ev_[:], count_e[:].rearrange("p (a e) -> p a e", a=1).to_broadcast([P, T, NE]), ALU.mult))
            own.link(dve.tensor_reduce(out=best[:], in_=ev_[:], axis=AX.X, op=ALU.max))
            tt(onehot[:], ev_[:], te(best[:]), ALU.is_equal).then_inc(ev("onehot"), 1)
            dve.wait_ge(ev("ranks"), 1)
            own.link(dve.tensor_copy(total[:], ps_u[0][:, 512:512 + T * NE].rearrange("p (t e) -> p e t", e=NE)))
            for e in range(NE):
                i = dve.tensor_tensor_scan(cum[:, e], ones[:, 0:T], total[:, e], 0.0, ALU.mult, ALU.add)
            own.link(i)
            own.link(ts(padded[:], cum[:, :, T - 1], float(P - 1), None, ALU.add))
            own.link(dve.tensor_copy(whole[:], padded[:]))
            own.link(ts(whole[:], whole[:], ((1 << 24) - 1) // P * P, None, ALU.bitwise_and))
            own.link(dve.tensor_copy(padded[:], whole[:]))
            own.link(dve.tensor_tensor_scan(offset[:], ones[:, 0:NE], padded[:], 0.0, ALU.mult, ALU.add))
            own.link(tt(offset[:], offset[:], padded[:], ALU.subtract))
            own.link(tt(cum[:], cum[:], total[:], ALU.subtract))
            own.link(tt(cum[:], cum[:], offset[:].rearrange("p (e t) -> p e t", t=1).to_broadcast([P, NE, T]), ALU.add))
            own.link(tt(ev_[:], ps_u[0][:, 0:T * NE].rearrange("p (t e) -> p t e", e=NE), cum[:].rearrange("p e t -> p t e"), ALU.add))
            own.link(tt(ev_[:], ev_[:], onehot[:], ALU.mult))
            own.link(dve.tensor_reduce(out=placef[:], in_=ev_[:], axis=AX.X, op=ALU.add))
            own.link(dve.tensor_copy(place[:], placef[:]))
            own.link(tt(owns[:], tile_row[:].rearrange("p (m e) -> p m e", e=1).to_broadcast([P, MT, NE]),
                        offset[:].rearrange("p (m e) -> p m e", m=1).to_broadcast([P, MT, NE]), ALU.is_ge))
            own.link(dve.tensor_reduce(out=expertf[:], in_=owns[:], axis=AX.X, op=ALU.add))
            own.link(ts(expertf[:], expertf[:], -1.0, None, ALU.add))
            dve.tensor_copy(expert[:], expertf[:]).then_inc(ev("places"), 1)

            with dve.Fori(0, MT) as m:
                dve.wait_ge(ev("u_ps"), 2 * m + 2)
                dve.wait_ge(ev("sig"), m + 1)
                tt(E[2][:, 0:HID], ps_u[0][:, 0:HID], E[0][:, 0:HID], ALU.mult).then_inc(ev("act"), 1)
                dve.wait_ge(ev("y_ps"), m + 1)
                dve.wait_ge(s_yr, 16 * m + 16)
                dve.tensor_copy(yr, ps_u[1][:, 0:D]).then_inc(ev("y_rows"), 1)
            for t in range(T):
                dve.wait_ge(s_bl[t % 2], 16 * (t // 2 + 1))
                dve.wait_ge(s_gt[t % 2], 16 * (t // 2 + 1))
                if t >= 2:
                    dve.wait_ge(s_out[t % 2], 16 * (t // 2))
                tt(fin[t % 2], got[t % 2], rows[t % 2], ALU.add).then_inc(ev("summed"), 1)


def rope_tables():
    inv = (np.float32(1.0) / np.float32(10000.0) ** (np.arange(0, HD, 2, dtype=np.float32) / np.float32(HD))).astype(np.float32)
    f = (np.arange(S, dtype=np.float32)[:, None] * inv[None, :]).astype(np.float32)
    c, s = np.cos(f.astype(np.float64)).astype(np.float32), np.sin(f.astype(np.float64)).astype(np.float32)
    return np.concatenate([c, c], 1), np.concatenate([-s, s], 1)


def layout(inputs):
    g = {k: np.asarray(v) for k, v in inputs.items()}
    f, x = "L0_ffn_", "L0_xattn_"
    r = {"x": g["x"].reshape(B * S, D), "ctxT": np.ascontiguousarray(g["ctx_1024"].transpose(0, 2, 1))}
    r["xw"] = np.stack([g[x + n].T for n in ("Wq", "Wk", "Wv", "Wo")])
    r["xb"] = np.stack([g[x + n] for n in ("bq", "bk", "bv", "bo")])
    r["w_qkv"] = np.concatenate([g[f + "Wq"], g[f + "Wk"], g[f + "Wv"]], 1)
    r["b_qkv"] = np.concatenate([g[f + "bq"], g[f + "bk"], g[f + "bv"]])[None]
    r["qk_w"] = np.concatenate([np.tile(g[f + "qn_w"], H), np.tile(g[f + "kn_w"], KV)])[None]
    for n, k in (("bo", "bo"), ("br", "br"), ("ln1", "ln1_w"), ("ln2", "ln2_w")):
        r[n] = g[f + k][None]
    for n in ("Wo", "Wr", "W1", "W2"):
        r[f + n] = g[f + n]
    w = np.zeros((P, P), g[f + "Wg"].dtype)
    for i in range(P // HD):
        w[i * HD:(i + 1) * HD, i * HD:(i + 1) * HD] = g[f + "Wg"]
    r["w_gate"] = w
    r["b_gate"] = np.tile(g[f + "bg"], P // HD)[:, None]
    for n, k in (("b1_rows", "b1"), ("b2_rows", "b2")):
        v = np.zeros((P, g[f + k].shape[1]), g[f + k].dtype)
        for s in range(3):
            v[32 * s:32 * s + NE] = g[f + k]
        r[n] = v
    r["identf"] = np.eye(P, dtype=np.float32)
    r["upper"], r["ones"] = np.triu(np.ones((P, P), np.float32), 1), np.ones((P, P), np.float32)
    r["count_e"] = (NE - np.arange(NE, dtype=np.float32))[None]
    r["tile_row"] = (P * np.arange(MT, dtype=np.float32))[None]
    r["rope_c"], r["rope_s"] = rope_tables()
    pick = np.zeros((P, NE, P), np.float32)
    which = np.zeros((2 * H, H, P + KR), np.float32)
    for s in range(3):
        for e in range(NE):
            pick[32 * s + e, e] = 1
    for s in range(2):
        for h in range(H):
            which[s * H + h, h, 0:C] = 1
    r["pick"], r["which_head"] = pick.reshape(P, -1), which.reshape(2 * H, -1)
    return {k: np.ascontiguousarray(v) for k, v in r.items()}


def kernel(**inputs):
    import concourse.bacc as bacc
    from concourse.bass_utils import run_bass_kernel_spmd

    nc = bacc.Bacc("TRN2", target_bir_lowering=False, num_devices=1)
    arrays = layout(inputs)
    aps = {n: nc.dram_tensor(f"in_{n}", v.shape, mybir.dt.from_np(v.dtype), kind="ExternalInput").ap() for n, v in arrays.items()}
    out = nc.dram_tensor("out", (B * S, D), fp32, kind="ExternalOutput").ap()
    build(nc, aps, out)
    r = run_bass_kernel_spmd(nc, [{f"in_{n}": v for n, v in arrays.items()}], core_ids=[0])
    return r.results[0]["out"].reshape(B, S, D)
```

```python
import numpy as np
import concourse.bass as bass
from concourse import mybir
from contextlib import ExitStack

fp32 = mybir.dt.float32
bf16 = mybir.dt.bfloat16
i32 = mybir.dt.int32
u32 = mybir.dt.uint32
ALU = mybir.AluOpType
ACT = mybir.ActivationFunctionType
AX = mybir.AxisListType

P = 128
B, S, D = 4, 1024, 256
C = 154
CR = C - P
KR = 32
H, HD = 16, 16
KV = 4
HQ = H // KV
ST = S // P
T = B * ST
NE, HID = 8, 512
MT = T + NE - 1
PARTS = 6
RS = PARTS * HD
QKV = D + 2 * KV * HD
NH2 = H + KV
EPS_LN, EPS_RMS = 1e-5, 1e-6
SCALE = HD ** -0.5

TILE_ORDER = (7, 0, 6, 1, 5, 2, 4, 3)
PAIRS = [(n, i) for n, j in enumerate(TILE_ORDER) for i in (j, *range(j))]
FIRST = [next(s for s, p in enumerate(PAIRS) if p[0] == n) for n in range(ST)]
LEAD = 2
TAIL_STEPS, X_STEPS, CTX_STEPS = 8, 20, 6
X_FIRST, X_EVERY, TAIL_EVERY = 2, 3, 4
SLOTS = 60


def tail_starts():
    out = []
    for n in range(ST):
        end = LEAD + FIRST[n] + TILE_ORDER[n] + 2
        out.append(max(end, out[-1] + TAIL_EVERY if out else 0))
    return out


def prep_starts():
    out = [LEAD + FIRST[n] - 3 for n in range(ST)]
    for n in reversed(range(ST - 1)):
        out[n] = min(out[n], out[n + 1] - 2)
    return out


def slot(s, second, first):
    tails = tail_starts()
    p = s - LEAD
    if second:
        if s == 0:
            yield "swap", 0, 0
        for half in range(2):
            if 0 <= p < len(PAIRS):
                yield "scores", p, half
            if 0 < p <= len(PAIRS):
                yield "values", p - 1, half
        for n in range(ST):
            if p == FIRST[n] + TILE_ORDER[n] + 1:
                yield "flush", 0, n
        for n in range(ST):
            if 0 <= s - tails[n] < TAIL_STEPS:
                yield "tail", s - tails[n], n
        for n in range(ST):
            at = prep_starts()[n]
            if n == 0:
                if s < 2:
                    yield from (("prep", 0, 0), ("prep", 1, 0)) if s == 0 else (("prep", 2, 0),)
            elif 0 <= s - at < 3:
                yield "prep", s - at, n
    if first:
        if s < CTX_STEPS:
            yield "ctx", s, 0
        for k in range(ST):
            r = s - X_FIRST - X_EVERY * k
            if r == 4:
                yield "q_stack", 0, k
            if 0 <= r < X_STEPS:
                yield "x", r, k


def frees(step):
    kind, r, _ = step
    return kind == "prep" and r == 2 or kind == "ctx" and r % 2 == 1 or kind == "q_stack"


def order(second, first):
    for s in range(SLOTS):
        yield from sorted(slot(s, second, first), key=lambda step: not frees(step))


U, M = "u", "m"
N_U, N_M, N_E = 2, 3, 5


def results(step):
    kind, r, k = step
    if kind == "scores":
        return [(U, ("s", r, k))]
    if kind == "prep":
        return [(U, ("qs", k))] if r == 1 else []
    if kind == "tail":
        return {0: [(M, ("so", k))], 1: [(M, ("soT", k))], 2: [(M, ("gate", k))], 3: [(M, ("wo", k))],
                5: [(M, ("h2T", k))], 6: [(M, ("logit", k))]}.get(r, [])
    if kind == "ctx":
        return {0: [(U, ("kv",)), (U, ("vr",))], 2: [(U, ("kT", 0))], 4: [(U, ("kT", 1))]}.get(r, [])
    if kind == "x":
        return {1: [(M, ("xnT", k))], 2: [(M, ("q", k))], 3: [(U, ("qT", k))],
                4: [(M, ("row", k, 0)), (M, ("row", k, 1))], 5: [(M, ("row", k, 2)), (M, ("row", k, 3))],
                6: [(M, ("row", k, 4)), (M, ("row", k, 5))], 7: [(M, ("shift", k))],
                8: [(U, ("key", k, 0)), (U, ("key", k, 1)), (U, ("key", k, 2))],
                9: [(M, ("oT", k))], 10: [(M, ("o", k))], 11: [(M, ("onT", k))], 12: [(M, ("xo", k))],
                15: [(M, ("hT", k))], 16: [(M, ("qkv", k))], 18: [(M, ("ksT", k))]}.get(r, [])
    return []


def exponentials(step):
    kind, r, k = step
    if kind == "scores":
        return [("s", r, k)]
    if kind == "x" and r == 8:
        return [("key", k, n) for n in range(3)]
    return []


class Turns:

    def __init__(self, sections, n, sems, names):
        self.n, self.sems, self.place, self.uses = n, sems, {}, {}
        for sec in sections:
            used = [0] * n
            turn = 0
            for step in sections[sec]:
                for name in names(step):
                    i = turn % n
                    self.place[sec, name] = (i, used[i])
                    used[i] += 1
                    turn += 1
            self.uses[sec] = used

    def at(self, sec, b, name):
        i, k = self.place[sec, name]
        if sec == "body":
            k = k + self.uses["pro"][i] + b * self.uses["body"][i]
        elif sec == "epi":
            k = k + self.uses["pro"][i] + (B - 1) * self.uses["body"][i]
        return i, self.sems[i], k, k + 1


def build(nc, a, out):
    ctx = ExitStack()
    with ctx:
        def sb(name, shape, dt=fp32):
            return ctx.enter_context(nc.sbuf_tensor(name, shape, dt))

        def ps(name, shape, dt=fp32):
            return ctx.enter_context(nc.psum_tensor(name, shape, dt))

        def sem(name):
            return ctx.enter_context(nc.semaphore(name))

        rows_dram = nc.dram_tensor("token_rows", ((T + 1) * P, 2 * D), fp32, kind="Internal").ap()

        identf = sb("identf", [P, P])
        identb = sb("identb", [P, P], bf16)
        xw = sb("xw", [P, 4, 2, D])
        xbias = sb("xbias", [P, 4, D])
        w_qkv = sb("w_qkv", [P, 2, QKV])
        b_qkv = sb("b_qkv", [P, QKV])
        w_o = sb("w_o", [P, 2, D])
        b_o = sb("b_o", [P, D])
        w_gate = sb("w_gate", [P, P])
        b_gate = sb("b_gate", [P, 1])
        w_r = sb("w_r", [P, 2, NE])
        b_r = sb("b_r", [P, NE])
        ln1 = sb("ln1", [P, D])
        ln2 = sb("ln2", [P, D])
        qk_w = sb("qk_w", [P, NH2, HD])
        rope_c = sb("rope_c", [P, ST, HD])
        rope_s = sb("rope_s", [P, ST, HD])
        W1 = sb("W1", [P, NE, 2, 2 * HID])
        W2 = sb("W2", [P, NE, HID // P, D])
        rows_w2 = W2[:].rearrange("p e k n -> p (e k n)")
        taken = 0

        def room(n_words):
            nonlocal taken
            taken += n_words
            assert taken <= NE * HID // P * D
            return rows_w2[:, taken - n_words:taken]

        b1_parts = sb("b1_parts", [P, 2 * HID], bf16)
        b2_parts = sb("b2_parts", [P, D], bf16)
        pick = sb("pick", [P, NE, P], bf16)
        bshift = sb("bshift", [P, 1])
        upper = sb("upper", [P, P])
        ones = sb("ones", [P, P])
        count_e = sb("count_e", [P, NE])
        tile_row = sb("tile_row", [P, MT])
        tile_no = sb("tile_no", [P, MT])
        row_no = sb("row_no", [P, P])
        token = sb("token", [P, T])
        spare = sb("spare", [P, 1])
        zero_rows = sb("zero_rows", [P, 2 * D])

        ctxT = sb("ctxT", [P, 2, C])
        kf = sb("kf", [P, D])
        kl = sb("kl", [P, D])
        k_rest = sb("k_rest", [P, D])
        k_tok = room(H * RS // 2).bitcast(bf16).rearrange("p (h n) -> p h n", n=RS)
        Kx = sb("Kx", [P, H, P + KR], bf16)
        Vx = sb("Vx", [P, H, 32])
        Vr = sb("Vr", [P, H // 4, P])
        stats = [sb(f"stats{i}", [P, 6]) for i in range(2)]
        mv = [sb(f"mv{i}", [P, 2]) for i in range(2)]
        rstd = [sb(f"rstd{i}", [P, 1]) for i in range(2)]
        xn = sb("xn", [P, D])
        xnT = sb("xnT", [P, 2 * P])
        qf = sb("qf", [P, D])
        rest = sb("rest", [P, D])
        q_tok = room(H * RS // 2).bitcast(bf16).rearrange("p (h n) -> p h n", n=RS)
        Qx = [room(H * P // 2).bitcast(bf16).rearrange("p (h n) -> p h n", n=P) for i in range(2)]
        mx = sb("mx", [P, H])
        nmx = sb("nmx", [P, 2, H], bf16)
        nmT = sb("nmT", [P, 1, P], bf16)
        oT = sb("oT", [P, 512])
        rsum = sb("rsum", [P, H])
        on = sb("on", [P, D])
        onT = sb("onT", [P, 2 * P])
        ss = sb("ss", [P, 1])
        rs_row = sb("rs_row", [P, 1])
        hh = sb("hh", [P, D])
        hT = sb("hT", [P, 2 * P])
        sq = sb("sq", [P, NH2 * HD])
        sqa = sb("sqa", [P, D])
        qkv = sb("qkv", [P, QKV])
        hs = sb("hs", [P, NH2])
        h_rs = sb("h_rs", [P, NH2])
        ra = sb("ra", [P, NH2 * HD])
        rb = sb("rb", [P, NH2 * HD])
        ks_rest = sb("ks_rest", [P, KV * HD])
        ks_tok = sb("ks_tok", [P, KV, RS + 1], bf16)
        safe = {name: sb(f"safe_{name}", [P, NH2]) for name in ("rstd0", "rstd1", "y0_rs", "h_rs", "x2_rs")}
        minus_half = sb("minus_half", [P, NH2])
        Va_next = sb("Va_next", [P, ST, KV, 32])

        E = [sb(f"E{i}", [P, 1024]) for i in range(N_E)]

        rows_w1 = W1[:].rearrange("p e k n -> p (e k n)")
        xb = rows_w1[:, 0:4096].rearrange("p (j n) -> p j n", n=D)
        y0 = rows_w1[:, 4096:8192].rearrange("p (j n) -> p j n", n=D)
        q_hat = rows_w1[:, 8192:12288].rearrange("p (j n) -> p j n", n=D)
        Kst = rows_w1[:, 12288:16384].bitcast(bf16).rearrange("p (c g n) -> p c g n", c=2, g=KV)
        Va = sb("Va", [P, ST, KV, 32])
        qs_rest = room(D)
        qs_tok = sb("qs_tok", [P, H, RS + 1], bf16)
        Qs = [room(H * P // 2).bitcast(bf16).rearrange("p (h n) -> p h n", n=P) for i in range(2)]
        soT = [room(512) for i in range(2)]
        s_rsum = sb("s_rsum", [P, H])
        s_on = room(D)
        s_onT = room(2 * P)
        gt = room(2 * P)
        x2 = room(D)
        s_sqa = room(D)
        s_ss = sb("s_ss", [P, 1])
        s_rs = sb("s_rs", [P, 1])
        base = sb("base", [P, D])
        h2 = sb("h2", [P, D])
        h2T = sb("h2T", [P, 2 * P])
        nb_gate = sb("nb_gate", [P, 1])
        logits = sb("logits", [P, T, NE])

        onehot = sb("onehot", [P, T, NE])
        first_e = sb("first_e", [P, T, NE])
        best = sb("best", [P, T])
        total = sb("total", [P, NE, T])
        cum = sb("cum", [P, NE, T])
        padded = sb("padded", [P, NE])
        whole = sb("whole", [P, NE], i32)
        offset = sb("offset", [P, NE])
        placef = sb("placef", [P, T])
        place = sb("place", [P, T], i32)
        place_tile = sb("place_tile", [P, T])
        place_row = sb("place_row", [P, T])
        split_i = sb("split_i", [P, 2, T], i32)
        taken_by = sb("taken_by", [P, MT])
        ids = sb("ids", [P, MT])
        idx = sb("idx", [P, MT], u32)
        idx_in = [sb(f"idx_in{i}", [P, 1], u32) for i in range(2)]
        idx_out = [sb(f"idx_out{i}", [P, 1], u32) for i in range(2)]
        G = T // 4
        row_hot = [E[g][:, 0:G * P].rearrange("p (t n) -> p t n", n=P) for g in range(4)]
        flat = lambda t: t[:].rearrange("p a b c -> p (a b c)")
        tile_hot = [r[:, 0:G * 2 * MT].rearrange("p (t a n) -> p t a n", a=2, n=MT) for r in
                    (E[4][:], flat(Va), flat(Va_next), Kx[:].rearrange("p h n -> p (h n)").bitcast(fp32))]
        owns = sb("owns", [P, MT, NE])
        expertf = sb("expertf", [P, MT])
        expert = sb("expert", [P, MT], i32)
        part = lambda e, n, w: E[e][:, n * w:(n + 1) * w]
        xr = [E[3][:, i * 2 * D:(i + 1) * 2 * D] for i in range(2)]
        yr, bs = [part(0, i, D) for i in range(2)], [part(0, 2 + i, D) for i in range(2)]
        sig, act_u = [part(1, i, HID) for i in range(2)]
        actT, xT = part(2, 0, HID), [part(2, 2 + i, D) for i in range(2)]

        ps_u = [ps(f"ps_u{i}", [P, 1024]) for i in range(N_U)]
        ps_m = [ps(f"ps_m{i}", [P, 512]) for i in range(N_M)]
        ps_o = ps("ps_o", [P, 512])

        names = {}

        def ev(name):
            if name not in names:
                names[name] = sem(name)
            return names[name]

        s_w = sem("s_w")
        s_big = sem("s_big")
        s_ctx = sem("s_ctx")
        s_x = [sem(f"s_x{i}") for i in range(ST)]
        s_st = sem("s_st")
        s_xr = [sem(f"s_xr{i}") for i in range(2)]
        s_yr = [sem(f"s_yr{i}") for i in range(2)]
        s_spare = sem("s_spare")
        s_alone = sem("s_alone")
        u_read = [sem(f"u_read{i}") for i in range(N_U)]
        m_read = [sem(f"m_read{i}") for i in range(N_M)]
        e_read = [sem(f"e_read{i}") for i in range(N_E)]

        sections = {"pro": list(order(False, True)), "body": list(order(True, True)), "epi": list(order(True, False))}
        turns = {U: Turns(sections, N_U, u_read, lambda st: [n for r, n in results(st) if r == U]),
                 M: Turns(sections, N_M, m_read, lambda st: [n for r, n in results(st) if r == M])}
        e_turns = Turns(sections, N_E, e_read, exponentials)
        last_pair = lambda n: FIRST[n] + TILE_ORDER[n]

        def alone(eng):
            eng.sem_inc(s_alone, 1)

        def wait(eng, sem_, n):
            if not (isinstance(n, int) and n <= 0):
                eng.wait_ge(sem_, n)

        def parity(b):
            return b % 2

        which_f = rows_w1[RS:P, 4096:4096 + H * (P + KR)]
        pick_f = rows_w1[:, 8192:8192 + NE * P]
        small = [
            (identf[:], a["identf"]),
            (which_f, a["which_head"]),
            (pick_f, a["pick"]),
            (E[0][:], a["b1_rows"]),
            (E[1][:, 0:D], a["b2_rows"]),
            (upper[:], a["upper"]), (ones[:], a["ones"]),
            (count_e[:], a["count_e"].to_broadcast([P, NE])),
            (tile_row[:], a["tile_row"].to_broadcast([P, MT])),
            (tile_no[:], a["row_no"][:, 0:MT].to_broadcast([P, MT])),
            (row_no[:], a["row_no"].to_broadcast([P, P])),
            (token[:], a["token"]), (spare[:], a["spare"]),
            (w_qkv[:], a["w_qkv"].rearrange("(k p) n -> p k n", p=P)),
            (w_o[:], a["L0_ffn_Wo"].rearrange("(k p) n -> p k n", p=P)),
            (w_gate[:], a["w_gate"]), (b_gate[:], a["b_gate"]),
            (w_r[:], a["L0_ffn_Wr"].rearrange("(k p) n -> p k n", p=P)),
            (b_qkv[:], a["b_qkv"].to_broadcast([P, QKV])),
            (b_o[:], a["bo"].to_broadcast([P, D])),
            (b_r[:], a["br"].to_broadcast([P, NE])),
            (ln1[:], a["ln1"].to_broadcast([P, D])),
            (ln2[:], a["ln2"].to_broadcast([P, D])),
            (qk_w[:].rearrange("p h d -> p (h d)"), a["qk_w"].to_broadcast([P, NH2 * HD])),
            (rope_c[:], a["rope_c"].rearrange("(j p) d -> p j d", p=P)),
            (rope_s[:], a["rope_s"].rearrange("(j p) d -> p j d", p=P)),
        ]
        for n in range(4):
            small.append((xw[:, n], a["xw"][n].rearrange("(k p) n -> p k n", p=P)))
            small.append((xbias[:, n, :], a["xb"][n:n + 1, :].to_broadcast([P, D])))
        NW = len(small)
        N_CLEARED = 15
        N_OWN = {"body": 182}

        class Own:

            def __init__(self, eng, sem_, base):
                self.eng, self.sem, self.n, self.base = eng, sem_, 0, base

            def link(self, ins):
                ins.then_inc(self.sem, 1)
                self.n += 1
                self.eng.wait_ge(self.sem, self.base + self.n)

        def go_through(eng, do):
            for step in sections["pro"]:
                do("pro", 0, step)
            copy_of_b = eng.alloc_register()
            with eng.Fori(0, B - 1) as b:
                for n, step in enumerate(sections["body"]):
                    if n % 8 == 0:
                        eng.reg_mov(copy_of_b, b)
                        batch = eng.snap(copy_of_b, min_val=0, max_val=B - 2)
                    do("body", batch, step)
            for step in sections["epi"]:
                do("epi", B - 1, step)

        def y0_row(sec, b, k, of=None):
            buf = y0 if of is None else of
            if sec == "pro":
                return buf[:, k]
            return buf[:, bass.ds(parity(b + 1) * ST + k, 1)].rearrange("p a n -> p (a n)")

        def own_row(sec, b, j, of):
            if isinstance(b, int):
                return of[:, (b % 2) * ST + j]
            return of[:, bass.ds(parity(b) * ST + j, 1)].rearrange("p a n -> p (a n)")

        block = ctx.enter_context(nc.Block())

        @block.sync
        def _(sp):
            def load_x(b, j, par):
                sp.dma_start(xb[:, par * ST + j if isinstance(par, int) else bass.ds(par * ST + j, 1)],
                             a["x"][bass.ds(b * S + j * P, P)] if not isinstance(b, int) else a["x"][b * S + j * P:b * S + j * P + P]).then_inc(s_x[j], 16)

            sp.sem_inc(s_st, 32)
            for dst, src in small[:5]:
                sp.dma_start(dst, src).then_inc(s_w, 16)
            sp.dma_start(ctxT[:], a["ctxT"][0].rearrange("(k p) n -> p k n", p=P)).then_inc(s_ctx, 16)
            for dst, src in small[5:]:
                sp.dma_start(dst, src).then_inc(s_w, 16)
            for j in range(ST):
                load_x(0, j, 0)
            sp.wait_ge(ev("ctx_proj"), 1)
            sp.dma_start(ctxT[:], a["ctxT"][1].rearrange("(k p) n -> p k n", p=P)).then_inc(s_ctx, 16)
            for j in range(ST):
                sp.wait_ge(s_x[j], 16)
                load_x(1, j, 1)
            sp.wait_ge(ev("zeros"), 1)
            sp.dma_start(rows_dram[T * P:], zero_rows[:]).then_inc(s_spare, 16)

            def stores(b, more):
                for n, j in enumerate(TILE_ORDER):
                    sp.wait_ge(ev("base"), b * ST + n + 1)
                    alone(sp)
                    t = b * ST + j
                    at = slice(t * P, t * P + P) if isinstance(t, int) else bass.ds(t * P, P)
                    sp.dma_start(rows_dram[at, D:], base[:]).then_inc(s_st, 16)
                    if more:
                        load_x(b + 2, j, parity(b))
                    sp.wait_ge(ev("h2"), b * ST + n + 1)
                    alone(sp)
                    sp.dma_start(rows_dram[at, 0:D], h2[:]).then_inc(s_st, 16)

            with sp.Fori(0, 2) as b:
                sp.wait_ge(ev("ctx_proj"), b + 2)
                sp.dma_start(ctxT[:], a["ctxT"][bass.ds(b + 2, 1)].rearrange("a (k p) n -> p (a k) n", p=P)).then_inc(s_ctx, 16)
                stores(b, True)
            stores(2, False)
            even = lambda e: e % 2 == 0
            for e in filter(even, range(NE)):
                sp.dma_start(W1[:, e], a["L0_ffn_W1"][e].rearrange("(k p) n -> p k n", p=P)).then_inc(s_big, 16)
            stores(3, False)
            for e in range(NE):
                if not even(e):
                    sp.dma_start(W1[:, e], a["L0_ffn_W1"][e].rearrange("(k p) n -> p k n", p=P)).then_inc(s_big, 16)
            for e in range(NE):
                sp.dma_start(W2[:, e], a["L0_ffn_W2"][e].rearrange("(k p) n -> p k n", p=P)).then_inc(s_big, 16)

        @block.gpsimd
        def _(pool):
            pool.sem_inc(ev("yr_free"), 2)
            pool.memset(zero_rows[:], 0.0).then_inc(ev("zeros"), 1)
            n = 0

            def fill(dst, value):
                nonlocal n
                pool.memset(dst, value).then_inc(ev("cleared"), 1)
                n += 1
                pool.wait_ge(ev("cleared"), n)

            for dst in (Vx[:], Vr[:], Va[:], Va_next[:], Kx[0:RS, :, P:P + KR], b1_parts[:], b2_parts[:]):
                fill(dst, 0.0)
            fill(minus_half[:], -0.5)
            for dst in (Vx[:, :, HD:HD + 1], Va_next[:, :, :, HD:HD + 1], ks_tok[:, :, RS:RS + 1],
                        *(Vr[32 * q:32 * q + CR, :, 32 * q + HD:32 * q + HD + 1] for q in range(4))):
                fill(dst, 1.0)
            assert n == N_CLEARED, n

            def root(ready, n, dst, src, eps, done):
                w = dst.shape[1]
                pool.wait_ge(ev(ready), n)
                alone(pool)
                pool.tensor_scalar(safe[done][:, 0:w], src, eps, None, ALU.add).then_inc(ev(f"safe_{done}"), 1)
                pool.wait_ge(ev(f"safe_{done}"), n)
                pool.tensor_tensor(dst, safe[done][:, 0:w], minus_half[:, 0:w], ALU.pow).then_inc(ev(done), 1)

            def do(sec, b, step):
                kind, r, k = step
                X = k if sec == "pro" else ST * (b + 1) + k
                Y = ST * b + k
                if kind == "x" and r == 0:
                    root("mv0", X + 1, rstd[0][:], mv[0][:, 1:2], EPS_LN, "rstd0")
                if kind == "x" and r == 13:
                    root("mv1", X + 1, rstd[1][:], mv[1][:, 1:2], EPS_LN, "rstd1")
                if kind == "x" and r == 14:
                    root("y0_ss", X + 1, rs_row[:], ss[:], EPS_RMS, "y0_rs")
                if kind == "x" and r == 17:
                    root("h_ms", X + 1, h_rs[:], hs[:], EPS_RMS, "h_rs")
                if kind == "tail" and r == 4:
                    root("x2_ss", Y + 1, s_rs[:], s_ss[:], EPS_RMS, "x2_rs")
                if kind == "scores" and PAIRS[r][1] == TILE_ORDER[PAIRS[r][0]]:
                    _, rd, _, after = turns[U].at(sec, b, ("s", r, k))
                    e, _, _, _ = e_turns.at(sec, b, ("s", r, k))
                    pool.wait_ge(rd, after)
                    alone(pool)
                    e3 = E[e][:].rearrange("p (h n) -> p h n", n=P)
                    pool.affine_select(out=e3, in_=e3, compare_op=ALU.is_ge, fill=0.0, base=0,
                                       pattern=[[0, 1024 // P], [1, P]], channel_multiplier=-1).then_inc(ev("masked"), 1)

            go_through(pool, do)
            pool.wait_ge(ev("places"), 1)
            pool.wait_ge(s_st, 32 * (T + 1))
            pool.wait_ge(s_spare, 16)

            def copy_idx(dst, m):
                src = idx[:, m:m + 1] if isinstance(m, int) else idx[:, bass.ds(m, 1)]
                pool.tensor_copy(dst[:], src).then_inc(ev("idx_copy"), 1)

            def gather(m, i, before):
                if not isinstance(m, int) or m >= 2:
                    pool.wait_ge(ev("rowsT"), m - 1)
                    alone(pool)
                copy_idx(idx_in[i], m)
                pool.wait_ge(ev("idx_copy"), before + 1)
                alone(pool)
                pool.indirect_dma_start(out=xr[i], out_offset=None, in_=rows_dram,
                                        in_offset=bass.IndirectOffsetOnAxis(ap=idx_in[i][:], axis=0)).then_inc(s_xr[i], 16)

            def scatter(m, i, n, before):
                pool.wait_ge(ev("y_rows"), m + 1)
                alone(pool)
                copy_idx(idx_out[i], m)
                pool.wait_ge(ev("idx_copy"), before + 1)
                alone(pool)
                pool.indirect_dma_start(out=out, out_offset=bass.IndirectOffsetOnAxis(ap=idx_out[i][:], axis=0),
                                        in_=yr[i], in_offset=None).then_inc(s_yr[i], 16)
                pool.wait_ge(s_yr[i], 16 * n + 16)
                pool.sem_inc(ev("yr_free"), 1)

            for i in range(2):
                gather(i, i, i)
            with pool.Fori(0, MT // 2 - 1) as n:
                for i in range(2):
                    gather(2 * n + 2 + i, i, 4 * n + 2 + 2 * i)
                    scatter(2 * n + i, i, n, 4 * n + 3 + 2 * i)
            gather(MT - 1, 0, 2 * MT - 4)
            for n, m in enumerate(range(MT - 3, MT)):
                scatter(m, m % 2, m // 2, 2 * MT - 3 + n)

        @block.tensor
        def _(pe):
            def take(which, sec, b, name):
                i, rd, before, _ = turns[which].at(sec, b, name)
                wait(pe, rd, before)
                return (ps_u if which == U else ps_m)[i]

            def await_read(which, sec, b, name):
                _, rd, _, after = turns[which].at(sec, b, name)
                pe.wait_ge(rd, after)

            def turn_blocks(dst, src, n):
                for k in range(n):
                    mm = pe.transpose(dst[:, k * P:(k + 1) * P], src[:, k * P:(k + 1) * P], identf[:])
                return mm

            def project(dst, xT_, w):
                for k in range(2):
                    mm = pe.matmul(dst, xT_[:, k * P:(k + 1) * P], w[:, k], start=(k == 0), stop=(k == 1), skip_group_check=True)
                return mm

            def ctx_step(sec, b, r):
                bx = 0 if sec == "pro" else b + 1
                if r == 0:
                    pe.wait_ge(s_ctx, 16 * (bx + 1))
                    kv = take(U, sec, b, ("kv",))
                    for w, o in ((1, 0), (2, 256)):
                        for k in range(2):
                            pe.matmul(kv[:, o:o + D], ctxT[:, k, 0:P], xw[:, w, k], start=(k == 0), stop=(k == 1), skip_group_check=True)
                    for k in range(2):
                        mm = pe.matmul(kv[0:CR, 512:512 + D], ctxT[:, k, P:C], xw[:, 1, k], start=(k == 0), stop=(k == 1))
                    mm.then_inc(ev("kv_ps"), 1)
                    vr = take(U, sec, b, ("vr",))
                    for q in range(4):
                        for k in range(2):
                            mm = pe.matmul(vr[32 * q:32 * q + CR, 0:D], ctxT[:, k, P:C], xw[:, 2, k], start=(k == 0), stop=(k == 1))
                    mm.then_inc(ev("ctx_proj"), 1)
                if r in (2, 4):
                    n = r // 2 - 1
                    rows_ = (P, CR)[n]
                    ub = take(U, sec, b, ("kT", n))[:].bitcast(bf16)
                    pe.wait_ge(ev("k_split"), bx * 2 + n + 1)
                    alone(pe)
                    for h in range(H):
                        mm = pe.transpose(ub[0:RS, h * P:h * P + rows_], k_tok[0:rows_, h, :], identb[0:rows_, 0:rows_])
                    mm.then_inc(ev("k_turned"), 1)

            def x_step(sec, b, r, k):
                X = k if sec == "pro" else ST * (b + 1) + k
                at = (sec, b)
                q = Qx[k % 2]
                if r == 1:
                    dst = take(M, *at, ("xnT", k))
                    pe.wait_ge(ev("xn"), X + 1)
                    turn_blocks(dst, xn, 2).then_inc(ev("xnT_ps"), 1)
                if r == 2:
                    dst = take(M, *at, ("q", k))
                    await_read(M, *at, ("xnT", k))
                    project(dst[:, 0:D], xnT, xw[:, 0]).then_inc(ev("q_ps"), 1)
                if r == 3:
                    ub = take(U, *at, ("qT", k))[:].bitcast(bf16)
                    pe.wait_ge(ev("q_split"), X + 1)
                    for h in range(H):
                        mm = pe.transpose(ub[0:RS, h * P:(h + 1) * P], q_tok[:, h, :], identb[:])
                    mm.then_inc(ev("q_turned"), 1)
                if r in (4, 5, 6):
                    if r == 4:
                        await_read(U, *at, ("kT", 1))
                        await_read(U, *at, ("qT", k))
                    for c in (2 * r - 8, 2 * r - 7):
                        dst = take(M, *at, ("row", k, c))
                        for h in range(3 * c, min(3 * c + 3, H)):
                            mm = pe.matmul(dst[:, (h % 3) * C:(h % 3 + 1) * C], q[0:RS, h], Kx[0:RS, h, 0:C], start=True, stop=True, skip_group_check=True)
                        mm.then_inc(ev("row_ps"), 1)
                if r == 7:
                    dst = take(M, *at, ("shift", k))
                    pe.wait_ge(ev("shift"), X + 1)
                    pe.transpose(dst[:].bitcast(bf16)[RS:P, 0:P], nmx[:].rearrange("p a h -> p (a h)"), identb[:], tile_position=(0, RS)).then_inc(ev("shiftT_ps"), 1)
                if r == 8:
                    pe.wait_ge(ev("shiftT"), X + 1)
                    for n in range(2):
                        dst = take(U, *at, ("key", k, n))
                        for h in range(8 * n, 8 * n + 8):
                            mm = pe.matmul(dst[:, (h % 8) * P:(h % 8 + 1) * P], Kx[:, h, 0:P], q[:, h], start=True, stop=True, skip_group_check=True)
                        mm.then_inc(ev("key_ps"), 1)
                    dst = take(U, *at, ("key", k, 2))
                    for h in range(H):
                        g = h // 4
                        mm = pe.matmul(dst[32 * (h % 4):32 * (h % 4) + 32, g * P:(g + 1) * P], Kx[:, h, P:P + KR], q[:, h],
                                       start=True, stop=True, skip_group_check=True)
                    mm.then_inc(ev("key_ps"), 1)
                if r == 9:
                    dst = take(M, *at, ("oT", k))
                    for n in range(2):
                        await_read(U, *at, ("key", k, n))
                        e, rd, _, _ = e_turns.at(*at, ("key", k, n))
                        for h in range(8 * n, 8 * n + 8):
                            g = h // 4
                            mm = pe.matmul(dst[32 * (h % 4):32 * (h % 4) + 32, g * P:(g + 1) * P], Vx[:, h], E[e][:, (h % 8) * P:(h % 8 + 1) * P],
                                           start=(g == 0), stop=False, skip_group_check=True)
                        mm.then_inc(rd, 1)
                    await_read(U, *at, ("key", k, 2))
                    e, rd, _, _ = e_turns.at(*at, ("key", k, 2))
                    for g in range(4):
                        mm = pe.matmul(dst[:, g * P:(g + 1) * P], Vr[:, g], E[e][:, g * P:(g + 1) * P], start=False, stop=True, skip_group_check=True)
                    mm.then_inc(rd, 1)
                if r == 10:
                    dst = take(M, *at, ("o", k))
                    await_read(M, *at, ("oT", k))
                    turn_blocks(dst, oT, 4).then_inc(ev("o_ps"), 1)
                if r == 11:
                    dst = take(M, *at, ("onT", k))
                    await_read(M, *at, ("o", k))
                    turn_blocks(dst, on, 2).then_inc(ev("onT_ps"), 1)
                if r == 12:
                    dst = take(M, *at, ("xo", k))
                    await_read(M, *at, ("onT", k))
                    project(dst[:, 0:D], onT, xw[:, 3]).then_inc(ev("xo_ps"), 1)
                if r == 15:
                    dst = take(M, *at, ("hT", k))
                    pe.wait_ge(ev("hh"), X + 1)
                    turn_blocks(dst, hh, 2).then_inc(ev("hT_ps"), 1)
                if r == 16:
                    dst = take(M, *at, ("qkv", k))
                    await_read(M, *at, ("hT", k))
                    project(dst[:, 0:QKV], hT, w_qkv[:]).then_inc(ev("qkv_ps"), 1)
                if r == 18:
                    dst = take(M, *at, ("ksT", k))[:].bitcast(bf16)
                    pe.wait_ge(ev("ks_split"), X + 1)
                    for g in range(KV):
                        mm = pe.transpose(dst[0:RS + 1, g * P:(g + 1) * P], ks_tok[:, g, :], identb[:])
                    mm.then_inc(ev("ks_ps"), 1)

            def second_step(sec, b, kind, r, k):
                at = (sec, b)
                if kind == "prep" and r == 1:
                    ub = take(U, *at, ("qs", k))[:].bitcast(bf16)
                    pe.wait_ge(ev("qs_split"), ST * b + k + 1)
                    for h in range(H):
                        mm = pe.transpose(ub[0:RS + 1, h * P:(h + 1) * P], qs_tok[:, h, :], identb[:])
                    mm.then_inc(ev("qs_ps"), 1)
                if kind == "scores":
                    n, i = PAIRS[r]
                    if r == 0 and k == 0:
                        pe.wait_ge(ev("ks_stack"), ST * (b + 1))
                    if r == FIRST[n] and k == 0:
                        await_read(U, *at, ("qs", n))
                    dst = take(U, *at, ("s", r, k))
                    for g in (2 * k, 2 * k + 1):
                        keys = Kst[0:RS + 1, b % 2, g, i * P:(i + 1) * P] if isinstance(b, int) else \
                            Kst[0:RS + 1, bass.ds(parity(b), 1), g, i * P:(i + 1) * P].rearrange("p a n -> p (a n)")
                        mm = pe.matmul(dst[:, (g % 2) * 512:(g % 2) * 512 + 512], keys,
                                       Qs[n % 2][0:RS + 1, HQ * g:HQ * g + HQ].rearrange("p h n -> p (h n)"), start=True, stop=True)
                    mm.then_inc(ev("s_ps"), 1)
                if kind == "values":
                    n, i = PAIRS[r]
                    j = TILE_ORDER[n]
                    if r == FIRST[n] and k == 0:
                        pe.wait_ge(ev("so_T"), ST * b + n + 1)
                        if n == 0:
                            pe.wait_ge(ev("va"), b + 1)
                    if i == j:
                        pe.wait_ge(ev("masked"), (ST * b + n) * 2 + k + 1)
                    else:
                        await_read(U, *at, ("s", r, k))
                    e, rd, _, _ = e_turns.at(*at, ("s", r, k))
                    for g in (2 * k, 2 * k + 1):
                        mm = pe.matmul(ps_o[32 * g:32 * g + 32, :], Va[:, i, g], E[e][:, (g % 2) * 512:(g % 2) * 512 + 512],
                                       start=(r == FIRST[n]), stop=(r == last_pair(n)), skip_group_check=True)
                    mm.then_inc(rd, 1)
                if kind == "tail":
                    Y = ST * b + k
                    if r == 0:
                        dst = take(M, *at, ("so", k))
                        pe.wait_ge(ev("so_T"), Y + 2)
                        turn_blocks(dst, soT[k % 2], 4).then_inc(ev("so_ps"), 1)
                    if r == 1:
                        dst = take(M, *at, ("soT", k))
                        await_read(M, *at, ("so", k))
                        turn_blocks(dst, s_on, 2).then_inc(ev("soT_ps"), 1)
                    if r == 2:
                        dst = take(M, *at, ("gate", k))
                        await_read(M, *at, ("soT", k))
                        pe.matmul(dst[:, 0:2 * P], w_gate[:], s_onT[:], start=True, stop=True).then_inc(ev("gate_ps"), 1)
                    if r == 3:
                        dst = take(M, *at, ("wo", k))
                        pe.wait_ge(ev("gated"), Y + 1)
                        project(dst[:, 0:D], gt, w_o[:]).then_inc(ev("wo_ps"), 1)
                    if r == 5:
                        dst = take(M, *at, ("h2T", k))
                        pe.wait_ge(ev("h2"), Y + 1)
                        turn_blocks(dst, h2, 2).then_inc(ev("h2T_ps"), 1)
                    if r == 6:
                        dst = take(M, *at, ("logit", k))
                        await_read(M, *at, ("h2T", k))
                        project(dst[:, 0:NE], h2T, w_r[:]).then_inc(ev("logit_ps"), 1)

            def do(sec, b, step):
                kind, r, k = step
                if kind == "ctx":
                    ctx_step(sec, b, r)
                elif kind == "x":
                    x_step(sec, b, r, k)
                else:
                    second_step(sec, b, kind, r, k)

            pe.sem_inc(ev("so_T"), 1)
            pe.wait_ge(s_w, NW * 16)
            go_through(pe, do)

            pe.wait_ge(ev("onehot"), 1)
            oh = onehot[:].rearrange("p t e -> p (t e)")
            pe.matmul(ps_u[0][:, 0:T * NE], upper[:], oh, start=True, stop=True)
            pe.matmul(ps_u[0][:, 512:512 + T * NE], ones[:], oh, start=True, stop=True).then_inc(ev("ranks"), 1)
            for g in range(4):
                pe.wait_ge(ev("hot"), g + 1)
                for t in range(G):
                    mm = pe.matmul(ps_o[:, 0:2 * MT], row_hot[g][:, t], tile_hot[g][:, t].rearrange("p a n -> p (a n)"),
                                   start=(g == 0 and t == 0), stop=(g == 3 and t == G - 1))
            mm.then_inc(ev("ids_ps"), 1)
            pe.wait_ge(ev("places"), 1)
            pe.wait_ge(s_big, 2 * NE * 16)

            def turn_rows(m, i, n):
                pe.wait_ge(s_xr[i], 16 * n + 16)
                turn_blocks(ps_m[0], xr[i], 2).then_inc(ev("rowsT_ps"), 1)

            def up(m, i, e):
                pe.wait_ge(ev("rowsT"), m + 1)
                for half in (1, 0):
                    dst = ps_u[i][:, half * HID:(half + 1) * HID]
                    for k in range(2):
                        w = W1[:, bass.ds(e, 1), k, half * HID:(half + 1) * HID].rearrange("p a n -> p (a n)")
                        pe.matmul(dst, xT[i][:, k * P:(k + 1) * P], w, start=(k == 0), stop=False)
                    mm = pe.matmul(dst, pick[:, bass.ds(e, 1), :].rearrange("p a n -> p (a n)"), b1_parts[:, half * HID:(half + 1) * HID], start=False, stop=True)
                    mm.then_inc(ev("up_ps"), 1)

            def turn_act(m, i):
                pe.wait_ge(ev("act"), m + 1)
                turn_blocks(ps_m[1], act_u, 4).then_inc(ev("actT_ps"), 1)

            def down(m, e):
                pe.wait_ge(ev("actT"), m + 1)
                for k in range(4):
                    w = W2[:, bass.ds(e, 1), k].rearrange("p a n -> p (a n)")
                    pe.matmul(ps_m[2][:, 0:D], actT[:, k * P:(k + 1) * P], w, start=(k == 0), stop=False)
                pe.matmul(ps_m[2][:, 0:D], pick[:, bass.ds(e, 1), :].rearrange("p a n -> p (a n)"), b2_parts[:], start=False, stop=True).then_inc(ev("y_ps"), 1)

            def load_expert(m):
                alone(pe)
                return pe.value_load(expert[0:1, bass.ds(m, 1)] if not isinstance(m, int) else expert[0:1, m:m + 1], min_val=0, max_val=NE - 1)

            e0 = load_expert(0)
            turn_rows(0, 0, 0)
            up(0, 0, e0)
            with pe.Fori(0, MT // 2) as n:
                for i in (1, 0):
                    m = 2 * n + (1 if i else 2)
                    turn_rows(m, i, n if i else n + 1)
                    turn_act(m - 1, 1 - i)
                    up(m, i, load_expert(m))
                    down(m - 1, load_expert(m - 1))
            turn_act(MT - 1, 0)
            down(MT - 1, load_expert(MT - 1))

        @block.scalar
        def _(act):
            def copy(dst, src):
                return act.activation(dst, src, ACT.Copy)

            def read(sec, b, name, ready, n, dst, width):
                i, rd, _, _ = turns[M].at(sec, b, name)
                act.wait_ge(ev(ready), n)
                copy(dst[:, 0:width], ps_m[i][:, 0:width]).then_inc(rd, 1)

            def exponentials_of(sec, b, name, ready, n, width):
                i, rd, _, _ = turns[U].at(sec, b, name)
                e, used, before, _ = e_turns.at(sec, b, name)
                act.wait_ge(ev(ready), n)
                wait(act, used, before)
                act.activation(E[e][:, 0:width], ps_u[i][:, 0:width], ACT.Exp).then_inc(rd, 1)

            def do(sec, b, step):
                kind, r, k = step
                at = (sec, b)
                X = k if sec == "pro" else ST * (b + 1) + k
                Y = ST * b + k
                if kind == "scores":
                    exponentials_of(*at, ("s", r, k), "s_ps", b * 2 * len(PAIRS) + 2 * r + k + 1, 1024)
                if kind == "q_stack":
                    i, rd, _, _ = turns[U].at(*at, ("qT", k))
                    act.wait_ge(ev("q_turned"), X + 1)
                    copy(Qx[k % 2][0:RS].rearrange("p h n -> p (h n)"), ps_u[i][:].bitcast(bf16)[0:RS, :]).then_inc(rd, 1)
                if kind == "flush":
                    _, used, _, after = e_turns.at(*at, ("s", last_pair(k), 1))
                    act.wait_ge(used, after)
                    copy(soT[k % 2][:], ps_o[:]).then_inc(ev("so_T"), 1)
                if kind == "x":
                    if r == 1:
                        read(*at, ("xnT", k), "xnT_ps", X + 1, xnT, 2 * P)
                    if r == 8:
                        for n in range(3):
                            exponentials_of(*at, ("key", k, n), "key_ps", 3 * X + n + 1, 1024 if n < 2 else 512)
                    if r == 9:
                        _, used, _, after = e_turns.at(*at, ("key", k, 2))
                        i, rd, _, _ = turns[M].at(*at, ("oT", k))
                        act.wait_ge(used, after)
                        copy(oT[:], ps_m[i][:]).then_inc(rd, 1)
                    if r == 11:
                        read(*at, ("onT", k), "onT_ps", X + 1, onT, 2 * P)
                    if r == 14:
                        act.wait_ge(ev("y0"), X + 1)
                        act.activation(sqa[:], y0_row(sec, b, k), ACT.Square, scale=D ** -0.5, accum_out=ss[:]).then_inc(ev("y0_ss"), 1)
                    if r == 15:
                        read(*at, ("hT", k), "hT_ps", X + 1, hT, 2 * P)
                if kind == "tail":
                    if r == 1:
                        read(*at, ("soT", k), "soT_ps", Y + 1, s_onT, 2 * P)
                    if r == 2:
                        i, rd, _, _ = turns[M].at(*at, ("gate", k))
                        act.wait_ge(ev("gate_ps"), Y + 1)
                        act.activation(gt[:], ps_m[i][:, 0:2 * P], ACT.Exp, bias=nb_gate[:], scale=-1.0).then_inc(rd, 1)
                    if r == 4:
                        act.wait_ge(ev("x2"), Y + 1)
                        act.activation(s_sqa[:], x2[:], ACT.Square, scale=D ** -0.5, accum_out=s_ss[:]).then_inc(ev("x2_ss"), 1)
                    if r == 5:
                        read(*at, ("h2T", k), "h2T_ps", Y + 1, h2T, 2 * P)

            go_through(act, do)
            def gates(m, i):
                act.wait_ge(ev("up_ps"), 2 * m + 1)
                act.activation(sig, ps_u[i][:, HID:2 * HID], ACT.Sigmoid).then_inc(ev("sig"), 1)

            gates(0, 0)
            with act.Fori(0, MT // 2) as n:
                gates(2 * n + 1, 1)
                gates(2 * n + 2, 0)

        @block.vector
        def _(dve):
            tt, ts, stt = dve.tensor_tensor, dve.tensor_scalar, dve.scalar_tensor_tensor
            heads = lambda ap: ap.rearrange("p (h d) -> p h d", d=HD)

            def parts(own, tok, rows_, n_heads, src, left, scale, hi, mid, lo, done):
                v = tok[0:rows_, :, 0:RS].rearrange("p h (s d) -> p h s d", d=HD)
                s4 = src.rearrange("p (h s d) -> p h s d", s=1, d=HD)
                for sl in hi:
                    n = len(range(*sl.indices(PARTS)))
                    i = ts(v[:, :, sl], s4.to_broadcast([rows_, n_heads, n, HD]), scale, None, ALU.mult)
                own.link(i)
                r4 = left[0:rows_, 0:n_heads * HD].rearrange("p (h s d) -> p h s d", s=1, d=HD)
                r3 = heads(left[0:rows_, 0:n_heads * HD])
                at = lambda sl: v[:, :, range(*sl.indices(PARTS))[0]]
                own.link(stt(r3, heads(src), scale, at(hi[0]), ALU.mult, ALU.subtract))
                for sl in mid:
                    n = len(range(*sl.indices(PARTS)))
                    own.link(dve.tensor_copy(v[:, :, sl], r4.to_broadcast([rows_, n_heads, n, HD])))
                tt(at(lo[0]), r3, at(mid[0]), ALU.subtract).then_inc(ev(done), 1)

            QP = dict(hi=(slice(0, 3),), mid=(slice(3, 5),), lo=(slice(5, 6),))
            KP = dict(hi=(slice(0, 4, 3), slice(5, 6)), mid=(slice(1, 5, 3),), lo=(slice(2, 3),))

            def read_own(rd, after, ins):
                ins.then_inc(rd, 1)
                dve.wait_ge(rd, after)

            def statistics(own, n, src):
                alone(dve)
                own.link(dve.bn_stats(stats[n][:], src))
                alone(dve)
                dve.bn_aggr(mv[n][:], stats[n][:]).then_inc(ev(f"mv{n}"), 1)

            def ctx_step(own, sec, b, r):
                bx = 0 if sec == "pro" else b + 1
                bias = lambda n, rows_: xbias[rows_, n]
                if r == 1:
                    i, rd, _, after = turns[U].at(sec, b, ("kv",))
                    dve.wait_ge(ev("kv_ps"), bx + 1)
                    tt(Vx[:, :, 0:HD], heads(ps_u[i][:, 256:512]), heads(xbias[:, 2]), ALU.add)
                    tt(kf[:], ps_u[i][:, 0:D], xbias[:, 1], ALU.add)
                    read_own(rd, after, tt(kl[0:CR], ps_u[i][0:CR, 512:512 + D], xbias[0:CR, 1], ALU.add))
                    i, rd, _, after = turns[U].at(sec, b, ("vr",))
                    dve.wait_ge(ev("ctx_proj"), bx + 1)
                    for q in range(4):
                        s_ = slice(32 * q, 32 * q + CR)
                        ins = tt(Vr[s_, :, 32 * q:32 * q + HD], heads(ps_u[i][s_, 0:D])[:, q:H:4], heads(xbias[s_, 2])[:, q:H:4], ALU.add)
                    ins.then_inc(rd, 1)
                    parts(own, k_tok, P, H, kf[:], k_rest, 1.0, done="k_split", **KP)
                if r in (3, 5):
                    n = r // 2 - 1
                    rows_, at = ((P, 0), (CR, P))[n]
                    i, rd, _, after = turns[U].at(sec, b, ("kT", n))
                    dve.wait_ge(ev("k_turned"), bx * 2 + n + 1)
                    ub = ps_u[i][:].bitcast(bf16).rearrange("p (h n) -> p h n", n=P)
                    dve.tensor_copy(Kx[0:RS, :, at:at + rows_], ub[0:RS, :, 0:rows_]).then_inc(rd, 1)
                    if n == 0:
                        parts(own, k_tok, CR, H, kl[0:CR], k_rest, 1.0, done="k_split", **KP)

            def x_step(own, sec, b, r, k):
                at = (sec, b)
                X = k if sec == "pro" else ST * (b + 1) + k
                if r == 0:
                    dve.wait_ge(s_x[k], 16 if sec == "pro" else 16 * b + 32)
                    statistics(own, 0, y0_row(sec, b, k, xb))
                if r == 1:
                    dve.wait_ge(ev("rstd0"), X + 1)
                    ts(xn[:], y0_row(sec, b, k, xb), mv[0][:, 0:1], rstd[0][:], ALU.subtract, ALU.mult).then_inc(ev("xn"), 1)
                if r == 3:
                    i, rd, _, after = turns[M].at(*at, ("q", k))
                    dve.wait_ge(ev("q_ps"), X + 1)
                    read_own(rd, after, tt(qf[:], ps_m[i][:, 0:D], xbias[:, 0], ALU.add))
                    parts(own, q_tok, P, H, qf[:], rest, SCALE, done="q_split", **QP)
                if r in (5, 6, 7):
                    for c in (2 * r - 10, 2 * r - 9):
                        n = 3 if c < 5 else 1
                        i, rd, _, after = turns[M].at(*at, ("row", k, c))
                        dve.wait_ge(ev("row_ps"), X * 6 + c + 1)
                        src = ps_m[i][:, 0:n * C].rearrange("p (h n) -> p h n", n=C)
                        dve.tensor_reduce(out=mx[:, 3 * c:3 * c + n], in_=src, axis=AX.X, op=ALU.max).then_inc(rd, 1)
                    if r == 7:
                        dve.wait_ge(rd, after)
                        own.link(ts(nmx[:, 0], mx[:], -1.0, None, ALU.mult))
                        stt(nmx[:, 1], mx[:], -1.0, nmx[:, 0], ALU.mult, ALU.subtract).then_inc(ev("shift"), 1)
                if r == 8:
                    i, rd, _, after = turns[M].at(*at, ("shift", k))
                    dve.wait_ge(ev("shiftT_ps"), X + 1)
                    read_own(rd, after, dve.tensor_copy(nmT[RS:P, 0, :], ps_m[i][:].bitcast(bf16)[RS:P, 0:P]))
                    dve.tensor_copy(Qx[k % 2][RS:P], nmT[RS:P].to_broadcast([P - RS, H, P])).then_inc(ev("shiftT"), 1)
                if r == 11:
                    i, rd, _, after = turns[M].at(*at, ("o", k))
                    dve.wait_ge(ev("o_ps"), X + 1)
                    o4 = ps_m[i][:].rearrange("p (h n) -> p h n", n=32)
                    own.link(dve.reciprocal(rsum[:], o4[:, :, HD]))
                    tt(heads(on[:]), o4[:, :, 0:HD], rsum[:].rearrange("p (h d) -> p h d", d=1).to_broadcast([P, H, HD]), ALU.mult).then_inc(rd, 1)
                if r == 13:
                    i, rd, _, after = turns[M].at(*at, ("xo", k))
                    dve.wait_ge(ev("xo_ps"), X + 1)
                    row = y0_row(sec, b, k, xb)
                    read_own(rd, after, tt(row, row, ps_m[i][:, 0:D], ALU.add))
                    own.link(tt(row, row, xbias[:, 3], ALU.add))
                    statistics(own, 1, row)
                if r == 14:
                    dve.wait_ge(ev("rstd1"), X + 1)
                    ts(y0_row(sec, b, k), y0_row(sec, b, k, xb), mv[1][:, 0:1], rstd[1][:], ALU.subtract, ALU.mult).then_inc(ev("y0"), 1)
                if r == 15:
                    dve.wait_ge(ev("y0_rs"), X + 1)
                    stt(hh[:], y0_row(sec, b, k), rs_row[:], ln1[:], ALU.mult, ALU.mult).then_inc(ev("hh"), 1)
                n = NH2 * HD
                if r == 17:
                    i, rd, _, after = turns[M].at(*at, ("qkv", k))
                    dve.wait_ge(ev("qkv_ps"), X + 1)
                    read_own(rd, after, tt(qkv[:], ps_m[i][:, 0:QKV], b_qkv[:], ALU.add))
                    dve.tensor_copy(Va_next[:, k, :, 0:HD], heads(qkv[:, n:]))
                    own.link(stt(sq[:], qkv[:, 0:n], 1.0 / HD, qkv[:, 0:n], ALU.mult, ALU.mult))
                    dve.tensor_reduce(out=hs[:], in_=heads(sq[:]), axis=AX.X, op=ALU.add).then_inc(ev("h_ms"), 1)
                    tt(heads(ra[:]), heads(qkv[:, 0:n]), rope_c[:, k:k + 1].to_broadcast([P, NH2, HD]), ALU.mult)
                    for half in range(2):
                        o, f = half * (HD // 2), (1 - half) * (HD // 2)
                        sn = rope_s[:, k:k + 1, o:o + HD // 2].to_broadcast([P, NH2, HD // 2])
                        ins = tt(heads(rb[:])[:, :, o:o + HD // 2], heads(qkv[:, 0:n])[:, :, f:f + HD // 2], sn, ALU.mult)
                    own.link(ins)
                    own.link(tt(ra[:], ra[:], rb[:], ALU.add))
                if r == 18:
                    w = qk_w[:].rearrange("p h d -> p (h d)")
                    dve.wait_ge(ev("h_rs"), X + 1)
                    own.link(tt(heads(ra[:]), heads(ra[:]), h_rs[:].rearrange("p (h d) -> p h d", d=1).to_broadcast([P, NH2, HD]), ALU.mult))
                    own.link(tt(ra[:, D:n], ra[:, D:n], w[:, D:n], ALU.mult))
                    parts(own, ks_tok, P, KV, ra[:, D:n], ks_rest, 1.0, done="ks_split", **KP)
                    tt(y0_row(sec, b, k, q_hat), ra[:, 0:D], w[:, 0:D], ALU.mult).then_inc(ev("q_hat"), 1)
                if r == 19:
                    i, rd, _, after = turns[M].at(*at, ("ksT", k))
                    dve.wait_ge(ev("ks_ps"), X + 1)
                    dst = Kst[0:RS + 1, 0, :, k * P:(k + 1) * P] if sec == "pro" else \
                        Kst[0:RS + 1, bass.ds(parity(b + 1), 1), :, k * P:(k + 1) * P].rearrange("p a g n -> p (a g) n")
                    read_own(rd, after, dve.tensor_copy(dst, ps_m[i][:].bitcast(bf16)[0:RS + 1, 0:KV * P].rearrange("p (g n) -> p g n", n=P)))
                    dve.sem_inc(ev("ks_stack"), 1)

            def second_step(own, sec, b, kind, r, k):
                at = (sec, b)
                Y = ST * b + k
                j = TILE_ORDER[k] if kind in ("prep", "tail") else 0
                if kind == "swap":
                    dve.wait_ge(ev("q_hat"), ST * (b + 1))
                    dve.tensor_copy(Va[:], Va_next[:]).then_inc(ev("va"), 1)
                if kind == "prep" and r == 0:
                    parts(own, qs_tok, P, H, own_row(sec, b, j, q_hat), qs_rest, SCALE, done="qs_split", **QP)
                if kind == "prep" and r == 2:
                    i, rd, _, after = turns[U].at(*at, ("qs", k))
                    if k >= 2:
                        _, rd2, _, after2 = turns[U].at(*at, ("s", last_pair(k - 2), 1))
                        dve.wait_ge(rd2, after2)
                    dve.wait_ge(ev("qs_ps"), Y + 1)
                    dve.tensor_copy(Qs[k % 2][0:RS + 1].rearrange("p h n -> p (h n)"), ps_u[i][:].bitcast(bf16)[0:RS + 1, :]).then_inc(rd, 1)
                if kind == "tail":
                    if r == 1:
                        i, rd, _, after = turns[M].at(*at, ("so", k))
                        dve.wait_ge(ev("so_ps"), Y + 1)
                        o4 = ps_m[i][:].rearrange("p (h n) -> p h n", n=32)
                        own.link(dve.reciprocal(s_rsum[:], o4[:, :, HD]))
                        dst4 = s_on[:].rearrange("p (g q d) -> p g q d", g=KV, d=HD)
                        for q in range(HQ):
                            f = s_rsum[:, KV * q:KV * q + KV].rearrange("p (g d) -> p g d", d=1).to_broadcast([P, KV, HD])
                            ins = tt(dst4[:, :, q], o4[:, KV * q:KV * q + KV, 0:HD], f, ALU.mult)
                        ins.then_inc(rd, 1)
                    if r == 3:
                        _, rd, _, after = turns[M].at(*at, ("gate", k))
                        dve.wait_ge(rd, after)
                        own.link(ts(gt[:], gt[:], 1.0, None, ALU.add))
                        own.link(dve.reciprocal(gt[:], gt[:]))
                        tt(gt[:], gt[:], s_onT[:], ALU.mult).then_inc(ev("gated"), 1)
                    if r == 4:
                        i, rd, _, after = turns[M].at(*at, ("wo", k))
                        dve.wait_ge(ev("wo_ps"), Y + 1)
                        read_own(rd, after, tt(x2[:], own_row(sec, b, j, y0), ps_m[i][:, 0:D], ALU.add))
                        tt(x2[:], x2[:], b_o[:], ALU.add).then_inc(ev("x2"), 1)
                        dve.wait_ge(ev("x2"), Y + 1)
                        dve.wait_ge(s_st, 32 * Y + 32)
                        tt(base[:], x2[:], own_row(sec, b, j, xb), ALU.add).then_inc(ev("base"), 1)
                    if r == 5:
                        dve.wait_ge(ev("x2_rs"), Y + 1)
                        stt(h2[:], x2[:], s_rs[:], ln2[:], ALU.mult, ALU.mult).then_inc(ev("h2"), 1)
                    if r == 7:
                        i, rd, _, after = turns[M].at(*at, ("logit", k))
                        dve.wait_ge(ev("logit_ps"), Y + 1)
                        t = ST * b + j
                        dst = logits[:, t] if isinstance(t, int) else logits[:, bass.ds(t, 1), :].rearrange("p a e -> p (a e)")
                        tt(dst, ps_m[i][:, 0:NE], b_r[:], ALU.add).then_inc(rd, 1)

            def do(sec, b, step):
                kind, r, k = step
                own = owns_[sec]
                if own is None:
                    own = owns_[sec] = Own(dve, ev(f"d_{sec}"), b * N_OWN[sec] if sec == "body" else 0)
                if kind == "ctx":
                    ctx_step(own, sec, b, r)
                elif kind == "x":
                    x_step(own, sec, b, r, k)
                else:
                    second_step(own, sec, b, kind, r, k)

            owns_ = dict.fromkeys(("pro", "body", "epi"))
            dve.wait_ge(s_w, NW * 16)
            dve.wait_ge(ev("cleared"), N_CLEARED)
            own = Own(dve, ev("d_first"), 0)
            dve.tensor_copy(identb[:], identf[:])
            dve.tensor_copy(pick[:].rearrange("p e n -> p (e n)"), pick_f)
            own.link(dve.tensor_copy(Kx[RS:P].rearrange("p h n -> p (h n)"), which_f))
            own.link(ts(nb_gate[:], b_gate[:], -1.0, None, ALU.mult))
            own.link(tt(ra[:, 0:HD], qk_w[:, 0], qk_w[:, H], ALU.mult))
            own.link(dve.tensor_reduce(out=bshift[:], in_=ra[:, 0:HD], axis=AX.X, op=ALU.max, apply_absolute_value=True))
            own.link(ts(bshift[:], bshift[:], -SCALE * HD, None, ALU.mult))
            own.link(dve.tensor_copy(qs_tok[:, :, RS:RS + 1], bshift[:].rearrange("p (a b) -> p a b", a=1).to_broadcast([P, H, 1])))
            for src, dst, n in ((E[0], b1_parts, 2 * HID), (E[1], b2_parts, D)):
                tb = E[2][:].bitcast(bf16)
                for r in (0, 32, 64):
                    g = slice(r, r + NE)
                    for left_over in range(r // 32):
                        own.link(dve.tensor_copy(tb[g, 0:n], src[g, 0:n]))
                        own.link(tt(src[g, 0:n], src[g, 0:n], tb[g, 0:n], ALU.subtract))
                    own.link(dve.tensor_copy(dst[g, 0:n], src[g, 0:n]))
            go_through(dve, do)
            assert owns_["body"].n == N_OWN["body"], owns_["body"].n

            own = Own(dve, ev("d_route"), 0)
            te = lambda ap: ap.rearrange("p (t e) -> p t e", e=1).to_broadcast([P, T, NE])
            _, rd, _, after = turns[M].at("epi", B - 1, ("logit", ST - 1))
            dve.wait_ge(rd, after)
            own.link(dve.tensor_reduce(out=best[:], in_=logits[:], axis=AX.X, op=ALU.max))
            own.link(tt(first_e[:], logits[:], te(best[:]), ALU.is_ge))
            own.link(tt(first_e[:], first_e[:], count_e[:].rearrange("p (a e) -> p a e", a=1).to_broadcast([P, T, NE]), ALU.mult))
            own.link(dve.tensor_reduce(out=best[:], in_=first_e[:], axis=AX.X, op=ALU.max))
            tt(onehot[:], first_e[:], te(best[:]), ALU.is_equal).then_inc(ev("onehot"), 1)
            dve.wait_ge(ev("ranks"), 1)
            own.link(dve.tensor_copy(total[:], ps_u[0][:, 512:512 + T * NE].rearrange("p (t e) -> p e t", e=NE)))
            for e in range(NE):
                i = dve.tensor_tensor_scan(cum[:, e], ones[:, 0:T], total[:, e], 0.0, ALU.mult, ALU.add)
            own.link(i)
            own.link(ts(padded[:], cum[:, :, T - 1], float(P - 1), None, ALU.add))
            own.link(dve.tensor_copy(whole[:], padded[:]))
            own.link(ts(whole[:], whole[:], ((1 << 24) - 1) // P * P, None, ALU.bitwise_and))
            own.link(dve.tensor_copy(padded[:], whole[:]))
            own.link(dve.tensor_tensor_scan(offset[:], ones[:, 0:NE], padded[:], 0.0, ALU.mult, ALU.add))
            own.link(tt(offset[:], offset[:], padded[:], ALU.subtract))
            own.link(tt(cum[:], cum[:], total[:], ALU.subtract))
            own.link(tt(cum[:], cum[:], offset[:].rearrange("p (e t) -> p e t", t=1).to_broadcast([P, NE, T]), ALU.add))
            own.link(tt(first_e[:], ps_u[0][:, 0:T * NE].rearrange("p (t e) -> p t e", e=NE), cum[:].rearrange("p e t -> p t e"), ALU.add))
            own.link(tt(first_e[:], first_e[:], onehot[:], ALU.mult))
            own.link(dve.tensor_reduce(out=placef[:], in_=first_e[:], axis=AX.X, op=ALU.add))
            own.link(dve.tensor_copy(place[:], placef[:]))
            ts(split_i[:, 0], place[:], P - 1, None, ALU.bitwise_and)
            own.link(ts(split_i[:, 1], place[:], P.bit_length() - 1, None, ALU.arith_shift_right))
            dve.tensor_copy(place_row[:], split_i[:, 0])
            own.link(dve.tensor_copy(place_tile[:], split_i[:, 1]))
            for g in range(4):
                of = lambda ap, n: ap[:, g * G:(g + 1) * G].rearrange("p (t n) -> p t n", n=1).to_broadcast([P, G, n])
                along = lambda ap, n: ap[:].rearrange("p (t n) -> p t n", t=1).to_broadcast([P, G, n])
                tt(row_hot[g], along(row_no, P), of(place_row, P), ALU.is_equal)
                own.link(tt(tile_hot[g][:, :, 0], along(tile_no, MT), of(place_tile, MT), ALU.is_equal))
                tt(tile_hot[g][:, :, 1], tile_hot[g][:, :, 0], of(token, MT), ALU.mult).then_inc(ev("hot"), 1)
            own.link(tt(owns[:], tile_row[:].rearrange("p (m e) -> p m e", e=1).to_broadcast([P, MT, NE]),
                        offset[:].rearrange("p (m e) -> p m e", m=1).to_broadcast([P, MT, NE]), ALU.is_ge))
            own.link(dve.tensor_reduce(out=expertf[:], in_=owns[:], axis=AX.X, op=ALU.add))
            own.link(ts(expertf[:], expertf[:], -1.0, None, ALU.add))
            dve.tensor_copy(expert[:], expertf[:])
            dve.wait_ge(ev("ids_ps"), 1)
            own.link(ts(taken_by[:], ps_o[:, 0:MT], -1.0, 1.0, ALU.mult, ALU.add))
            own.link(stt(ids[:], taken_by[:], spare[:], ps_o[:, MT:2 * MT], ALU.mult, ALU.add))
            dve.tensor_copy(idx[:], ids[:]).then_inc(ev("places"), 1)

            def take_rows(m, i):
                dve.wait_ge(ev("rowsT_ps"), m + 1)
                dve.tensor_copy(bs[i], xr[i][:, D:])
                dve.tensor_copy(xT[i], ps_m[0][:, 0:2 * P]).then_inc(ev("rowsT"), 1)

            def gate_rows(m, i):
                dve.wait_ge(ev("up_ps"), 2 * m + 2)
                dve.wait_ge(ev("sig"), m + 1)
                tt(act_u, ps_u[i][:, 0:HID], sig, ALU.mult).then_inc(ev("act"), 1)

            def take_act(m):
                dve.wait_ge(ev("actT_ps"), m + 1)
                dve.tensor_copy(actT, ps_m[1][:]).then_inc(ev("actT"), 1)

            def take_result(m, i):
                dve.wait_ge(ev("y_ps"), m + 1)
                dve.wait_ge(ev("yr_free"), m + 1)
                tt(yr[i], ps_m[2][:, 0:D], bs[i], ALU.add).then_inc(ev("y_rows"), 1)
                dve.wait_ge(ev("y_rows"), m + 1)

            take_rows(0, 0)
            gate_rows(0, 0)
            with dve.Fori(0, MT // 2) as n:
                for i in (1, 0):
                    m = 2 * n + (1 if i else 2)
                    take_rows(m, i)
                    take_act(m - 1)
                    gate_rows(m, i)
                    take_result(m - 1, 1 - i)
            take_act(MT - 1)
            take_result(MT - 1, 0)


def rope_tables():
    inv = (np.float32(1.0) / np.float32(10000.0) ** (np.arange(0, HD, 2, dtype=np.float32) / np.float32(HD))).astype(np.float32)
    f = (np.arange(S, dtype=np.float32)[:, None] * inv[None, :]).astype(np.float32)
    c, s = np.cos(f.astype(np.float64)).astype(np.float32), np.sin(f.astype(np.float64)).astype(np.float32)
    return np.concatenate([c, c], 1), np.concatenate([-s, s], 1)


def layout(inputs):
    g = {k: np.asarray(v) for k, v in inputs.items()}
    f, x = "L0_ffn_", "L0_xattn_"
    r = {"x": g["x"].reshape(B * S, D), "ctxT": np.ascontiguousarray(g["ctx_1024"].transpose(0, 2, 1))}
    r["xw"] = np.stack([g[x + n].T for n in ("Wq", "Wk", "Wv", "Wo")])
    r["xb"] = np.stack([g[x + n] for n in ("bq", "bk", "bv", "bo")])
    r["w_qkv"] = np.concatenate([g[f + "Wq"], g[f + "Wk"], g[f + "Wv"]], 1)
    r["b_qkv"] = np.concatenate([g[f + "bq"], g[f + "bk"], g[f + "bv"]])[None]
    r["qk_w"] = np.concatenate([np.tile(g[f + "qn_w"], H), np.tile(g[f + "kn_w"], KV)])[None]
    for n, k in (("bo", "bo"), ("br", "br"), ("ln1", "ln1_w"), ("ln2", "ln2_w")):
        r[n] = g[f + k][None]
    for n in ("Wo", "Wr", "W1", "W2"):
        r[f + n] = g[f + n]
    w = np.zeros((P, P), g[f + "Wg"].dtype)
    for i in range(P // HD):
        w[i * HD:(i + 1) * HD, i * HD:(i + 1) * HD] = g[f + "Wg"]
    r["w_gate"] = w
    r["b_gate"] = np.tile(g[f + "bg"], P // HD)[:, None]
    for n, k in (("b1_rows", "b1"), ("b2_rows", "b2")):
        v = np.zeros((P, g[f + k].shape[1]), g[f + k].dtype)
        for s in range(3):
            v[32 * s:32 * s + NE] = g[f + k]
        r[n] = v
    r["identf"] = np.eye(P, dtype=np.float32)
    r["upper"], r["ones"] = np.triu(np.ones((P, P), np.float32), 1), np.ones((P, P), np.float32)
    r["count_e"] = (NE - np.arange(NE, dtype=np.float32))[None]
    r["tile_row"] = (P * np.arange(MT, dtype=np.float32))[None]
    r["row_no"] = np.arange(P, dtype=np.float32)[None]
    r["token"] = (np.arange(P)[:, None] + P * np.arange(T)[None]).astype(np.float32)
    r["spare"] = (T * P + np.arange(P, dtype=np.float32))[:, None]
    r["rope_c"], r["rope_s"] = rope_tables()
    pick = np.zeros((P, NE, P), np.float32)
    which = np.zeros((2 * H, H, P + KR), np.float32)
    for s in range(3):
        for e in range(NE):
            pick[32 * s + e, e] = 1
    for s in range(2):
        for h in range(H):
            which[s * H + h, h, 0:C] = 1
    r["pick"], r["which_head"] = pick.reshape(P, -1), which.reshape(2 * H, -1)
    return {k: np.ascontiguousarray(v) for k, v in r.items()}


def kernel(**inputs):
    import concourse.bacc as bacc
    from concourse.bass_utils import run_bass_kernel_spmd

    nc = bacc.Bacc("TRN2", target_bir_lowering=False, num_devices=1)
    arrays = layout(inputs)
    aps = {n: nc.dram_tensor(f"in_{n}", v.shape, mybir.dt.from_np(v.dtype), kind="ExternalInput").ap() for n, v in arrays.items()}
    out = nc.dram_tensor("out", (B * S + P, D), fp32, kind="ExternalOutput").ap()
    build(nc, aps, out)
    r = run_bass_kernel_spmd(nc, [{f"in_{n}": v for n, v in arrays.items()}], core_ids=[0])
    return r.results[0]["out"][:B * S].reshape(B, S, D)
```

```python
import numpy as np
import concourse.bass as bass
from concourse import mybir
from contextlib import ExitStack

fp32 = mybir.dt.float32
bf16 = mybir.dt.bfloat16
i32 = mybir.dt.int32
u32 = mybir.dt.uint32
ALU = mybir.AluOpType
ACT = mybir.ActivationFunctionType
AX = mybir.AxisListType

P = 128
B, S, D = 4, 1024, 256
C = 154
CR = C - P
KR = 32
H, HD = 16, 16
KV = 4
HQ = H // KV
ST = S // P
T = B * ST
NE, HID = 8, 512
MT = T + NE - 1
PARTS = 6
RS = PARTS * HD
QKV = D + 2 * KV * HD
NH2 = H + KV
EPS_LN, EPS_RMS = 1e-5, 1e-6
SCALE = HD ** -0.5

TILE_ORDER = (5, 0, 7, 2, 6, 1, 4, 3)
PAIRS = [(n, i) for n, j in enumerate(TILE_ORDER) for i in (j, *range(j))]
FIRST = [next(s for s, p in enumerate(PAIRS) if p[0] == n) for n in range(ST)]
LEAD = 2
TAIL_STEPS, X_STEPS, CTX_STEPS = 8, 20, 6
TAIL_EVERY = 4 
X_START = (1, 6, 11, 16, 21, 26, 31, 36)
SLOTS = 51
X_AT = (0, 2, 3, 4, 5, 6, 7, 8, 9, 10, 11, 12, 13, 14, 15, 16, 17, 18, 20, 21)
TAIL_AT = (0, 1, 2, 3, 4, 6, 7, 8)
RANK = {name: n for n, name in enumerate((
    ("swap", 0), ("scores", 0), ("values", 0), ("values", 1), ("tail", 7), ("flush", 0), ("tail", 6),
    ("tail", 4), ("scores", 1), ("x", 1), ("tail", 2), ("tail", 1), ("prep", 0), ("prep", 1), ("ctx", 0),
    ("ctx", 1), ("ctx", 2), ("ctx", 3), ("tail", 3), ("ctx", 4), ("ctx", 5), ("x", 19), ("x", 18), ("x", 17),
    ("x", 16), ("tail", 5), ("x", 15), ("x", 14), ("tail", 0), ("x", 13), ("x", 12), ("x", 11), ("x", 10),
    ("x", 9), ("x", 8), ("key", 0), ("key", 1), ("key", 2), ("x", 7), ("x", 6), ("x", 5), ("x", 4), ("x", 3),
    ("x", 2), ("x", 0)), 1)}


def tail_starts():
    out = []
    for n in range(ST):
        end = LEAD + FIRST[n] + TILE_ORDER[n] + 2
        out.append(max(end, out[-1] + TAIL_EVERY if out else 0))
    return out


def prep_starts():
    out = [LEAD + FIRST[n] - 3 for n in range(ST)]
    for n in reversed(range(ST - 1)):
        out[n] = min(out[n], out[n + 1] - 2)
    return out


def slot(s, second, first):
    tails = tail_starts()
    p = s - LEAD
    if second:
        if s == 0:
            yield "swap", 0, 0
        for half in range(2):
            if 0 <= p < len(PAIRS):
                yield "scores", p, half
            if 0 < p <= len(PAIRS):
                yield "values", p - 1, half
        for n in range(ST):
            if p == FIRST[n] + TILE_ORDER[n] + 1:
                yield "flush", 0, n
        for n in range(ST):
            for r in range(TAIL_STEPS):
                if s == tails[n] + TAIL_AT[r]:
                    yield "tail", r, n
        for n in range(ST):
            at = prep_starts()[n]
            if n == 0:
                if s < 2:
                    yield from (("prep", 0, 0), ("prep", 1, 0)) if s == 0 else (("prep", 2, 0),)
            elif 0 <= s - at < 3:
                yield "prep", s - at, n
    if first:
        if s < CTX_STEPS:
            yield "ctx", s, 0
        yield from first_steps(s, "x")
    if second:
        yield from first_steps(s + SLOTS, "late")


def first_steps(s, kind):
    for k in range(ST):
        for r in reversed(range(X_STEPS)):
            if s == X_START[k] + X_AT[r]:
                if r == 4:
                    yield "q_stack", 0, k
                yield kind, r, k
                if r == 8:
                    yield from (("key", n, k) for n in range(3))


CLEAN = (0, 14, 15, 18)
for k in range(ST):
    assert next((r for r in range(X_STEPS) if X_START[k] + X_AT[r] >= SLOTS), 0) in CLEAN
EARLY_V = [k for k in range(ST) if X_START[k] + X_AT[17] < SLOTS]


def frees(step):
    kind, r, _ = step
    return kind == "prep" and r == 2 or kind == "ctx" and r % 2 == 1 or kind == "q_stack"


def rank(step):
    kind, r, k = step
    if frees(step):
        return 0
    name = (kind, k) if kind in ("scores", "values") else ("x" if kind == "late" else kind, r)
    return RANK.get(name, 50)


def order(second, first):
    for s in range(SLOTS):
        yield from sorted(slot(s, second, first), key=rank)


U, M = "u", "m"
N_U, N_M, N_E = 2, 3, 5


def results(step):
    kind, r, k = step
    if kind == "scores":
        return [(U, ("s", r, k))]
    if kind == "key":
        return [(U, ("key", k, r))]
    if kind == "prep":
        return [(U, ("qs", k))] if r == 1 else []
    if kind == "tail":
        return {0: [(M, ("so", k))], 1: [(M, ("soT", k))], 2: [(M, ("gate", k))], 3: [(M, ("wo", k))],
                5: [(M, ("h2T", k))], 6: [(M, ("logit", k))]}.get(r, [])
    if kind == "ctx":
        return {0: [(U, ("kv",)), (U, ("vr",))], 2: [(U, ("kT", 0))], 4: [(U, ("kT", 1))]}.get(r, [])
    if kind in ("x", "late"):
        return {1: [(M, ("xnT", k))], 2: [(M, ("q", k))], 3: [(U, ("qT", k))],
                4: [(M, ("row", k, 0)), (M, ("row", k, 1))], 5: [(M, ("row", k, 2)), (M, ("row", k, 3))],
                6: [(M, ("row", k, 4)), (M, ("row", k, 5))], 7: [(M, ("shift", k))],
                9: [(M, ("oT", k))], 10: [(M, ("o", k))], 11: [(M, ("onT", k))], 12: [(M, ("xo", k))],
                15: [(M, ("hT", k))], 16: [(M, ("qkv", k))], 18: [(M, ("ksT", k))]}.get(r, [])
    return []


def exponentials(step):
    kind, r, k = step
    if kind == "scores":
        return [("s", r, k)]
    if kind == "key":
        return [("key", k, r)]
    return []


class Turns:

    def __init__(self, sections, n, sems, names):
        self.n, self.sems, self.place, self.uses = n, sems, {}, {}
        for sec in sections:
            used = [0] * n
            turn = 0
            for step in sections[sec]:
                for name in names(step):
                    i = turn % n
                    self.place[sec, name] = (i, used[i])
                    used[i] += 1
                    turn += 1
            self.uses[sec] = used

    def at(self, sec, b, name):
        i, k = self.place[sec, name]
        if sec == "body":
            k = k + self.uses["pro"][i] + b * self.uses["body"][i]
        elif sec == "epi":
            k = k + self.uses["pro"][i] + (B - 1) * self.uses["body"][i]
        return i, self.sems[i], k, k + 1


def build(nc, a, out):
    ctx = ExitStack()
    with ctx:
        def sb(name, shape, dt=fp32):
            return ctx.enter_context(nc.sbuf_tensor(name, shape, dt))

        def ps(name, shape, dt=fp32):
            return ctx.enter_context(nc.psum_tensor(name, shape, dt))

        def sem(name):
            return ctx.enter_context(nc.semaphore(name))

        rows_dram = nc.dram_tensor("token_rows", ((T + 1) * P, 2 * D), fp32, kind="Internal").ap()

        identf = sb("identf", [P, P])
        identb = sb("identb", [P, P], bf16)
        xw = sb("xw", [P, 4, 2, D])
        xbias = sb("xbias", [P, 4, D])
        w_qkv = sb("w_qkv", [P, 2, QKV])
        b_qkv = sb("b_qkv", [P, QKV])
        w_o = sb("w_o", [P, 2, D])
        b_o = sb("b_o", [P, D])
        w_gate = sb("w_gate", [P, P])
        b_gate = sb("b_gate", [P, 1])
        w_r = sb("w_r", [P, 2, NE])
        b_r = sb("b_r", [P, NE])
        ln1 = sb("ln1", [P, D])
        ln2 = sb("ln2", [P, D])
        qk_w = sb("qk_w", [P, NH2, HD])
        rope_c = sb("rope_c", [P, ST, HD])
        rope_s = sb("rope_s", [P, ST, HD])
        W1 = sb("W1", [P, NE, 2, 2 * HID])
        W2 = sb("W2", [P, NE, HID // P, D])
        rows_w2 = W2[:].rearrange("p e k n -> p (e k n)")
        taken = 0

        def room(n_words):
            nonlocal taken
            taken += n_words
            assert taken <= NE * HID // P * D
            return rows_w2[:, taken - n_words:taken]

        b1_parts = sb("b1_parts", [P, 2 * HID], bf16)
        b2_parts = sb("b2_parts", [P, D], bf16)
        pick = sb("pick", [P, NE, P], bf16)
        bshift = sb("bshift", [P, 1])
        upper = sb("upper", [P, P])
        ones = sb("ones", [P, P])
        count_e = sb("count_e", [P, NE])
        tile_row = sb("tile_row", [P, MT])
        tile_no = sb("tile_no", [P, MT])
        row_no = sb("row_no", [P, P])
        token = sb("token", [P, T, 2])
        spare = sb("spare", [P, 1])
        zero_rows = sb("zero_rows", [P, 2 * D])

        ctxT = sb("ctxT", [P, 2, C])
        kf = sb("kf", [P, D])
        kl = sb("kl", [P, D])
        k_rest = sb("k_rest", [P, D])
        k_tok = room(H * RS // 2).bitcast(bf16).rearrange("p (h n) -> p h n", n=RS)
        Kx = sb("Kx", [P, H, P + KR], bf16)
        Vx = sb("Vx", [P, H, 32])
        Vr = sb("Vr", [P, H // 4, P])
        stats = [sb(f"stats{i}", [P, 6]) for i in range(2)]
        mv = [sb(f"mv{i}", [P, 2]) for i in range(2)]
        rstd = [sb(f"rstd{i}", [P, 1]) for i in range(2)]
        xn = sb("xn", [P, D])
        xnT = sb("xnT", [P, 2 * P])
        qf = sb("qf", [P, D])
        rest = sb("rest", [P, D])
        q_tok = room(H * RS // 2).bitcast(bf16).rearrange("p (h n) -> p h n", n=RS)
        Qx = [room(H * P // 2).bitcast(bf16).rearrange("p (h n) -> p h n", n=P) for i in range(2)]
        mx = sb("mx", [P, H])
        nmx = sb("nmx", [P, 2, H], bf16)
        nmT = sb("nmT", [P, 1, P], bf16)
        oT = sb("oT", [P, 512])
        rsum = sb("rsum", [P, H])
        on = sb("on", [P, D])
        onT = sb("onT", [P, 2 * P])
        ss = sb("ss", [P, 1])
        rs_row = sb("rs_row", [P, 1])
        hh = sb("hh", [P, D])
        hT = sb("hT", [P, 2 * P])
        sq = sb("sq", [P, NH2 * HD])
        sqa = sb("sqa", [P, D])
        qkv = sb("qkv", [P, QKV])
        hs = sb("hs", [P, NH2])
        h_rs = sb("h_rs", [P, NH2])
        ra = sb("ra", [P, NH2 * HD])
        rb = sb("rb", [P, NH2 * HD])
        ks_rest = sb("ks_rest", [P, KV * HD])
        ks_tok = sb("ks_tok", [P, KV, RS + 1], bf16)
        safe = {name: sb(f"safe_{name}", [P, NH2]) for name in ("rstd0", "rstd1", "y0_rs", "h_rs", "x2_rs")}
        minus_half = sb("minus_half", [P, NH2])
        Va_next = sb("Va_next", [P, ST, KV, 32])

        E = [sb(f"E{i}", [P, 1024]) for i in range(N_E)]

        rows_w1 = W1[:].rearrange("p e k n -> p (e k n)")
        xb = rows_w1[:, 0:4096].rearrange("p (j n) -> p j n", n=D)
        y0 = rows_w1[:, 4096:8192].rearrange("p (j n) -> p j n", n=D)
        q_hat = rows_w1[:, 8192:12288].rearrange("p (j n) -> p j n", n=D)
        Kst = rows_w1[:, 12288:16384].bitcast(bf16).rearrange("p (c g n) -> p c g n", c=2, g=KV)
        Va = sb("Va", [P, ST, KV, 32])
        qs_rest = room(D)
        qs_tok = sb("qs_tok", [P, H, RS + 1], bf16)
        Qs_room = [room(H * P // 2) for i in range(2)]
        Qs = [r.bitcast(bf16).rearrange("p (h n) -> p h n", n=P) for r in Qs_room]
        soT = [room(512) for i in range(2)]
        s_rsum = sb("s_rsum", [P, H])
        s_on = room(D)
        s_onT = room(2 * P)
        gt = room(2 * P)
        x2 = room(D)
        s_sqa = room(D)
        s_ss = sb("s_ss", [P, 1])
        s_rs = sb("s_rs", [P, 1])
        base = sb("base", [P, D])
        h2 = sb("h2", [P, D])
        h2T = sb("h2T", [P, 2 * P])
        half_b_gate = sb("half_b_gate", [P, 1])
        logits = sb("logits", [P, T, NE])

        onehot = sb("onehot", [P, T, NE])
        first_e = sb("first_e", [P, T, NE])
        best = sb("best", [P, T])
        total = sb("total", [P, NE, T])
        cum = sb("cum", [P, NE, T])
        padded = sb("padded", [P, NE])
        whole = sb("whole", [P, NE], i32)
        offset = sb("offset", [P, NE])
        placef = sb("placef", [P, T])
        place = sb("place", [P, T], i32)
        place_tile = sb("place_tile", [P, T])
        place_row = sb("place_row", [P, T])
        split_i = sb("split_i", [P, 2, T], i32)
        taken_by = sb("taken_by", [P, MT])
        ids = sb("ids", [P, MT])
        idx = sb("idx", [P, MT], u32)
        idx_in = [sb(f"idx_in{i}", [P, 1], u32) for i in range(2)]
        idx_out = [sb(f"idx_out{i}", [P, 1], u32) for i in range(2)]
        G = T // 4
        row_hot = [E[g][:].bitcast(bf16)[:, 0:G * P].rearrange("p (t n) -> p t n", n=P) for g in range(4)]
        flat = lambda t: t[:].rearrange("p a b c -> p (a b c)")
        tile_hot = [r[:, 0:G * 3 * MT].rearrange("p (t a n) -> p t a n", a=3, n=MT) for r in
                    (E[4][:].bitcast(bf16), flat(Va).bitcast(bf16), flat(Va_next).bitcast(bf16), Kx[:].rearrange("p h n -> p (h n)"))]
        owns = sb("owns", [P, MT, NE])
        expertf = sb("expertf", [P, MT])
        expert = sb("expert", [P, MT], i32)
        part = lambda e, n, w: E[e][:, n * w:(n + 1) * w]
        xr = [E[3][:, i * 2 * D:(i + 1) * 2 * D] for i in range(2)]
        yr, bs = [part(0, i, D) for i in range(2)], [part(0, 2 + i, D) for i in range(2)]
        sig, act_u = [part(1, i, HID) for i in range(2)]
        actT, xT = part(2, 0, HID), [part(2, 2 + i, D) for i in range(2)]

        ps_u = [ps(f"ps_u{i}", [P, 1024]) for i in range(N_U)]
        ps_m = [ps(f"ps_m{i}", [P, 512]) for i in range(N_M)]
        ps_o = ps("ps_o", [P, 512])

        names = {}

        def ev(name):
            if name not in names:
                names[name] = sem(name)
            return names[name]

        s_first = sem("s_first")
        s_w = sem("s_w")
        s_big = sem("s_big")
        s_ctx = sem("s_ctx")
        s_x = [sem(f"s_x{i}") for i in range(ST)]
        s_st = sem("s_st")
        s_xr = [sem(f"s_xr{i}") for i in range(2)]
        s_yr = [sem(f"s_yr{i}") for i in range(2)]
        s_spare = sem("s_spare")
        s_alone = sem("s_alone")
        u_read = [sem(f"u_read{i}") for i in range(N_U)]
        m_read = [sem(f"m_read{i}") for i in range(N_M)]
        e_read = [sem(f"e_read{i}") for i in range(N_E)]

        sections = {"pro": list(order(False, True)), "body": list(order(True, True)), "epi": list(order(True, False))}
        turns = {U: Turns(sections, N_U, u_read, lambda st: [n for r, n in results(st) if r == U]),
                 M: Turns(sections, N_M, m_read, lambda st: [n for r, n in results(st) if r == M])}
        e_turns = Turns(sections, N_E, e_read, exponentials)
        last_pair = lambda n: FIRST[n] + TILE_ORDER[n]

        def alone(eng):
            eng.sem_inc(s_alone, 1)

        def wait(eng, sem_, n):
            if not (isinstance(n, int) and n <= 0):
                eng.wait_ge(sem_, n)

        def parity(b):
            return b % 2

        which_f = rows_w1[RS:P, 4096:4096 + H * (P + KR)]
        pick_f, b1_f, b2_f = Qs_room[0], Qs_room[1], soT[0][:, 0:D]
        urgent = [(identf[:], a["identf"]), (which_f, a["which_head"])]
        for n in (1, 2, 0, 3):
            urgent.append((xw[:, n], a["xw"][n].rearrange("(k p) n -> p k n", p=P)))
            urgent.append((xbias[:, n, :], a["xb"][n:n + 1, :].to_broadcast([P, D])))
        small = [
            (count_e[:], a["count_e"].to_broadcast([P, NE])),
            (tile_row[:], a["tile_row"].to_broadcast([P, MT])),
            (tile_no[:], a["row_no"][:, 0:MT].to_broadcast([P, MT])),
            (row_no[:], a["row_no"].to_broadcast([P, P])),
            (token[:], a["token"]), (spare[:], a["spare"]),
            (w_qkv[:], a["w_qkv"].rearrange("(k p) n -> p k n", p=P)),
            (w_o[:], a["L0_ffn_Wo"].rearrange("(k p) n -> p k n", p=P)),
            (w_gate[:], a["w_gate"]), (b_gate[:], a["b_gate"]),
            (w_r[:], a["L0_ffn_Wr"].rearrange("(k p) n -> p k n", p=P)),
            (b_qkv[:], a["b_qkv"].to_broadcast([P, QKV])),
            (b_o[:], a["bo"].to_broadcast([P, D])),
            (b_r[:], a["br"].to_broadcast([P, NE])),
            (ln1[:], a["ln1"].to_broadcast([P, D])),
            (ln2[:], a["ln2"].to_broadcast([P, D])),
            (qk_w[:].rearrange("p h d -> p (h d)"), a["qk_w"].to_broadcast([P, NH2 * HD])),
            (rope_c[:], a["rope_c"].rearrange("(j p) d -> p j d", p=P)),
            (rope_s[:], a["rope_s"].rearrange("(j p) d -> p j d", p=P)),
            (pick_f, a["pick"]), (b1_f, a["b1_rows"]), (b2_f, a["b2_rows"]),
            (upper[:], a["upper"]), (ones[:], a["ones"]),
        ]
        NW = len(small)
        N_CLEARED = 16
        N_OWN = {"body": 158}

        class Own:

            def __init__(self, eng, sem_, base):
                self.eng, self.sem, self.n, self.base = eng, sem_, 0, base

            def link(self, ins):
                ins.then_inc(self.sem, 1)
                self.n += 1
                self.eng.wait_ge(self.sem, self.base + self.n)

        def go_through(eng, do):
            for step in sections["pro"]:
                do("pro", 0, step)
            copy_of_b = eng.alloc_register()
            with eng.Fori(0, B - 1) as b:
                for n, step in enumerate(sections["body"]):
                    if n % 8 == 0:
                        eng.reg_mov(copy_of_b, b)
                        batch = eng.snap(copy_of_b, min_val=0, max_val=B - 2)
                    do("body", batch, step)
            for step in sections["epi"]:
                do("epi", B - 1, step)

        def batch_of(sec, b, kind):
            return 0 if sec == "pro" else b if kind == "late" else b + 1

        def row(b, j, of):
            if isinstance(b, int):
                return of[:, (b % 2) * ST + j]
            return of[:, bass.ds(parity(b) * ST + j, 1)].rearrange("p a n -> p (a n)")

        block = ctx.enter_context(nc.Block())

        @block.sync
        def _(sp):
            def load_x(b, j, par):
                sp.dma_start(xb[:, par * ST + j if isinstance(par, int) else bass.ds(par * ST + j, 1)],
                             a["x"][bass.ds(b * S + j * P, P)] if not isinstance(b, int) else a["x"][b * S + j * P:b * S + j * P + P]).then_inc(s_x[j], 16)

            sp.sem_inc(s_st, 32)
            sp.dma_start(ctxT[:], a["ctxT"][0].rearrange("(k p) n -> p k n", p=P)).then_inc(s_ctx, 16)
            load_x(0, 0, 0)
            for dst, src in urgent:
                sp.dma_start(dst, src).then_inc(s_first, 16)
            for dst, src in small:
                sp.dma_start(dst, src).then_inc(s_w, 16)
            for j in range(1, ST):
                load_x(0, j, 0)
            sp.wait_ge(ev("ctx_proj"), 1)
            sp.dma_start(ctxT[:], a["ctxT"][1].rearrange("(k p) n -> p k n", p=P)).then_inc(s_ctx, 16)
            for j in range(ST):
                sp.wait_ge(s_x[j], 16)
                load_x(1, j, 1)
            sp.wait_ge(ev("zeros"), 1)
            sp.dma_start(rows_dram[T * P:], zero_rows[:]).then_inc(s_spare, 16)

            def stores(b, more):
                for n, j in enumerate(TILE_ORDER):
                    sp.wait_ge(ev("base"), b * ST + n + 1)
                    alone(sp)
                    t = b * ST + j
                    at = slice(t * P, t * P + P) if isinstance(t, int) else bass.ds(t * P, P)
                    sp.dma_start(rows_dram[at, D:], base[:]).then_inc(s_st, 16)
                    if more:
                        load_x(b + 2, j, parity(b))
                    sp.wait_ge(ev("h2"), b * ST + n + 1)
                    alone(sp)
                    sp.dma_start(rows_dram[at, 0:D], h2[:]).then_inc(s_st, 16)

            with sp.Fori(0, 2) as b:
                sp.wait_ge(ev("ctx_proj"), b + 2)
                sp.dma_start(ctxT[:], a["ctxT"][bass.ds(b + 2, 1)].rearrange("a (k p) n -> p (a k) n", p=P)).then_inc(s_ctx, 16)
                stores(b, True)
            stores(2, False)
            even = lambda e: e % 2 == 0
            for e in filter(even, range(NE)):
                sp.dma_start(W1[:, e], a["L0_ffn_W1"][e].rearrange("(k p) n -> p k n", p=P)).then_inc(s_big, 16)
            stores(3, False)
            for e in range(NE):
                if not even(e):
                    sp.dma_start(W1[:, e], a["L0_ffn_W1"][e].rearrange("(k p) n -> p k n", p=P)).then_inc(s_big, 16)
            for e in range(NE):
                sp.dma_start(W2[:, e], a["L0_ffn_W2"][e].rearrange("(k p) n -> p k n", p=P)).then_inc(s_big, 16)

        @block.gpsimd
        def _(pool):
            pool.sem_inc(ev("yr_free"), 2)
            pool.memset(zero_rows[:], 0.0).then_inc(ev("zeros"), 1)
            n = 0

            def fill(dst, value):
                nonlocal n
                pool.memset(dst, value).then_inc(ev("cleared"), 1)
                n += 1
                pool.wait_ge(ev("cleared"), n)

            for dst in (Vx[:], Vr[:], Va[:], Va_next[:], Kx[0:RS, :, P:P + KR], b1_parts[:], b2_parts[:]):
                fill(dst, 0.0)
            fill(minus_half[:], -0.5)
            for dst in (Vx[:, :, HD:HD + 1], Va[:, :, :, HD:HD + 1], Va_next[:, :, :, HD:HD + 1], ks_tok[:, :, RS:RS + 1],
                        *(Vr[32 * q:32 * q + CR, :, 32 * q + HD:32 * q + HD + 1] for q in range(4))):
                fill(dst, 1.0)
            assert n == N_CLEARED, n

            def root(ready, n, dst, src, eps, done):
                w = dst.shape[1]
                pool.wait_ge(ev(ready), n)
                alone(pool)
                pool.tensor_scalar(safe[done][:, 0:w], src, eps, None, ALU.add).then_inc(ev(f"safe_{done}"), 1)
                pool.wait_ge(ev(f"safe_{done}"), n)
                pool.tensor_tensor(dst, safe[done][:, 0:w], minus_half[:, 0:w], ALU.pow).then_inc(ev(done), 1)

            def add_bias(of, bx, k, bias, used, n, done):
                pool.wait_ge(ev(used), n)
                alone(pool)
                pool.tensor_tensor(row(bx, k, of), row(bx, k, of), bias, ALU.add).then_inc(ev(done), 1)

            def do(sec, b, step):
                kind, r, k = step
                bx = batch_of(sec, b, kind)
                X = ST * bx + k
                Y = ST * b + k
                if kind in ("x", "late") and r == 0:
                    root("mv0", X + 1, rstd[0][:], mv[0][:, 1:2], EPS_LN, "rstd0")
                if kind in ("x", "late") and r == 2:
                    add_bias(xb, bx, k, xbias[:, 3], "xn", X + 1, "x_biased")
                if kind in ("x", "late") and r == 16:
                    add_bias(y0, bx, k, b_o[:], "hh", X + 1, "y0_biased")
                if kind in ("x", "late") and r == 13:
                    root("mv1", X + 1, rstd[1][:], mv[1][:, 1:2], EPS_LN, "rstd1")
                if kind in ("x", "late") and r == 14:
                    root("y0_ss", X + 1, rs_row[:], ss[:], EPS_RMS, "y0_rs")
                if kind in ("x", "late") and r == 17:
                    root("h_ms", X + 1, h_rs[:], hs[:], EPS_RMS, "h_rs")
                if kind == "tail" and r == 4:
                    root("x2_ss", Y + 1, s_rs[:], s_ss[:], EPS_RMS, "x2_rs")
                if kind == "scores" and PAIRS[r][1] == TILE_ORDER[PAIRS[r][0]]:
                    _, rd, _, after = turns[U].at(sec, b, ("s", r, k))
                    e, _, _, _ = e_turns.at(sec, b, ("s", r, k))
                    pool.wait_ge(rd, after)
                    alone(pool)
                    e3 = E[e][:].rearrange("p (h n) -> p h n", n=P)
                    pool.affine_select(out=e3, in_=e3, compare_op=ALU.is_ge, fill=0.0, base=0,
                                       pattern=[[0, 1024 // P], [1, P]], channel_multiplier=-1).then_inc(ev("masked"), 1)

            go_through(pool, do)
            pool.wait_ge(ev("places"), 1)
            pool.wait_ge(s_st, 32 * (T + 1))
            pool.wait_ge(s_spare, 16)

            def copy_idx(dst, m):
                src = idx[:, m:m + 1] if isinstance(m, int) else idx[:, bass.ds(m, 1)]
                pool.tensor_copy(dst[:], src).then_inc(ev("idx_copy"), 1)

            def gather(m, i, before):
                if not isinstance(m, int) or m >= 2:
                    pool.wait_ge(ev("base_rows"), m - 1)
                    alone(pool)
                copy_idx(idx_in[i], m)
                pool.wait_ge(ev("idx_copy"), before + 1)
                alone(pool)
                pool.indirect_dma_start(out=xr[i], out_offset=None, in_=rows_dram,
                                        in_offset=bass.IndirectOffsetOnAxis(ap=idx_in[i][:], axis=0)).then_inc(s_xr[i], 16)

            def scatter(m, i, before):
                pool.wait_ge(ev("y_rows"), m + 1)
                alone(pool)
                copy_idx(idx_out[i], m)
                pool.wait_ge(ev("idx_copy"), before + 1)
                alone(pool)
                pool.indirect_dma_start(out=out, out_offset=bass.IndirectOffsetOnAxis(ap=idx_out[i][:], axis=0),
                                        in_=yr[i], in_offset=None).then_inc(s_yr[i], 16)

            def scattered(i, n):
                pool.wait_ge(s_yr[i], 16 * n + 16)
                pool.sem_inc(ev("yr_free"), 1)

            for m in range(4):
                gather(m, m % 2, m)
            scatter(0, 0, 4)
            with pool.Fori(0, MT // 2 - 2) as n:
                for m, i, last in ((2 * n + 1, 1, (0, n)), (2 * n + 2, 0, (1, n))):
                    gather(m + 3, 1 - i, 2 * m + 3)
                    scattered(*last)
                    scatter(m, i, 2 * m + 4)
            m = MT - 4
            gather(m + 3, 0, 2 * m + 3)
            for m in range(MT - 4, MT):
                scattered((m - 1) % 2, (m - 1) // 2)
                scatter(m, m % 2, MT + m)
            pool.wait_ge(s_yr[(MT - 1) % 2], 16 * ((MT + 1) // 2))

        @block.tensor
        def _(pe):
            def take(which, sec, b, name):
                i, rd, before, _ = turns[which].at(sec, b, name)
                wait(pe, rd, before)
                return (ps_u if which == U else ps_m)[i]

            def await_read(which, sec, b, name):
                _, rd, _, after = turns[which].at(sec, b, name)
                pe.wait_ge(rd, after)

            def turn_blocks(dst, src, n):
                for k in range(n):
                    mm = pe.transpose(dst[:, k * P:(k + 1) * P], src[:, k * P:(k + 1) * P], identf[:])
                return mm

            def project(dst, xT_, w):
                for k in range(2):
                    mm = pe.matmul(dst, xT_[:, k * P:(k + 1) * P], w[:, k], start=(k == 0), stop=(k == 1), skip_group_check=True)
                return mm

            def ctx_step(sec, b, r):
                bx = 0 if sec == "pro" else b + 1
                if r == 0:
                    pe.wait_ge(s_ctx, 16 * (bx + 1))
                    kv = take(U, sec, b, ("kv",))
                    for w, o in ((1, 0), (2, 256)):
                        for k in range(2):
                            pe.matmul(kv[:, o:o + D], ctxT[:, k, 0:P], xw[:, w, k], start=(k == 0), stop=(k == 1), skip_group_check=True)
                    for k in range(2):
                        mm = pe.matmul(kv[0:CR, 512:512 + D], ctxT[:, k, P:C], xw[:, 1, k], start=(k == 0), stop=(k == 1))
                    mm.then_inc(ev("kv_ps"), 1)
                    vr = take(U, sec, b, ("vr",))
                    for q in range(4):
                        for k in range(2):
                            mm = pe.matmul(vr[32 * q:32 * q + CR, 0:D], ctxT[:, k, P:C], xw[:, 2, k], start=(k == 0), stop=(k == 1))
                    mm.then_inc(ev("ctx_proj"), 1)
                if r in (2, 4):
                    n = r // 2 - 1
                    rows_ = (P, CR)[n]
                    ub = take(U, sec, b, ("kT", n))[:].bitcast(bf16)
                    pe.wait_ge(ev("k_split"), bx * 2 + n + 1)
                    alone(pe)
                    for h in range(H):
                        mm = pe.transpose(ub[0:RS, h * P:h * P + rows_], k_tok[0:rows_, h, :], identb[0:rows_, 0:rows_])
                    mm.then_inc(ev("k_turned"), 1)

            def x_step(sec, b, bx, r, k):
                X = ST * bx + k
                at = (sec, b)
                q = Qx[k % 2]
                if r == 1:
                    dst = take(M, *at, ("xnT", k))
                    pe.wait_ge(ev("xn"), X + 1)
                    turn_blocks(dst, xn, 2).then_inc(ev("xnT_ps"), 1)
                if r == 2:
                    dst = take(M, *at, ("q", k))
                    await_read(M, *at, ("xnT", k))
                    project(dst[:, 0:D], xnT, xw[:, 0]).then_inc(ev("q_ps"), 1)
                if r == 3:
                    ub = take(U, *at, ("qT", k))[:].bitcast(bf16)
                    pe.wait_ge(ev("q_split"), X + 1)
                    for h in range(H):
                        mm = pe.transpose(ub[0:RS, h * P:(h + 1) * P], q_tok[:, h, :], identb[:])
                    mm.then_inc(ev("q_turned"), 1)
                if r in (4, 5, 6):
                    if r == 4:
                        await_read(U, *at, ("kT", 1))
                        await_read(U, *at, ("qT", k))
                    for c in (2 * r - 8, 2 * r - 7):
                        dst = take(M, *at, ("row", k, c))
                        for h in range(3 * c, min(3 * c + 3, H)):
                            mm = pe.matmul(dst[:, (h % 3) * C:(h % 3 + 1) * C], q[0:RS, h], Kx[0:RS, h, 0:C], start=True, stop=True, skip_group_check=True)
                        mm.then_inc(ev("row_ps"), 1)
                if r == 7:
                    dst = take(M, *at, ("shift", k))
                    pe.wait_ge(ev("shift"), X + 1)
                    pe.transpose(dst[:].bitcast(bf16)[RS:P, 0:P], nmx[:].rearrange("p a h -> p (a h)"), identb[:], tile_position=(0, RS)).then_inc(ev("shiftT_ps"), 1)
                if r == 9:
                    dst = take(M, *at, ("oT", k))
                    for n in range(2):
                        await_read(U, *at, ("key", k, n))
                        e, rd, _, _ = e_turns.at(*at, ("key", k, n))
                        for h in range(8 * n, 8 * n + 8):
                            g = h // 4
                            mm = pe.matmul(dst[32 * (h % 4):32 * (h % 4) + 32, g * P:(g + 1) * P], Vx[:, h], E[e][:, (h % 8) * P:(h % 8 + 1) * P],
                                           start=(g == 0), stop=False, skip_group_check=True)
                        mm.then_inc(rd, 1)
                    await_read(U, *at, ("key", k, 2))
                    e, rd, _, _ = e_turns.at(*at, ("key", k, 2))
                    for g in range(4):
                        mm = pe.matmul(dst[:, g * P:(g + 1) * P], Vr[:, g], E[e][:, g * P:(g + 1) * P], start=False, stop=True, skip_group_check=True)
                    mm.then_inc(rd, 1)
                if r == 10:
                    dst = take(M, *at, ("o", k))
                    await_read(M, *at, ("oT", k))
                    turn_blocks(dst, oT, 4).then_inc(ev("o_ps"), 1)
                if r == 11:
                    dst = take(M, *at, ("onT", k))
                    await_read(M, *at, ("o", k))
                    turn_blocks(dst, on, 2).then_inc(ev("onT_ps"), 1)
                if r == 12:
                    dst = take(M, *at, ("xo", k))
                    await_read(M, *at, ("onT", k))
                    project(dst[:, 0:D], onT, xw[:, 3]).then_inc(ev("xo_ps"), 1)
                if r == 15:
                    dst = take(M, *at, ("hT", k))
                    pe.wait_ge(ev("hh"), X + 1)
                    turn_blocks(dst, hh, 2).then_inc(ev("hT_ps"), 1)
                if r == 16:
                    if sec == "pro" and k == 0:
                        pe.wait_ge(s_w, NW * 16)
                    dst = take(M, *at, ("qkv", k))
                    await_read(M, *at, ("hT", k))
                    project(dst[:, 0:QKV], hT, w_qkv[:]).then_inc(ev("qkv_ps"), 1)
                if r == 18:
                    dst = take(M, *at, ("ksT", k))[:].bitcast(bf16)
                    pe.wait_ge(ev("ks_split"), X + 1)
                    for g in range(KV):
                        mm = pe.transpose(dst[0:RS + 1, g * P:(g + 1) * P], ks_tok[:, g, :], identb[:])
                    mm.then_inc(ev("ks_ps"), 1)

            def key_step(sec, b, n, k):
                X = ST * batch_of(sec, b, "x") + k
                q = Qx[k % 2]
                if n == 0:
                    pe.wait_ge(ev("shiftT"), X + 1)
                dst = take(U, sec, b, ("key", k, n))
                if n < 2:
                    for h in range(8 * n, 8 * n + 8):
                        mm = pe.matmul(dst[:, (h % 8) * P:(h % 8 + 1) * P], Kx[:, h, 0:P], q[:, h], start=True, stop=True, skip_group_check=True)
                else:
                    for h in range(H):
                        g = h // 4
                        mm = pe.matmul(dst[32 * (h % 4):32 * (h % 4) + 32, g * P:(g + 1) * P], Kx[:, h, P:P + KR], q[:, h],
                                       start=True, stop=True, skip_group_check=True)
                mm.then_inc(ev("key_ps"), 1)

            def second_step(sec, b, kind, r, k):
                at = (sec, b)
                if kind == "prep" and r == 1:
                    ub = take(U, *at, ("qs", k))[:].bitcast(bf16)
                    pe.wait_ge(ev("qs_split"), ST * b + k + 1)
                    for h in range(H):
                        mm = pe.transpose(ub[0:RS + 1, h * P:(h + 1) * P], qs_tok[:, h, :], identb[:])
                    mm.then_inc(ev("qs_ps"), 1)
                if kind == "scores":
                    n, i = PAIRS[r]
                    if r == FIRST[n] and k == 0:
                        pe.wait_ge(ev("ks_stack"), ST * b + TILE_ORDER[n] + 1)
                    if r == FIRST[n] and k == 0:
                        await_read(U, *at, ("qs", n))
                    dst = take(U, *at, ("s", r, k))
                    for g in (2 * k, 2 * k + 1):
                        keys = Kst[0:RS + 1, b % 2, g, i * P:(i + 1) * P] if isinstance(b, int) else \
                            Kst[0:RS + 1, bass.ds(parity(b), 1), g, i * P:(i + 1) * P].rearrange("p a n -> p (a n)")
                        mm = pe.matmul(dst[:, (g % 2) * 512:(g % 2) * 512 + 512], keys,
                                       Qs[n % 2][0:RS + 1, HQ * g:HQ * g + HQ].rearrange("p h n -> p (h n)"), start=True, stop=True)
                    mm.then_inc(ev("s_ps"), 1)
                if kind == "values":
                    n, i = PAIRS[r]
                    j = TILE_ORDER[n]
                    if r == FIRST[n] and k == 0:
                        pe.wait_ge(ev("so_T"), ST * b + n + 1)
                        if n == 0:
                            pe.wait_ge(ev("va"), b + 1)
                    if i == j:
                        pe.wait_ge(ev("masked"), (ST * b + n) * 2 + k + 1)
                    else:
                        await_read(U, *at, ("s", r, k))
                    e, rd, _, _ = e_turns.at(*at, ("s", r, k))
                    for g in (2 * k, 2 * k + 1):
                        mm = pe.matmul(ps_o[32 * g:32 * g + 32, :], Va[:, i, g], E[e][:, (g % 2) * 512:(g % 2) * 512 + 512],
                                       start=(r == FIRST[n]), stop=(r == last_pair(n)), skip_group_check=True)
                    mm.then_inc(rd, 1)
                if kind == "tail":
                    Y = ST * b + k
                    if r == 0:
                        dst = take(M, *at, ("so", k))
                        pe.wait_ge(ev("so_T"), Y + 2)
                        turn_blocks(dst, soT[k % 2], 4).then_inc(ev("so_ps"), 1)
                    if r == 1:
                        dst = take(M, *at, ("soT", k))
                        await_read(M, *at, ("so", k))
                        turn_blocks(dst, s_on, 2).then_inc(ev("soT_ps"), 1)
                    if r == 2:
                        dst = take(M, *at, ("gate", k))
                        await_read(M, *at, ("soT", k))
                        pe.matmul(dst[:, 0:2 * P], w_gate[:], s_onT[:], start=True, stop=True).then_inc(ev("gate_ps"), 1)
                    if r == 3:
                        dst = take(M, *at, ("wo", k))
                        pe.wait_ge(ev("gated"), Y + 1)
                        project(dst[:, 0:D], gt, w_o[:]).then_inc(ev("wo_ps"), 1)
                    if r == 5:
                        dst = take(M, *at, ("h2T", k))
                        pe.wait_ge(ev("h2"), Y + 1)
                        turn_blocks(dst, h2, 2).then_inc(ev("h2T_ps"), 1)
                    if r == 6:
                        dst = take(M, *at, ("logit", k))
                        await_read(M, *at, ("h2T", k))
                        project(dst[:, 0:NE], h2T, w_r[:]).then_inc(ev("logit_ps"), 1)

            def do(sec, b, step):
                kind, r, k = step
                if kind == "ctx":
                    ctx_step(sec, b, r)
                elif kind in ("x", "late"):
                    x_step(sec, b, batch_of(sec, b, kind), r, k)
                elif kind == "key":
                    key_step(sec, b, r, k)
                else:
                    second_step(sec, b, kind, r, k)

            pe.sem_inc(ev("so_T"), 1)
            pe.wait_ge(s_first, len(urgent) * 16)
            go_through(pe, do)

            pe.wait_ge(ev("onehot"), 1)
            oh = onehot[:].rearrange("p t e -> p (t e)")
            pe.matmul(ps_u[0][:, 0:T * NE], upper[:], oh, start=True, stop=True)
            pe.matmul(ps_u[0][:, 512:512 + T * NE], ones[:], oh, start=True, stop=True).then_inc(ev("ranks"), 1)
            for g in range(4):
                pe.wait_ge(ev("hot"), g + 1)
                for t in range(G):
                    mm = pe.matmul(ps_o[:, 0:3 * MT], row_hot[g][:, t], tile_hot[g][:, t].rearrange("p a n -> p (a n)"),
                                   start=(g == 0 and t == 0), stop=(g == 3 and t == G - 1))
            mm.then_inc(ev("ids_ps"), 1)
            pe.wait_ge(ev("places"), 1)
            pe.wait_ge(s_big, 2 * NE * 16)

            def turn_rows(m, i, n):
                pe.wait_ge(s_xr[i], 16 * n + 16)
                turn_blocks(ps_m[0], xr[i], 2).then_inc(ev("rowsT_ps"), 1)

            def up(m, i, e):
                pe.wait_ge(ev("rowsT"), m + 1)
                for half in (1, 0):
                    dst = ps_u[i][:, half * HID:(half + 1) * HID]
                    for k in range(2):
                        w = W1[:, bass.ds(e, 1), k, half * HID:(half + 1) * HID].rearrange("p a n -> p (a n)")
                        pe.matmul(dst, xT[i][:, k * P:(k + 1) * P], w, start=(k == 0), stop=False)
                    mm = pe.matmul(dst, pick[:, bass.ds(e, 1), :].rearrange("p a n -> p (a n)"), b1_parts[:, half * HID:(half + 1) * HID], start=False, stop=True)
                    mm.then_inc(ev("up_ps"), 1)

            def turn_act(m, i):
                pe.wait_ge(ev("act"), m + 1)
                turn_blocks(ps_m[1], act_u, 4).then_inc(ev("actT_ps"), 1)

            def down(m, e):
                pe.wait_ge(ev("actT"), m + 1)
                for k in range(4):
                    w = W2[:, bass.ds(e, 1), k].rearrange("p a n -> p (a n)")
                    pe.matmul(ps_m[2][:, 0:D], actT[:, k * P:(k + 1) * P], w, start=(k == 0), stop=False)
                pe.matmul(ps_m[2][:, 0:D], pick[:, bass.ds(e, 1), :].rearrange("p a n -> p (a n)"), b2_parts[:], start=False, stop=True).then_inc(ev("y_ps"), 1)

            def load_expert(m):
                alone(pe)
                return pe.value_load(expert[0:1, bass.ds(m, 1)] if not isinstance(m, int) else expert[0:1, m:m + 1], min_val=0, max_val=NE - 1)

            def one_tile(m, i, n, more=True):
                before, own_e = load_expert(m - 1), load_expert(m)
                turn_act(m - 1, 1 - i)
                up(m, i, own_e)
                if more:
                    turn_rows(m + 1, 1 - i, n + i)
                down(m - 1, before)

            e0 = load_expert(0)
            turn_rows(0, 0, 0)
            up(0, 0, e0)
            turn_rows(1, 1, 0)
            with pe.Fori(0, MT // 2 - 1) as n:
                one_tile(2 * n + 1, 1, n)
                one_tile(2 * n + 2, 0, n + 1)
            one_tile(MT - 2, 1, MT // 2 - 1)
            one_tile(MT - 1, 0, MT // 2, more=False)
            turn_act(MT - 1, 0)
            down(MT - 1, load_expert(MT - 1))

        @block.scalar
        def _(act):
            def copy(dst, src, scale=1.0):
                return act.activation(dst, src, ACT.Copy, scale=scale)

            def read(sec, b, name, ready, n, dst, width, scale=1.0):
                i, rd, _, _ = turns[M].at(sec, b, name)
                act.wait_ge(ev(ready), n)
                copy(dst[:, 0:width], ps_m[i][:, 0:width], scale).then_inc(rd, 1)

            def exponentials_of(sec, b, name, ready, n, width):
                i, rd, _, _ = turns[U].at(sec, b, name)
                e, used, before, _ = e_turns.at(sec, b, name)
                act.wait_ge(ev(ready), n)
                wait(act, used, before)
                act.activation(E[e][:, 0:width], ps_u[i][:, 0:width], ACT.Exp).then_inc(rd, 1)

            def do(sec, b, step):
                kind, r, k = step
                at = (sec, b)
                bx = batch_of(sec, b, kind)
                X = ST * bx + k
                Y = ST * b + k
                if kind == "scores":
                    exponentials_of(*at, ("s", r, k), "s_ps", b * 2 * len(PAIRS) + 2 * r + k + 1, 1024)
                if kind == "key":
                    exponentials_of(*at, ("key", k, r), "key_ps", 3 * X + r + 1, 1024 if r < 2 else 512)
                if kind == "q_stack":
                    i, rd, _, _ = turns[U].at(*at, ("qT", k))
                    act.wait_ge(ev("q_turned"), X + 1)
                    copy(Qx[k % 2][0:RS].rearrange("p h n -> p (h n)"), ps_u[i][:].bitcast(bf16)[0:RS, :]).then_inc(rd, 1)
                if kind == "flush":
                    _, used, _, after = e_turns.at(*at, ("s", last_pair(k), 1))
                    act.wait_ge(used, after)
                    copy(soT[k % 2][:], ps_o[:]).then_inc(ev("so_T"), 1)
                if kind in ("x", "late"):
                    if r == 1:
                        read(*at, ("xnT", k), "xnT_ps", X + 1, xnT, 2 * P)
                    if r == 9:
                        _, used, _, after = e_turns.at(*at, ("key", k, 2))
                        i, rd, _, _ = turns[M].at(*at, ("oT", k))
                        act.wait_ge(used, after)
                        copy(oT[:], ps_m[i][:]).then_inc(rd, 1)
                    if r == 11:
                        read(*at, ("onT", k), "onT_ps", X + 1, onT, 2 * P)
                    if r == 14:
                        act.wait_ge(ev("y0"), X + 1)
                        act.activation(sqa[:], row(bx, k, y0), ACT.Square, scale=D ** -0.5, accum_out=ss[:]).then_inc(ev("y0_ss"), 1)
                    if r == 15:
                        read(*at, ("hT", k), "hT_ps", X + 1, hT, 2 * P)
                if kind == "tail":
                    if r == 1:
                        read(*at, ("soT", k), "soT_ps", Y + 1, s_onT, 2 * P, scale=0.5)
                    if r == 2:
                        i, rd, _, _ = turns[M].at(*at, ("gate", k))
                        act.wait_ge(ev("gate_ps"), Y + 1)
                        act.activation(gt[:], ps_m[i][:, 0:2 * P], ACT.Tanh, bias=half_b_gate[:]).then_inc(rd, 1)
                    if r == 4:
                        act.wait_ge(ev("x2"), Y + 1)
                        act.activation(s_sqa[:], x2[:], ACT.Square, scale=D ** -0.5, accum_out=s_ss[:]).then_inc(ev("x2_ss"), 1)
                    if r == 5:
                        read(*at, ("h2T", k), "h2T_ps", Y + 1, h2T, 2 * P)

            go_through(act, do)
            def gates(m, i):
                act.wait_ge(ev("up_ps"), 2 * m + 1)
                act.activation(sig, ps_u[i][:, HID:2 * HID], ACT.Sigmoid).then_inc(ev("sig"), 1)

            gates(0, 0)
            with act.Fori(0, MT // 2) as n:
                gates(2 * n + 1, 1)
                gates(2 * n + 2, 0)

        @block.vector
        def _(dve):
            tt, ts, stt = dve.tensor_tensor, dve.tensor_scalar, dve.scalar_tensor_tensor
            heads = lambda ap: ap.rearrange("p (h d) -> p h d", d=HD)

            def parts(own, tok, rows_, n_heads, src, left, scale, hi, mid, lo, done):
                v = tok[0:rows_, :, 0:RS].rearrange("p h (s d) -> p h s d", d=HD)
                s4 = src.rearrange("p (h s d) -> p h s d", s=1, d=HD)
                for sl in hi:
                    n = len(range(*sl.indices(PARTS)))
                    i = ts(v[:, :, sl], s4.to_broadcast([rows_, n_heads, n, HD]), scale, None, ALU.mult)
                own.link(i)
                r4 = left[0:rows_, 0:n_heads * HD].rearrange("p (h s d) -> p h s d", s=1, d=HD)
                r3 = heads(left[0:rows_, 0:n_heads * HD])
                at = lambda sl: v[:, :, range(*sl.indices(PARTS))[0]]
                own.link(stt(r3, heads(src), scale, at(hi[0]), ALU.mult, ALU.subtract))
                for sl in mid:
                    n = len(range(*sl.indices(PARTS)))
                    own.link(dve.tensor_copy(v[:, :, sl], r4.to_broadcast([rows_, n_heads, n, HD])))
                tt(at(lo[0]), r3, at(mid[0]), ALU.subtract).then_inc(ev(done), 1)

            QP = dict(hi=(slice(0, 3),), mid=(slice(3, 5),), lo=(slice(5, 6),))
            KP = dict(hi=(slice(0, 4, 3), slice(5, 6)), mid=(slice(1, 5, 3),), lo=(slice(2, 3),))

            def read_own(rd, after, ins):
                ins.then_inc(rd, 1)
                dve.wait_ge(rd, after)

            def statistics(own, n, src):
                alone(dve)
                own.link(dve.bn_stats(stats[n][:], src))
                alone(dve)
                dve.bn_aggr(mv[n][:], stats[n][:]).then_inc(ev(f"mv{n}"), 1)

            def ctx_step(own, sec, b, r):
                bx = 0 if sec == "pro" else b + 1
                bias = lambda n, rows_: xbias[rows_, n]
                if r == 1:
                    i, rd, _, after = turns[U].at(sec, b, ("kv",))
                    dve.wait_ge(ev("kv_ps"), bx + 1)
                    tt(Vx[:, :, 0:HD], heads(ps_u[i][:, 256:512]), heads(xbias[:, 2]), ALU.add)
                    tt(kf[:], ps_u[i][:, 0:D], xbias[:, 1], ALU.add)
                    read_own(rd, after, tt(kl[0:CR], ps_u[i][0:CR, 512:512 + D], xbias[0:CR, 1], ALU.add))
                    i, rd, _, after = turns[U].at(sec, b, ("vr",))
                    dve.wait_ge(ev("ctx_proj"), bx + 1)
                    for q in range(4):
                        s_ = slice(32 * q, 32 * q + CR)
                        ins = tt(Vr[s_, :, 32 * q:32 * q + HD], heads(ps_u[i][s_, 0:D])[:, q:H:4], heads(xbias[s_, 2])[:, q:H:4], ALU.add)
                    ins.then_inc(rd, 1)
                    parts(own, k_tok, P, H, kf[:], k_rest, 1.0, done="k_split", **KP)
                if r in (3, 5):
                    n = r // 2 - 1
                    rows_, at = ((P, 0), (CR, P))[n]
                    i, rd, _, after = turns[U].at(sec, b, ("kT", n))
                    dve.wait_ge(ev("k_turned"), bx * 2 + n + 1)
                    ub = ps_u[i][:].bitcast(bf16).rearrange("p (h n) -> p h n", n=P)
                    dve.tensor_copy(Kx[0:RS, :, at:at + rows_], ub[0:RS, :, 0:rows_]).then_inc(rd, 1)
                    if n == 0:
                        parts(own, k_tok, CR, H, kl[0:CR], k_rest, 1.0, done="k_split", **KP)

            def x_step(own, sec, b, bx, r, k, late):
                at = (sec, b)
                X = ST * bx + k
                if r == 0:
                    dve.wait_ge(s_x[k], 16 if sec == "pro" else 16 * b + 32)
                    statistics(own, 0, row(bx, k, xb))
                if r == 1:
                    dve.wait_ge(ev("rstd0"), X + 1)
                    ts(xn[:], row(bx, k, xb), mv[0][:, 0:1], rstd[0][:], ALU.subtract, ALU.mult).then_inc(ev("xn"), 1)
                if r == 3:
                    i, rd, _, after = turns[M].at(*at, ("q", k))
                    dve.wait_ge(ev("q_ps"), X + 1)
                    read_own(rd, after, tt(qf[:], ps_m[i][:, 0:D], xbias[:, 0], ALU.add))
                    parts(own, q_tok, P, H, qf[:], rest, SCALE, done="q_split", **QP)
                if r in (5, 6, 7):
                    for c in (2 * r - 10, 2 * r - 9):
                        n = 3 if c < 5 else 1
                        i, rd, _, after = turns[M].at(*at, ("row", k, c))
                        dve.wait_ge(ev("row_ps"), X * 6 + c + 1)
                        src = ps_m[i][:, 0:n * C].rearrange("p (h n) -> p h n", n=C)
                        dve.tensor_reduce(out=mx[:, 3 * c:3 * c + n], in_=src, axis=AX.X, op=ALU.max).then_inc(rd, 1)
                    if r == 7:
                        dve.wait_ge(rd, after)
                        own.link(ts(nmx[:, 0], mx[:], -1.0, None, ALU.mult))
                        stt(nmx[:, 1], mx[:], -1.0, nmx[:, 0], ALU.mult, ALU.subtract).then_inc(ev("shift"), 1)
                if r == 8:
                    i, rd, _, after = turns[M].at(*at, ("shift", k))
                    dve.wait_ge(ev("shiftT_ps"), X + 1)
                    read_own(rd, after, dve.tensor_copy(nmT[RS:P, 0, :], ps_m[i][:].bitcast(bf16)[RS:P, 0:P]))
                    dve.tensor_copy(Qx[k % 2][RS:P], nmT[RS:P].to_broadcast([P - RS, H, P])).then_inc(ev("shiftT"), 1)
                if r == 11:
                    i, rd, _, after = turns[M].at(*at, ("o", k))
                    dve.wait_ge(ev("o_ps"), X + 1)
                    o4 = ps_m[i][:].rearrange("p (h n) -> p h n", n=32)
                    own.link(dve.reciprocal(rsum[:], o4[:, :, HD]))
                    tt(heads(on[:]), o4[:, :, 0:HD], rsum[:].rearrange("p (h d) -> p h d", d=1).to_broadcast([P, H, HD]), ALU.mult).then_inc(rd, 1)
                if r == 13:
                    i, rd, _, after = turns[M].at(*at, ("xo", k))
                    dve.wait_ge(ev("xo_ps"), X + 1)
                    x1 = row(bx, k, xb)
                    dve.wait_ge(ev("x_biased"), X + 1)
                    read_own(rd, after, tt(x1, x1, ps_m[i][:, 0:D], ALU.add))
                    statistics(own, 1, x1)
                if r == 14:
                    dve.wait_ge(ev("rstd1"), X + 1)
                    ts(row(bx, k, y0), row(bx, k, xb), mv[1][:, 0:1], rstd[1][:], ALU.subtract, ALU.mult).then_inc(ev("y0"), 1)
                if r == 15:
                    if sec == "pro" and k == 0:
                        dve.wait_ge(s_w, NW * 16)
                    dve.wait_ge(ev("y0_rs"), X + 1)
                    stt(hh[:], row(bx, k, y0), rs_row[:], ln1[:], ALU.mult, ALU.mult).then_inc(ev("hh"), 1)
                n = NH2 * HD
                if r == 17:
                    i, rd, _, after = turns[M].at(*at, ("qkv", k))
                    dve.wait_ge(ev("qkv_ps"), X + 1)
                    read_own(rd, after, tt(qkv[:], ps_m[i][:, 0:QKV], b_qkv[:], ALU.add))
                    dve.tensor_copy((Va if late else Va_next)[:, k, :, 0:HD], heads(qkv[:, n:]))
                    own.link(stt(sq[:], qkv[:, 0:n], 1.0 / HD, qkv[:, 0:n], ALU.mult, ALU.mult))
                    dve.tensor_reduce(out=hs[:], in_=heads(sq[:]), axis=AX.X, op=ALU.add).then_inc(ev("h_ms"), 1)
                    tt(heads(ra[:]), heads(qkv[:, 0:n]), rope_c[:, k:k + 1].to_broadcast([P, NH2, HD]), ALU.mult)
                    for half in range(2):
                        o, f = half * (HD // 2), (1 - half) * (HD // 2)
                        sn = rope_s[:, k:k + 1, o:o + HD // 2].to_broadcast([P, NH2, HD // 2])
                        ins = tt(heads(rb[:])[:, :, o:o + HD // 2], heads(qkv[:, 0:n])[:, :, f:f + HD // 2], sn, ALU.mult)
                    own.link(ins)
                    own.link(tt(ra[:], ra[:], rb[:], ALU.add))
                if r == 18:
                    w = qk_w[:].rearrange("p h d -> p (h d)")
                    dve.wait_ge(ev("h_rs"), X + 1)
                    own.link(tt(heads(ra[:]), heads(ra[:]), h_rs[:].rearrange("p (h d) -> p h d", d=1).to_broadcast([P, NH2, HD]), ALU.mult))
                    own.link(tt(ra[:, D:n], ra[:, D:n], w[:, D:n], ALU.mult))
                    parts(own, ks_tok, P, KV, ra[:, D:n], ks_rest, 1.0, done="ks_split", **KP)
                    tt(row(bx, k, q_hat), ra[:, 0:D], w[:, 0:D], ALU.mult).then_inc(ev("q_hat"), 1)
                if r == 19:
                    i, rd, _, after = turns[M].at(*at, ("ksT", k))
                    dve.wait_ge(ev("ks_ps"), X + 1)
                    dst = Kst[0:RS + 1, bx % 2, :, k * P:(k + 1) * P] if isinstance(bx, int) else \
                        Kst[0:RS + 1, bass.ds(parity(bx), 1), :, k * P:(k + 1) * P].rearrange("p a g n -> p (a g) n")
                    read_own(rd, after, dve.tensor_copy(dst, ps_m[i][:].bitcast(bf16)[0:RS + 1, 0:KV * P].rearrange("p (g n) -> p g n", n=P)))
                    dve.sem_inc(ev("ks_stack"), 1)

            def second_step(own, sec, b, kind, r, k):
                at = (sec, b)
                Y = ST * b + k
                j = TILE_ORDER[k] if kind in ("prep", "tail") else 0
                if kind == "swap":
                    dve.wait_ge(ev("q_hat"), ST * b + len(EARLY_V) - 1)
                    dve.tensor_copy(Va[:, 0:len(EARLY_V)], Va_next[:, 0:len(EARLY_V)]).then_inc(ev("va"), 1)
                if kind == "prep" and r == 0:
                    dve.wait_ge(ev("q_hat"), ST * b + j + 1)
                    parts(own, qs_tok, P, H, row(b, j, q_hat), qs_rest, SCALE, done="qs_split", **QP)
                if kind == "prep" and r == 2:
                    i, rd, _, after = turns[U].at(*at, ("qs", k))
                    if k >= 2:
                        _, rd2, _, after2 = turns[U].at(*at, ("s", last_pair(k - 2), 1))
                        dve.wait_ge(rd2, after2)
                    dve.wait_ge(ev("qs_ps"), Y + 1)
                    dve.tensor_copy(Qs[k % 2][0:RS + 1].rearrange("p h n -> p (h n)"), ps_u[i][:].bitcast(bf16)[0:RS + 1, :]).then_inc(rd, 1)
                if kind == "tail":
                    if r == 1:
                        i, rd, _, after = turns[M].at(*at, ("so", k))
                        dve.wait_ge(ev("so_ps"), Y + 1)
                        o4 = ps_m[i][:].rearrange("p (h n) -> p h n", n=32)
                        own.link(dve.reciprocal(s_rsum[:], o4[:, :, HD]))
                        dst4 = s_on[:].rearrange("p (g q d) -> p g q d", g=KV, d=HD)
                        for q in range(HQ):
                            f = s_rsum[:, KV * q:KV * q + KV].rearrange("p (g d) -> p g d", d=1).to_broadcast([P, KV, HD])
                            ins = tt(dst4[:, :, q], o4[:, KV * q:KV * q + KV, 0:HD], f, ALU.mult)
                        ins.then_inc(rd, 1)
                    if r == 3:
                        _, rd, _, after = turns[M].at(*at, ("gate", k))
                        dve.wait_ge(rd, after)
                        stt(gt[:], gt[:], 1.0, s_onT[:], ALU.add, ALU.mult).then_inc(ev("gated"), 1)
                    if r == 4:
                        i, rd, _, after = turns[M].at(*at, ("wo", k))
                        dve.wait_ge(ev("wo_ps"), Y + 1)
                        dve.wait_ge(ev("y0_biased"), ST * b + j + 1)
                        read_own(rd, after, tt(x2[:], row(b, j, y0), ps_m[i][:, 0:D], ALU.add))
                        dve.sem_inc(ev("x2"), 1)
                        dve.wait_ge(s_st, 32 * Y + 32)
                        tt(base[:], x2[:], row(b, j, xb), ALU.add).then_inc(ev("base"), 1)
                    if r == 5:
                        dve.wait_ge(ev("x2_rs"), Y + 1)
                        stt(h2[:], x2[:], s_rs[:], ln2[:], ALU.mult, ALU.mult).then_inc(ev("h2"), 1)
                    if r == 7:
                        i, rd, _, after = turns[M].at(*at, ("logit", k))
                        dve.wait_ge(ev("logit_ps"), Y + 1)
                        t = ST * b + j
                        dst = logits[:, t] if isinstance(t, int) else logits[:, bass.ds(t, 1), :].rearrange("p a e -> p (a e)")
                        tt(dst, ps_m[i][:, 0:NE], b_r[:], ALU.add).then_inc(rd, 1)

            def do(sec, b, step):
                kind, r, k = step
                own = owns_[sec]
                if own is None:
                    own = owns_[sec] = Own(dve, ev(f"d_{sec}"), b * N_OWN[sec] if sec == "body" else 0)
                if kind == "ctx":
                    ctx_step(own, sec, b, r)
                elif kind in ("x", "late"):
                    x_step(own, sec, b, batch_of(sec, b, kind), r, k, kind == "late")
                    if sec == "pro" and r == 12 and k > 0:
                        next(pieces)
                else:
                    second_step(own, sec, b, kind, r, k)

            owns_ = dict.fromkeys(("pro", "body", "epi"))
            dve.wait_ge(s_first, len(urgent) * 16)
            dve.wait_ge(ev("cleared"), N_CLEARED)
            own = Own(dve, ev("d_first"), 0)
            dve.tensor_copy(identb[:], identf[:])
            own.link(dve.tensor_copy(Kx[RS:P].rearrange("p h n -> p (h n)"), which_f))

            def once():
                own = Own(dve, ev("d_once"), 0)
                dve.tensor_copy(pick[:].rearrange("p e n -> p (e n)"), pick_f)
                own.link(ts(half_b_gate[:], b_gate[:], 0.5, None, ALU.mult))
                own.link(tt(qs_rest[:, 0:HD], qk_w[:, 0], qk_w[:, H], ALU.mult))
                own.link(dve.tensor_reduce(out=bshift[:], in_=qs_rest[:, 0:HD], axis=AX.X, op=ALU.max, apply_absolute_value=True))
                own.link(ts(bshift[:], bshift[:], -SCALE * HD, None, ALU.mult))
                own.link(dve.tensor_copy(qs_tok[:, :, RS:RS + 1], bshift[:].rearrange("p (a b) -> p a b", a=1).to_broadcast([P, H, 1])))
                yield
                for src, dst, n in ((b1_f, b1_parts, 2 * HID), (b2_f, b2_parts, D)):
                    tb = soT[1].bitcast(bf16)
                    for r in (0, 32, 64):
                        g = slice(r, r + NE)
                        for left_over in range(r // 32):
                            own.link(dve.tensor_copy(tb[g, 0:n], src[g, 0:n]))
                            own.link(tt(src[g, 0:n], src[g, 0:n], tb[g, 0:n], ALU.subtract))
                        own.link(dve.tensor_copy(dst[g, 0:n], src[g, 0:n]))
                        yield

            pieces = once()
            go_through(dve, do)
            assert owns_["body"].n == N_OWN["body"], owns_["body"].n

            own = Own(dve, ev("d_route"), 0)
            te = lambda ap: ap.rearrange("p (t e) -> p t e", e=1).to_broadcast([P, T, NE])
            _, rd, _, after = turns[M].at("epi", B - 1, ("logit", ST - 1))
            dve.wait_ge(rd, after)
            own.link(dve.tensor_reduce(out=best[:], in_=logits[:], axis=AX.X, op=ALU.max))
            own.link(tt(first_e[:], logits[:], te(best[:]), ALU.is_ge))
            own.link(tt(first_e[:], first_e[:], count_e[:].rearrange("p (a e) -> p a e", a=1).to_broadcast([P, T, NE]), ALU.mult))
            own.link(dve.tensor_reduce(out=best[:], in_=first_e[:], axis=AX.X, op=ALU.max))
            tt(onehot[:], first_e[:], te(best[:]), ALU.is_equal).then_inc(ev("onehot"), 1)
            dve.wait_ge(ev("ranks"), 1)
            own.link(dve.tensor_copy(total[:], ps_u[0][:, 512:512 + T * NE].rearrange("p (t e) -> p e t", e=NE)))
            for e in range(NE):
                i = dve.tensor_tensor_scan(cum[:, e], ones[:, 0:T], total[:, e], 0.0, ALU.mult, ALU.add)
            own.link(i)
            own.link(ts(padded[:], cum[:, :, T - 1], float(P - 1), None, ALU.add))
            own.link(dve.tensor_copy(whole[:], padded[:]))
            own.link(ts(whole[:], whole[:], ((1 << 24) - 1) // P * P, None, ALU.bitwise_and))
            own.link(dve.tensor_copy(padded[:], whole[:]))
            own.link(dve.tensor_tensor_scan(offset[:], ones[:, 0:NE], padded[:], 0.0, ALU.mult, ALU.add))
            own.link(tt(offset[:], offset[:], padded[:], ALU.subtract))
            own.link(tt(cum[:], cum[:], total[:], ALU.subtract))
            own.link(tt(cum[:], cum[:], offset[:].rearrange("p (e t) -> p e t", t=1).to_broadcast([P, NE, T]), ALU.add))
            own.link(tt(first_e[:], ps_u[0][:, 0:T * NE].rearrange("p (t e) -> p t e", e=NE), cum[:].rearrange("p e t -> p t e"), ALU.add))
            own.link(tt(first_e[:], first_e[:], onehot[:], ALU.mult))
            own.link(dve.tensor_reduce(out=placef[:], in_=first_e[:], axis=AX.X, op=ALU.add))
            own.link(dve.tensor_copy(place[:], placef[:]))
            ts(split_i[:, 0], place[:], P - 1, None, ALU.bitwise_and)
            own.link(ts(split_i[:, 1], place[:], P.bit_length() - 1, None, ALU.arith_shift_right))
            dve.tensor_copy(place_row[:], split_i[:, 0])
            own.link(dve.tensor_copy(place_tile[:], split_i[:, 1]))
            for g in range(4):
                of = lambda ap, n: ap[:, g * G:(g + 1) * G].rearrange("p (t n) -> p t n", n=1).to_broadcast([P, G, n])
                along = lambda ap, n: ap[:].rearrange("p (t n) -> p t n", t=1).to_broadcast([P, G, n])
                tt(row_hot[g], along(row_no, P), of(place_row, P), ALU.is_equal)
                own.link(tt(tile_hot[g][:, :, 0], along(tile_no, MT), of(place_tile, MT), ALU.is_equal))
                tt(tile_hot[g][:, :, 1:3], tile_hot[g][:, :, 0:1].to_broadcast([P, G, 2, MT]),
                   token[:, g * G:(g + 1) * G].rearrange("p t (a n) -> p t a n", n=1).to_broadcast([P, G, 2, MT]), ALU.mult).then_inc(ev("hot"), 1)
            own.link(tt(owns[:], tile_row[:].rearrange("p (m e) -> p m e", e=1).to_broadcast([P, MT, NE]),
                        offset[:].rearrange("p (m e) -> p m e", m=1).to_broadcast([P, MT, NE]), ALU.is_ge))
            own.link(dve.tensor_reduce(out=expertf[:], in_=owns[:], axis=AX.X, op=ALU.add))
            own.link(ts(expertf[:], expertf[:], -1.0, None, ALU.add))
            dve.tensor_copy(expert[:], expertf[:])
            dve.wait_ge(ev("ids_ps"), 1)
            own.link(ts(taken_by[:], ps_o[:, 0:MT], -1.0, 1.0, ALU.mult, ALU.add))
            own.link(stt(ids[:], taken_by[:], spare[:], ps_o[:, MT:2 * MT], ALU.mult, ALU.add))
            own.link(stt(ids[:], ps_o[:, 2 * MT:3 * MT], float(P), ids[:], ALU.mult, ALU.add))
            dve.tensor_copy(idx[:], ids[:]).then_inc(ev("places"), 1)

            def take_rows(m, i):
                dve.wait_ge(ev("rowsT_ps"), m + 1)
                dve.tensor_copy(xT[i], ps_m[0][:, 0:2 * P]).then_inc(ev("rowsT"), 1)

            def keep_base(i):
                dve.tensor_copy(bs[i], xr[i][:, D:]).then_inc(ev("base_rows"), 1)

            def gate_rows(m, i):
                dve.wait_ge(ev("up_ps"), 2 * m + 2)
                dve.wait_ge(ev("sig"), m + 1)
                tt(act_u, ps_u[i][:, 0:HID], sig, ALU.mult).then_inc(ev("act"), 1)

            def take_act(m):
                dve.wait_ge(ev("actT_ps"), m + 1)
                dve.tensor_copy(actT, ps_m[1][:]).then_inc(ev("actT"), 1)

            def take_result(m, i):
                dve.wait_ge(ev("y_ps"), m + 1)
                dve.wait_ge(ev("yr_free"), m + 1)
                tt(yr[i], ps_m[2][:, 0:D], bs[i], ALU.add).then_inc(ev("y_rows"), 1)
                dve.wait_ge(ev("y_rows"), m + 1)

            def one_tile(m, i, more=True):
                take_act(m - 1)
                if more:
                    take_rows(m + 1, 1 - i)
                gate_rows(m, i)
                take_result(m - 1, 1 - i)
                if more:
                    keep_base(1 - i)

            take_rows(0, 0)
            keep_base(0)
            take_rows(1, 1)
            gate_rows(0, 0)
            keep_base(1)
            with dve.Fori(0, MT // 2 - 1) as n:
                one_tile(2 * n + 1, 1)
                one_tile(2 * n + 2, 0)
            one_tile(MT - 2, 1)
            one_tile(MT - 1, 0, more=False)
            take_act(MT - 1)
            take_result(MT - 1, 0)


def rope_tables():
    inv = (np.float32(1.0) / np.float32(10000.0) ** (np.arange(0, HD, 2, dtype=np.float32) / np.float32(HD))).astype(np.float32)
    f = (np.arange(S, dtype=np.float32)[:, None] * inv[None, :]).astype(np.float32)
    c, s = np.cos(f.astype(np.float64)).astype(np.float32), np.sin(f.astype(np.float64)).astype(np.float32)
    return np.concatenate([c, c], 1), np.concatenate([-s, s], 1)


def layout(inputs):
    g = {k: np.asarray(v) for k, v in inputs.items()}
    f, x = "L0_ffn_", "L0_xattn_"
    r = {"x": g["x"].reshape(B * S, D), "ctxT": np.ascontiguousarray(g["ctx_1024"].transpose(0, 2, 1))}
    r["xw"] = np.stack([g[x + n].T for n in ("Wq", "Wk", "Wv", "Wo")])
    r["xb"] = np.stack([g[x + n] for n in ("bq", "bk", "bv", "bo")])
    r["w_qkv"] = np.concatenate([g[f + "Wq"], g[f + "Wk"], g[f + "Wv"]], 1)
    r["b_qkv"] = np.concatenate([g[f + "bq"], g[f + "bk"], g[f + "bv"]])[None]
    r["qk_w"] = np.concatenate([np.tile(g[f + "qn_w"], H), np.tile(g[f + "kn_w"], KV)])[None]
    for n, k in (("bo", "bo"), ("br", "br"), ("ln1", "ln1_w"), ("ln2", "ln2_w")):
        r[n] = g[f + k][None]
    for n in ("Wo", "Wr", "W1", "W2"):
        r[f + n] = g[f + n]
    w = np.zeros((P, P), g[f + "Wg"].dtype)
    for i in range(P // HD):
        w[i * HD:(i + 1) * HD, i * HD:(i + 1) * HD] = g[f + "Wg"]
    r["w_gate"] = w
    r["b_gate"] = np.tile(g[f + "bg"], P // HD)[:, None]
    for n, k in (("b1_rows", "b1"), ("b2_rows", "b2")):
        v = np.zeros((P, g[f + k].shape[1]), g[f + k].dtype)
        for s in range(3):
            v[32 * s:32 * s + NE] = g[f + k]
        r[n] = v
    r["identf"] = np.eye(P, dtype=np.float32)
    r["upper"], r["ones"] = np.triu(np.ones((P, P), np.float32), 1), np.ones((P, P), np.float32)
    r["count_e"] = (NE - np.arange(NE, dtype=np.float32))[None]
    r["tile_row"] = (P * np.arange(MT, dtype=np.float32))[None]
    r["row_no"] = np.arange(P, dtype=np.float32)[None]
    r["token"] = np.stack(np.broadcast_arrays(np.arange(P)[:, None], np.arange(T)[None]), -1).astype(np.float32)
    r["spare"] = (T * P + np.arange(P, dtype=np.float32))[:, None]
    r["rope_c"], r["rope_s"] = rope_tables()
    pick = np.zeros((P, NE, P), np.float32)
    which = np.zeros((2 * H, H, P + KR), np.float32)
    for s in range(3):
        for e in range(NE):
            pick[32 * s + e, e] = 1
    for s in range(2):
        for h in range(H):
            which[s * H + h, h, 0:C] = 1
    r["pick"], r["which_head"] = pick.reshape(P, -1), which.reshape(2 * H, -1)
    return {k: np.ascontiguousarray(v) for k, v in r.items()}


def kernel(**inputs):
    import concourse.bacc as bacc
    from concourse.bass_utils import run_bass_kernel_spmd

    nc = bacc.Bacc("TRN2", target_bir_lowering=False, num_devices=1)
    arrays = layout(inputs)
    aps = {n: nc.dram_tensor(f"in_{n}", v.shape, mybir.dt.from_np(v.dtype), kind="ExternalInput").ap() for n, v in arrays.items()}
    out = nc.dram_tensor("out", (B * S + P, D), fp32, kind="ExternalOutput").ap()
    build(nc, aps, out)
    r = run_bass_kernel_spmd(nc, [{f"in_{n}": v for n, v in arrays.items()}], core_ids=[0])
    return r.results[0]["out"][:B * S].reshape(B, S, D)
```
